# Optimizing a Trainium2 kernel written in Bass

```python
import numpy as np
import jax
import jax.numpy as jnp

def _softmax(x, axis=-1):
    return jax.nn.softmax(x, axis=axis)
def _gelu(x):
    return jax.nn.gelu(x, approximate=True)
def _silu(x):
    return jax.nn.silu(x)
def _sigmoid(x):
    return jax.nn.sigmoid(x)
def _layernorm(x, axis=-1, eps=1e-5):
    m = jnp.mean(x, axis=axis, keepdims=True)
    v = jnp.var(x, axis=axis, keepdims=True)
    return (x - m) / jnp.sqrt(v + eps)
def _scatter_add(tgt, idx, src, axis=0):
    return tgt.at[idx].add(src)
def _segment_sum(src, seg, n):
    return jax.ops.segment_sum(src, seg, n)

kernel_name = 'mk_conv_preact_d4_conv_nchw64_3fa3f0'

def setup_inputs(seed: int = 0):
    np.random.seed(seed)
    _w = jnp.asarray
    def _rec_inputs():
        import jax
        import jax.numpy as jnp
        _gk = jax.random.key(seed)
        x = -8.268e-05 + 0.9999 * jax.random.normal(jax.random.fold_in(_gk, 1), (32, 64, 112, 112), jnp.float32)
        return x
    x = _rec_inputs()
    def _L0_conv_setup():
        import jax, jax.numpy as jnp
        import numpy as np
        key = jax.random.key(seed)
        k1, k2 = jax.random.split(key)
        x = jax.random.normal(k1, (64, 64, 112, 112), dtype=jnp.float32)
        weight = jax.random.normal(k2, (64, 64, 3, 3), dtype=jnp.float32) * 0.1
        alpha = jnp.ones((64, 1, 1), dtype=jnp.float32)
        return {'x': x, 'weight': weight, 'alpha': alpha}
    _L0_conv_all = _L0_conv_setup()
    _L0_conv_in = {k: v for k, v in _L0_conv_all.items() if k in ('weight', 'alpha', )}
    del _L0_conv_all

    def _L1_conv_setup():
        import jax, jax.numpy as jnp
        import numpy as np
        key = jax.random.key(seed)
        k1, k2 = jax.random.split(key)
        x = jax.random.normal(k1, (8, 64, 256, 512), dtype=jnp.float32)
        weight = jax.random.normal(k2, (64, 64, 64, 64, 2), dtype=jnp.float32) * 0.01
        return {'x': x, 'weight': weight}
    _L1_conv_all = _L1_conv_setup()
    _L1_conv_in = {k: v for k, v in _L1_conv_all.items() if k in ('weight', )}
    del _L1_conv_all

    def _L2_conv_setup():
        import jax, jax.numpy as jnp
        import numpy as np
        PADDING = (3, 3)
        STRIDE = (1, 1)
        key = jax.random.key(seed)
        k1, k2, k3 = jax.random.split(key, 3)
        B, Cin, H, W = (16, 64, 256, 256)
        Cout, kH, kW = (64, 7, 7)
        signal = jax.random.normal(k1, (B, Cin, H, W), dtype=jnp.float32)
        weight = jax.random.normal(k2, (Cout, Cin, kH, kW), dtype=jnp.float32) * 0.02
        bias = jax.random.normal(k3, (Cout,), dtype=jnp.float32) * 0.02
        return {'signal': signal, 'weight': weight, 'bias': bias}
    _L2_conv_all = _L2_conv_setup()
    _L2_conv_in = {k: v for k, v in _L2_conv_all.items() if k in ('weight', 'bias', )}
    del _L2_conv_all

    def _L3_conv_setup():
        import jax, jax.numpy as jnp
        import numpy as np
        WS = 8
        NH = 8
        DIM = 64
        HD = DIM // NH
        FF = 3
        KS = 5
        EPS = 1e-06

        def _norm(t):
            return jnp.sqrt(jnp.sum(t * t, axis=-1, keepdims=True))
        key = jax.random.key(seed)
        ks = jax.random.split(key, 9)
        B, C, H, W = (8, DIM, 256, 256)
        x = jax.random.normal(ks[0], (B, C, H, W), dtype=jnp.float32)
        qkv_w = jax.random.normal(ks[1], (3 * C, C), dtype=jnp.float32) * 0.02
        qkv_b = jax.random.normal(ks[2], (3 * C,), dtype=jnp.float32) * 0.02
        proj_w = jax.random.normal(ks[3], (C, C), dtype=jnp.float32) * 0.02
        proj_b = jax.random.normal(ks[4], (C,), dtype=jnp.float32) * 0.02
        scale = jax.random.normal(ks[5], (1, 1, C), dtype=jnp.float32) * 0.02
        pos_enc = jax.random.normal(ks[6], (1, WS * WS, C), dtype=jnp.float32) * 0.02
        dwc_w = jax.random.normal(ks[7], (HD, 1, KS, KS), dtype=jnp.float32) * 0.02
        dwc_b = jax.random.normal(ks[8], (HD,), dtype=jnp.float32) * 0.02
        return {'x': x, 'qkv_w': qkv_w, 'qkv_b': qkv_b, 'proj_w': proj_w, 'proj_b': proj_b, 'scale': scale, 'pos_enc': pos_enc, 'dwc_w': dwc_w, 'dwc_b': dwc_b}
    _L3_conv_all = _L3_conv_setup()
    _L3_conv_in = {k: v for k, v in _L3_conv_all.items() if k in ('qkv_w', 'qkv_b', 'proj_w', 'proj_b', 'scale', 'pos_enc', 'dwc_w', 'dwc_b', )}
    del _L3_conv_all

    return {
        "x": x,
        "L0_conv_weight": _L0_conv_in["weight"],
        "L0_conv_alpha": _L0_conv_in["alpha"],
        "L1_conv_weight": _L1_conv_in["weight"],
        "L2_conv_weight": _L2_conv_in["weight"],
        "L2_conv_bias": _L2_conv_in["bias"],
        "L3_conv_qkv_w": _L3_conv_in["qkv_w"],
        "L3_conv_qkv_b": _L3_conv_in["qkv_b"],
        "L3_conv_proj_w": _L3_conv_in["proj_w"],
        "L3_conv_proj_b": _L3_conv_in["proj_b"],
        "L3_conv_scale": _L3_conv_in["scale"],
        "L3_conv_pos_enc": _L3_conv_in["pos_enc"],
        "L3_conv_dwc_w": _L3_conv_in["dwc_w"],
        "L3_conv_dwc_b": _L3_conv_in["dwc_b"],
    }

def reference(x, L0_conv_weight, L0_conv_alpha, L1_conv_weight, L2_conv_weight, L2_conv_bias, L3_conv_qkv_w, L3_conv_qkv_b, L3_conv_proj_w, L3_conv_proj_b, L3_conv_scale, L3_conv_pos_enc, L3_conv_dwc_w, L3_conv_dwc_b):
    import jax
    import jax.numpy as jnp
    def _L0_conv_ref(x, weight, alpha):
        import jax, jax.numpy as jnp
        import numpy as np
        x_bin = jnp.sign(x)
        w_tern = jnp.round(jnp.tanh(weight))
        out = jax.lax.conv_general_dilated(x_bin, w_tern, window_strides=(1, 1), padding=((1, 1), (1, 1)), dimension_numbers=('NCHW', 'OIHW', 'NCHW'))
        return out * alpha

    def _L1_conv_ref(x, weight):
        import jax, jax.numpy as jnp
        import numpy as np
        B, C, H, W = x.shape
        O = weight.shape[1]
        x_ft = jnp.fft.rfft2(x, norm='ortho')
        full_w = x_ft.shape[-1]
        mlat = min(weight.shape[2], H // 2)
        mlon = min(weight.shape[3], full_w)
        xt = x_ft[:, :, :mlat, :mlon]
        w = jax.lax.complex(weight[:, :, :mlat, :mlon, 0], weight[:, :, :mlat, :mlon, 1])
        out_ft = jnp.einsum('bchw,cohw->bohw', xt, w)
        out_ft_full = jnp.zeros((B, O, H, full_w), dtype=out_ft.dtype)
        out_ft_full = out_ft_full.at[:, :, :mlat, :mlon].set(out_ft)
        return jnp.fft.irfft2(out_ft_full, s=(H, W), norm='ortho')

    def _L2_conv_ref(signal, weight, bias):
        import jax, jax.numpy as jnp
        import numpy as np
        PADDING = (3, 3)
        STRIDE = (1, 1)
        ph, pw = PADDING
        sh, sw = STRIDE
        kH, kW = (weight.shape[-2], weight.shape[-1])
        sig = jnp.pad(signal, ((0, 0), (0, 0), (ph, ph), (pw, pw)))
        Hp, Wp = (sig.shape[-2], sig.shape[-1])
        X = jnp.fft.rfftn(sig, axes=(-2, -1))
        K = jnp.fft.rfftn(weight, s=(Hp, Wp), axes=(-2, -1))
        Y = jnp.einsum('bchw,ochw->bohw', X, jnp.conj(K))
        y = jnp.fft.irfftn(Y, s=(Hp, Wp), axes=(-2, -1))
        out = y[..., :Hp - kH + 1:sh, :Wp - kW + 1:sw]
        out = out + bias[None, :, None, None]
        return out

    def _L3_conv_ref(x, qkv_w, qkv_b, proj_w, proj_b, scale, pos_enc, dwc_w, dwc_b):
        import jax, jax.numpy as jnp
        import numpy as np
        WS = 8
        NH = 8
        DIM = 64
        HD = DIM // NH
        FF = 3
        KS = 5
        EPS = 1e-06

        def _norm(t):
            return jnp.sqrt(jnp.sum(t * t, axis=-1, keepdims=True))
        B, C, H, W = x.shape
        xw = x.reshape(B, C, H // WS, WS, W // WS, WS)
        xw = xw.transpose(0, 2, 4, 3, 5, 1).reshape(-1, WS * WS, C)
        Bw, N, _ = xw.shape
        qkv = xw @ qkv_w.T + qkv_b
        q, k, v = jnp.split(qkv, 3, axis=-1)
        k = k + pos_enc
        q = jax.nn.relu(q) + EPS
        k = jax.nn.relu(k) + EPS
        sc = jax.nn.softplus(scale)
        q = q / sc
        k = k / sc
        qn, kn = (_norm(q), _norm(k))
        q = q ** FF
        k = k ** FF
        q = q / _norm(q) * qn
        k = k / _norm(k) * kn
        q = q.reshape(Bw, N, NH, HD).transpose(0, 2, 1, 3)
        k = k.reshape(Bw, N, NH, HD).transpose(0, 2, 1, 3)
        v = v.reshape(Bw, N, NH, HD).transpose(0, 2, 1, 3)
        kmean = k.mean(axis=2, keepdims=True)
        z = 1.0 / (jnp.einsum('bhnd,bhmd->bhnm', q, kmean) + EPS)
        s = N ** (-0.5)
        kv = jnp.einsum('bhnd,bhne->bhde', k * s, v * s)
        out = jnp.einsum('bhnd,bhde->bhne', q, kv) * z
        out = out.transpose(0, 2, 1, 3).reshape(Bw, N, C)
        vimg = v.reshape(Bw * NH, WS, WS, HD).transpose(0, 3, 1, 2)
        pad = KS // 2
        dwc = jax.lax.conv_general_dilated(vimg, dwc_w, window_strides=(1, 1), padding=[(pad, pad), (pad, pad)], feature_group_count=HD)
        dwc = dwc + dwc_b[None, :, None, None]
        dwc = dwc.reshape(Bw, C, N).transpose(0, 2, 1)
        out = out + dwc
        out = out @ proj_w.T + proj_b
        xr = out.reshape(B, H // WS, W // WS, WS, WS, C)
        xr = xr.transpose(0, 5, 1, 3, 2, 4).reshape(B, C, H, W)
        return xr

    def _gn(v, G=32, eps=1e-5):
        B_, C_, H_, W_ = v.shape
        g = v.reshape(B_, G, C_ // G, H_, W_)
        m = jnp.mean(g, axis=(2, 3, 4), keepdims=True)
        s = jnp.var(g, axis=(2, 3, 4), keepdims=True)
        return ((g - m) / jnp.sqrt(s + eps)).reshape(v.shape)

    def _ln_c(v, eps=1e-6):
        m = jnp.mean(v, axis=1, keepdims=True)
        s = jnp.var(v, axis=1, keepdims=True)
        return (v - m) / jnp.sqrt(s + eps)

    def _ln_t(v, eps=1e-5):
        m = jnp.mean(v, axis=-1, keepdims=True)
        s = jnp.var(v, axis=-1, keepdims=True)
        return (v - m) / jnp.sqrt(s + eps)

    def _to_tokens(v):
        B_, C_, H_, W_ = v.shape
        return v.reshape(B_, C_, H_ * W_).transpose(0, 2, 1)
    def _from_tokens(t, like):
        B_, C_, H_, W_ = like.shape
        return t.transpose(0, 2, 1).reshape(B_, C_, H_, W_)

    x = x + _L0_conv_ref(_gn(x), L0_conv_weight, L0_conv_alpha)
    x = x + _L1_conv_ref(_gn(x), L1_conv_weight)
    x = x + _L2_conv_ref(_gn(x), L2_conv_weight, L2_conv_bias)
    x = x + _L3_conv_ref(_gn(x), L3_conv_qkv_w, L3_conv_qkv_b, L3_conv_proj_w, L3_conv_proj_b, L3_conv_scale, L3_conv_pos_enc, L3_conv_dwc_w, L3_conv_dwc_b)
    return x


_drawn_inputs = setup_inputs


def setup_inputs(seed=0):
    import zlib

    import numpy as np

    out = dict(_drawn_inputs(seed))
    spreads = {'L0_conv_alpha': (1.0, 0.2)}
    factors = {'L2_conv_bias': 4.422,
     'L3_conv_qkv_w': 8.0,
     'L3_conv_qkv_b': 8.0,
     'L3_conv_proj_w': 8.0,
     'L3_conv_proj_b': 4.39,
     'L3_conv_scale': 8.0,
     'L3_conv_pos_enc': 8.0,
     'L3_conv_dwc_w': 8.0,
     'L3_conv_dwc_b': 8.0}
    for name, (base, spread) in spreads.items():
        noise = np.random.default_rng([zlib.crc32(name.encode()), seed]).standard_normal(out[name].shape)
        drawn = base * np.exp(spread * noise) if base else spread * noise
        out[name] = jnp.asarray(drawn.astype(out[name].dtype))
    for name, factor in factors.items():
        out[name] = (out[name] * factor).astype(out[name].dtype)
    return out
```

```python
from contextlib import ExitStack

import numpy as np

import concourse.bass as bass
from concourse import mybir

ALU = mybir.AluOpType
ACT = mybir.ActivationFunctionType
AX = mybir.AxisListType
F32 = mybir.dt.float32
F16 = mybir.dt.float16
BF16 = mybir.dt.bfloat16

P = 128
C = 64
H = W = 112
J = H // 2
PIX = J * W
KH = H // 2
KW = W // 2 + 1
KP = KH // 2
FR = 2 * KW
FP = 128
ROWS = 4
CHUNKS = J // ROWS
N4 = ROWS * W
BANK = 512
GN_EPS = 1e-5


def wait(eng, sem, value):
    if isinstance(value, int) and value <= 0:
        return
    eng.wait_ge(sem, value)
    if eng.engine in (mybir.EngineType.SP, mybir.EngineType.Pool) and not isinstance(value, int):
        eng.nop(nofuse=True)


def wait_apart(eng, sem, value):
    wait(eng, sem, value)
    if not isinstance(value, int):
        eng.nop(nofuse=True)


class Chain:

    def __init__(self, eng, sem, per, n):
        self.eng, self.sem, self.at = eng, sem, n * per

    def __call__(self, ins):
        ins.then_inc(self.sem, 1)
        self.at = self.at + 1
        self.eng.wait_ge(self.sem, self.at)


def constants():
    k, w = np.arange(KH), np.arange(KW)
    n = np.arange(H)
    ang = 2 * np.pi * np.outer(n, k) / H
    fwd_h = (np.stack([np.cos(ang), -np.sin(ang)], -1).reshape(H, 2 * KH) / H).reshape(J, 2, -1).transpose(1, 0, 2)
    fwd_h = fwd_h.reshape(H, -1)
    aw = 2 * np.pi * np.outer(n, w) / W
    fwd_w = np.concatenate([
        np.stack([np.cos(aw), -np.sin(aw)], -1).reshape(W, FR),
        np.stack([np.sin(aw), np.cos(aw)], -1).reshape(W, FR)], 1)
    inv_h = np.zeros((P, 2, H))
    inv_h[0:KH, 0], inv_h[64:64 + KH, 0] = np.cos(ang).T, -np.sin(ang).T
    inv_h[0:KH, 1], inv_h[64:64 + KH, 1] = np.sin(ang).T, np.cos(ang).T
    inv_w = np.zeros((P, W))
    twice = np.where((w == 0) | (w == W // 2), 1.0, 2.0)[:, None] / W
    inv_w[0:KW], inv_w[64:64 + KW] = np.cos(aw).T * twice, -np.sin(aw).T * twice
    p = np.arange(P)
    group = ((p[:, None] % C) // 2 == (p[None, :] % C) // 2) / 4.0
    head = (p[:, None] // 8 == p[None, :] // 8) / 64.0
    tok = np.arange(P)
    win, y, x = tok // 64, tok % 64 // 8, tok % 8
    taps = np.zeros((P, 25, P))
    for t in range(25):
        ok = ((win[:, None] == win[None, :]) & (y[:, None] == y[None, :] + t // 5 - 2)
              & (x[:, None] == x[None, :] + t % 5 - 2))
        taps[:, t] = ok
    made = dict(fwd_h=fwd_h, fwd_w=fwd_w, inv_h=inv_h.reshape(P, 2 * H), inv_w=inv_w, group=group,
                head=head, ident=np.eye(P), taps=taps.reshape(P, 25 * P))
    return {k: np.ascontiguousarray(v, np.float32) for k, v in made.items()}


def pairs(eng, images, step):
    if images > 2:
        step(0)
    if images > 4:
        with eng.Fori(1, images // 2 - 1) as t:
            step(t)


def overlapped(eng, images, prep, conv, rest):
    def step(t):
        for odd in range(2):
            prep(2 * t + (2 + odd), odd)
            conv(2 * t + (1 + odd), 1 - odd)
            rest(2 * t + odd, odd)

    prep(0, 0)
    prep(1, 1)
    conv(0, 0)
    pairs(eng, images, step)
    conv(images - 1, 1)
    rest(images - 2, 0)
    rest(images - 1, 1)


def local_conv_and_forward_dft(nc, B, x, weight, alpha, cst, x1, xf):
    with ExitStack() as ctx:
        sb = lambda name, shape, dt=F32: ctx.enter_context(nc.sbuf_tensor("a_" + name, shape, dt))
        sem = lambda name: ctx.enter_context(nc.semaphore("a_" + name))
        ps = ctx.enter_context(nc.psum_tensor("a_ps", [P, 8, BANK], F32))
        xc = sb("xc", [P, 2, J, W])
        x1s = sb("x1s", [P, J, W])
        signs = sb("signs", [P, 2, J + 1, W + 2], BF16)
        xh = sb("xh", [P, C, W])
        yw = sb("yw", [P, 2, KH, C])
        freq = sb("freq", [P, KP, FP])
        wraw = sb("wraw", [C, C, 9])
        wpos = sb("wpos", [C, C, 9])
        wtern = sb("wtern", [C, C, 9])
        wst = sb("wst", [P, 2, 3, 2, C], BF16)
        ident = sb("ident", [P, P])
        group = sb("group", [P, P])
        fh = sb("fh", [H, 2 * KH])
        fw = sb("fw", [W, 2, FR])
        alph = sb("alph", [P, 1])
        bn = sb("bn", [P, CHUNKS, 6])
        mv = sb("mv", [P, 2])
        stx = sb("stx", [P, 2, 2])
        sty = sb("sty", [P, 2, 2])
        negm = sb("negm", [P, 2])
        gst = sb("gst", [P, 4])
        rstd = sb("rstd", [P, 1])
        dc = sb("dc", [P, 1])

        cst_in = sem("cst_in")
        pads = sem("pads")
        w_tern = sem("w_tern")
        w_turned = sem("w_turned")
        w_put = sem("w_put")
        x_in = [sem("x_in0"), sem("x_in1")]
        x_stats = sem("x_stats")
        x_mean = sem("x_mean")
        neg_mean = sem("neg_mean")
        signed = sem("signed")
        conv_done = sem("conv_done")
        x1_done = sem("x1_done")
        x1_out = sem("x1_out")
        x1_stats = sem("x1_stats")
        x1_group = sem("x1_group")
        x1_var = sem("x1_var")
        x1_std = sem("x1_std")
        x1_rstd = sem("x1_rstd")
        xh_in = sem("xh_in")
        dft_done = sem("dft_done")
        dft_copied = sem("dft_copied")
        dc_done = sem("dc_done")
        freq_out = sem("freq_out")
        prep_at, conv_at, rest_at = sem("prep_at"), sem("conv_at"), sem("rest_at")
        PREP_LINKS, CONV_LINKS, REST_LINKS = 3, 3, 3
        GROUPS = C // 4 + KP // 4

        block = ctx.enter_context(nc.Block())

        @block.sync
        def _(sp):
            for dst, src in ((wraw[:], weight.rearrange("o c h w -> o c (h w)")), (ident[:], cst["ident"]),
                             (group[:], cst["group"]), (fh[:], cst["fwd_h"]),
                             (fw[:], cst["fwd_w"].rearrange("h (r f) -> h r f", r=2)),
                             (alph[0:C], alpha), (alph[C:P], alpha)):
                sp.dma_start(dst, src).then_inc(cst_in, 16)

            def load(n, odd):
                for hp in range(2):
                    src = x[bass.ds(n, 1)].rearrange("b c (j hp) w -> hp (b c) j w", hp=2)[hp]
                    sp.dma_start(xc[C * hp:C * hp + C, odd], src).then_inc(x_in[odd], 16)

            def turn(n):
                wait(sp, x1_out, 16 * (n + 1))
                wait(sp, dft_done, n * GROUPS)
                for hp in range(2):
                    src = x1[bass.ds(n, 1)].rearrange("b hp c j w -> hp (b j) c w")[hp]
                    sp.dma_start(xh[J * hp:J * hp + J], src).then_inc(xh_in, 16)

            load(0, 0)
            load(1, 1)

            def step(t):
                for odd in range(2):
                    wait(sp, x1_done, (2 * t + (odd + 1)) * CHUNKS)
                    load(2 * t + (2 + odd), odd)
                    turn(2 * t + odd)

            pairs(sp, B, step)
            turn(B - 2)
            turn(B - 1)

        @block.gpsimd
        def _(pool):
            pool.memset(signs[:], 0.0)
            pool.memset(freq[:], 0.0)
            pool.memset(wst[:], 0.0).then_inc(pads, 1)

            def store_x1(n):
                wait(pool, x1_done, (n + 1) * CHUNKS)
                dst = x1[bass.ds(n, 1)].rearrange("b hp c j w -> (b hp c) j w")
                pool.dma_start(dst, x1s[:]).then_inc(x1_out, 16)

            def store_freq(n):
                wait(pool, dft_copied, (n + 1) * GROUPS)
                wait(pool, dc_done, n + 1)
                dst = xf[:, :, bass.ds(n, 1)].rearrange("k p b f -> p k (b f)")
                pool.dma_start(dst, freq[:]).then_inc(freq_out, 16)

            overlapped(pool, B, lambda n, odd: None, lambda n, odd: store_x1(n), lambda n, odd: store_freq(n))
            pool.wait_ge(x1_out, 16 * B)
            pool.wait_ge(freq_out, 16 * B)

        @block.vector
        def _(dve):
            EDGE = 0.5493061443340549
            dve.wait_ge(cst_in, 16 * 7)
            dve.tensor_scalar(wpos[:], wraw[:], EDGE, None, ALU.is_gt).then_inc(w_tern, 1)
            dve.tensor_scalar(wtern[:], wraw[:], -EDGE, None, ALU.is_lt).then_inc(w_tern, 1)
            dve.wait_ge(w_tern, 2)
            dve.tensor_tensor(wtern[:], wpos[:], wtern[:], ALU.subtract).then_inc(w_tern, 1)
            dve.wait_ge(w_turned, 3)
            dve.wait_ge(pads, 1)
            for ky in range(3):
                for q in range(2):
                    pr, rp = divmod(ky + q, 2)
                    dve.tensor_copy(wst[C * rp:C * rp + C, pr, :, q, :],
                                    ps[0:C, ky, 0:3 * C].rearrange("c (k o) -> c k o", k=3)).then_inc(w_put, 1)

            def moments(st, link):
                dve.nop(nofuse=True)
                link(dve.bn_aggr(mv[:], bn[:]))
                link(dve.tensor_copy(st[:, 0:1], mv[:, 0:1]))
                return dve.scalar_tensor_tensor(st[:, 1:2], mv[:, 0:1], mv[:, 0:1], mv[:, 1:2],
                                                ALU.mult, ALU.add)

            def prep(n, odd):
                link = Chain(dve, prep_at, PREP_LINKS, n)
                wait(dve, x_in[odd], 16 * (n + (2 - odd)))
                for c in range(CHUNKS):
                    ins = dve.bn_stats(bn[:, c], xc[:, odd, ROWS * c:ROWS * c + ROWS].rearrange("p a w -> p (a w)"))
                link(ins)
                moments(stx[:, odd], link).then_inc(x_stats, 1)

            def conv(n, odd):
                link = Chain(dve, conv_at, CONV_LINKS, n)
                wait(dve, x1_out, 16 * n)
                for c in range(CHUNKS):
                    wait(dve, conv_done, n * CHUNKS + (c + 1))
                    dve.scalar_tensor_tensor(
                        x1s[:, ROWS * c:ROWS * c + ROWS].rearrange("p a w -> p (a w)"), ps[:, c % 3, 0:N4],
                        alph[:], xc[:, odd, ROWS * c:ROWS * c + ROWS].rearrange("p a w -> p (a w)"),
                        ALU.mult, ALU.add).then_inc(x1_done, 1)
                wait(dve, x1_done, (n + 1) * CHUNKS)
                for c in range(CHUNKS):
                    ins = dve.bn_stats(bn[:, c], x1s[:, ROWS * c:ROWS * c + ROWS].rearrange("p a w -> p (a w)"))
                link(ins)
                moments(sty[:, odd], link).then_inc(x1_stats, 1)

            def rest(n, odd):
                link = Chain(dve, rest_at, REST_LINKS, n)
                wait(dve, x1_group, n + 1)
                wait(dve, dc_done, n)
                link(dve.tensor_copy(gst[:, 0:2], ps[:, 7, 0:2]))
                link(dve.scalar_tensor_tensor(gst[:, 2:3], gst[:, 0:1], gst[:, 0:1], gst[:, 1:2],
                                              ALU.mult, ALU.subtract))
                wait(dve, dft_copied, n * GROUPS)
                dve.tensor_scalar(gst[:, 3:4], gst[:, 2:3], -1.0, GN_EPS, ALU.mult, ALU.add).then_inc(x1_var, 1)
                wait(dve, x1_std, n + 1)
                link(dve.reciprocal(rstd[:], rstd[:]))
                dve.scalar_tensor_tensor(dc[:], gst[:, 0:1], -float(H), rstd[:], ALU.mult, ALU.mult).then_inc(x1_rstd, 1)
                wait(dve, x1_rstd, n + 1)
                wait(dve, dft_copied, n * GROUPS + (C // 4 + 1))
                dve.tensor_tensor(freq[0:C, 0, 0:1], freq[0:C, 0, 0:1], dc[0:C], ALU.add).then_inc(dc_done, 1)

            overlapped(dve, B, prep, conv, rest)

        @block.scalar
        def _(act):
            act.wait_ge(pads, 1)

            def prep(n, odd):
                wait(act, x_mean, n + 1)
                act.activation(negm[:, odd:odd + 1], ps[:, 3, 0:1], ACT.Copy, scale=-1.0).then_inc(neg_mean, 1)
                wait(act, neg_mean, n + 1)
                wait(act, conv_done, (n - 1) * CHUNKS)
                act.activation(signs[C:P, odd, 0:J, 1:W + 1], xc[0:C, odd], ACT.Sign,
                               bias=negm[0:C, odd:odd + 1]).then_inc(signed, 1)
                act.activation(signs[0:C, odd, 1:J + 1, 1:W + 1], xc[C:P, odd], ACT.Sign,
                               bias=negm[C:P, odd:odd + 1]).then_inc(signed, 1)

            def rest(n, odd):
                wait(act, x1_var, n + 1)
                act.activation(rstd[:], gst[:, 3:4], ACT.Sqrt).then_inc(x1_std, 1)
                for g in range(C // 4):
                    wait(act, dft_done, n * GROUPS + (g + 1))
                    act.activation(yw[0:W, :, :, 4 * g:4 * g + 4].rearrange("w r k c -> w c k r"),
                                   ps[0:W, 4 + g % 3, 0:4 * H].rearrange("w (c k r) -> w c k r", c=4, r=2),
                                   ACT.Copy).then_inc(dft_copied, 1)
                wait(act, x1_rstd, n + 1)
                wait(act, freq_out, 16 * n)
                for g in range(KP // 4):
                    wait(act, dft_done, n * GROUPS + (C // 4 + g + 1))
                    act.activation(freq[:, 4 * g:4 * g + 4, 0:FR],
                                   ps[:, 4 + (C // 4 + g) % 3, 0:4 * FR].rearrange("p (k f) -> p k f", k=4), ACT.Copy,
                                   scale=rstd[:]).then_inc(dft_copied, 1)

            overlapped(act, B, prep, lambda n, odd: None, rest)

        @block.tensor
        def _(pe):
            pe.wait_ge(w_tern, 3)
            for ky in range(3):
                for kx in range(3):
                    ins = pe.transpose(ps[0:C, ky, C * kx:C * kx + C], wtern[:, :, 3 * ky + kx], ident[0:C, 0:C])
                ins.then_inc(w_turned, 1)
            pe.wait_ge(w_put, 6)

            def prep(n, odd):
                wait(pe, x_stats, n + 1)
                wait(pe, neg_mean, n)
                pe.matmul(ps[:, 3, 0:2], group[:], stx[:, odd], start=True, stop=True,
                          skip_group_check=True).then_inc(x_mean, 1)

            def conv(n, odd):
                wait(pe, signed, 2 * (n + 1))
                for c in range(CHUNKS):
                    wait(pe, x1_done, n * CHUNKS + max(c - 2, 0))
                    for t in range(6):
                        pr, kx = divmod(t, 3)
                        ins = pe.matmul(ps[:, c % 3, 0:N4], wst[:, pr, kx].rearrange("p q o -> p (q o)"),
                                        signs[:, odd, ROWS * c + pr:ROWS * c + pr + ROWS, kx:kx + W],
                                        start=(t == 0), stop=(t == 5))
                    ins.then_inc(conv_done, 1)

            def rest(n, odd):
                wait(pe, x1_stats, n + 1)
                wait(pe, x1_var, n)
                pe.matmul(ps[:, 7, 0:2], group[:], sty[:, odd], start=True, stop=True,
                          skip_group_check=True).then_inc(x1_group, 1)
                wait(pe, xh_in, 32 * (n + 1))
                for g in range(C // 4):
                    wait(pe, dft_copied, n * GROUPS + max(g - 2, 0))
                    for c in range(4):
                        ins = pe.matmul(ps[0:W, 4 + g % 3, H * c:H * c + H], xh[0:H, 4 * g + c], fh[:],
                                        start=(c == 0), stop=(c == 3), skip_group_check=True)
                    ins.then_inc(dft_done, 1)
                for g in range(KP // 4):
                    wait(pe, dft_copied, n * GROUPS + (C // 4 if g == 0 else C // 4 + g - 2))
                    for k in range(4 * g, 4 * g + 4):
                        for r in range(2):
                            ins = pe.matmul(ps[:, 4 + (C // 4 + g) % 3, FR * (k % 4):FR * (k % 4) + FR],
                                            yw[0:W, r, 2 * k:2 * k + 2].rearrange("w k c -> w (k c)"), fw[:, r],
                                            start=(k % 4 == 0 and r == 0), stop=(k % 4 == 3 and r == 1),
                                            skip_group_check=True)
                    ins.then_inc(dft_done, 1)

            overlapped(pe, B, prep, conv, rest)


def mix_frequencies(nc, B, weight, xf, yf):
    with ExitStack() as ctx:
        sb = lambda name, shape, dt=F32: ctx.enter_context(nc.sbuf_tensor("b_" + name, shape, dt))
        sem = lambda name: ctx.enter_context(nc.semaphore("b_" + name))
        ps = ctx.enter_context(nc.psum_tensor("b_ps", [P, 8, BANK], F32))
        wt = sb("wt", [P, 2, C, FP // 2, 2])
        xs = sb("xs", [P, 2, B, FP // 2, 2])
        xj = sb("xj", [P, 2, B, FP // 2, 2])
        ys = sb("ys", [P, 2, B, FP // 2, 2])
        loaded = [sem("loaded0"), sem("loaded1")]
        turned = sem("turned")
        mixed = [sem("mixed_low"), sem("mixed_high")]
        copied = [sem("copied_low"), sem("copied_high")]
        stored = [sem("stored0"), sem("stored1")]
        padded = sem("padded")
        PER = min(BANK // (2 * B), 8)
        GROUPS = -(-KW // PER)

        block = ctx.enter_context(nc.Block())

        @block.sync
        def _(sp):
            def load(k, odd):
                for half in range(2):
                    wait(sp, mixed[half], (k - 1) * GROUPS)
                src = weight.rearrange("c o (k two) w r -> two k c o w r", two=2)
                for half in range(2):
                    sp.dma_start(wt[C * half:C * half + C, odd],
                                 src[half, bass.ds(k, 1)].rearrange("k c o w r -> (k c) o (w r)")
                                 ).then_inc(loaded[odd], 16)
                sp.dma_start(xs[:, odd], xf[bass.ds(k, 1)].rearrange("k p b f -> (k p) (b f)")).then_inc(loaded[odd], 16)

            load(0, 0)
            load(1, 1)
            with sp.Fori(0, KP // 2 - 1) as t:
                for odd in range(2):
                    load(2 * t + (2 + odd), odd)

        @block.gpsimd
        def _(pool):
            pool.memset(ys[:], 0.0).then_inc(padded, 1)

            def turn(k, odd):
                wait(pool, loaded[odd], 24 * (k + (2 - odd)))
                for half in range(2):
                    wait_apart(pool, mixed[half], (k - 1) * GROUPS)
                pool.tensor_scalar(xj[:, odd, :, 0:KW, 0], xs[:, odd, :, 0:KW, 1], -1.0, None, ALU.mult).then_inc(turned, 1)
                pool.tensor_copy(xj[:, odd, :, 0:KW, 1], xs[:, odd, :, 0:KW, 0]).then_inc(turned, 1)

            def store(k, odd):
                for half in range(2):
                    wait(pool, copied[half], (k + 1) * GROUPS)
                pool.dma_start(yf[bass.ds(k, 1)].rearrange("k p b f -> (k p) (b f)"), ys[:, odd]
                               ).then_inc(stored[odd], 16)

            def step(t):
                for odd in range(2):
                    turn(2 * t + (1 + odd), 1 - odd)
                    store(2 * t + odd, odd)

            turn(0, 0)
            pairs(pool, KP, step)
            turn(KP - 1, 1)
            store(KP - 2, 0)
            store(KP - 1, 1)
            for odd in range(2):
                pool.wait_ge(stored[odd], 16 * (KP // 2))

        def take(eng, copy, half):
            def body(k, odd):
                wait(eng, stored[odd], 8 * (k - odd))
                for g in range(GROUPS):
                    lo, hi = g * PER, min(g * PER + PER, KW)
                    wait(eng, mixed[half], k * GROUPS + (g + 1))
                    copy(ys[C * half:C * half + C, odd, :, lo:hi].rearrange("p b w r -> p w b r"),
                         ps[C * half:C * half + C, 4 * half + g % 4, 0:2 * B * (hi - lo)].rearrange(
                             "p (w b r) -> p w b r", b=B, r=2)).then_inc(copied[half], 1)
            eng.wait_ge(padded, 1)
            body(0, 0)
            body(1, 1)
            with eng.Fori(1, KP // 2) as t:
                for odd in range(2):
                    body(2 * t + odd, odd)

        @block.scalar
        def _(act):
            take(act, lambda o, i: act.activation(o, i, ACT.Copy), 0)

        @block.vector
        def _(dve):
            take(dve, lambda o, i: dve.tensor_copy(o, i), 1)

        @block.tensor
        def _(pe):
            def body(k, odd):
                wait(pe, loaded[odd], 24 * (k + (2 - odd)))
                wait(pe, turned, 2 * (k + 1))
                for g in range(GROUPS):
                    lo, hi = g * PER, min(g * PER + PER, KW)
                    for half in range(2):
                        rows = slice(C * half, C * half + C)
                        wait_apart(pe, copied[half], k * GROUPS + (g - 3))
                        for f in range(lo, hi):
                            at = 2 * B * (f - lo)
                            for r, src in ((0, xs), (1, xj)):
                                ins = pe.matmul(ps[rows, 4 * half + g % 4, at:at + 2 * B], wt[rows, odd, :, f, r],
                                                src[rows, odd, :, f], start=(f == lo and r == 0),
                                                stop=(f == hi - 1 and r == 1), skip_group_check=True)
                        ins.then_inc(mixed[half], 1)
            body(0, 0)
            body(1, 1)
            with pe.Fori(1, KP // 2) as t:
                for odd in range(2):
                    body(2 * t + odd, odd)


WS = 8
TOK = WS * WS
A7 = H // (2 * WS)
Q7 = W // (2 * WS)
QTOK = Q7 * 2 * TOK
CONV_MMS = 28 * 3
NCH = 15
EPS = 1e-6


def prepare_weights(nc, args, cst, to):
    with ExitStack() as ctx:
        sb = lambda name, shape, dt=F32: ctx.enter_context(nc.sbuf_tensor("w_" + name, shape, dt))
        sem = lambda name: ctx.enter_context(nc.semaphore("w_" + name))
        ps = ctx.enter_context(nc.psum_tensor("w_ps", [P, 8, BANK], F32))
        conv_w = sb("conv_w", [P, C, 49])
        taps = sb("taps", [P, 25, P])
        stencil = sb("stencil", [P, WS, 25])
        qkw = sb("qkw", [P, C])
        vw = sb("vw", [C, C])
        pw = sb("pw", [C, C])
        qkvb = sb("qkvb", [P, 3 * C])
        pos = sb("pos", [P, C])
        scale = sb("scale", [P, C])
        soft = sb("soft", [P, C])
        inv_sc = sb("inv_sc", [P, C])
        top = sb("top", [P, 1])
        up = sb("up", [P, 1])
        sbias = sb("sbias", [P, 1])
        pb = sb("pb", [P, 1])
        loaded, act_at, dve_at = sem("loaded"), sem("act_at"), sem("dve_at")
        cleared, turned, put, bias_sum = sem("cleared"), sem("turned"), sem("put"), sem("bias_sum")
        soft_done, scaled_up = sem("soft_done"), sem("scaled_up")
        LOADS = [
            (to["ident"][:], cst["ident"]), (to["group"][:], cst["group"]), (to["head"][:], cst["head"]),
            (to["inv_h"][:], cst["inv_h"].rearrange("p (r h) -> p r h", r=2)), (to["inv_w"][:], cst["inv_w"]),
            (taps[:], cst["taps"].rearrange("p (t q) -> p t q", t=25)),
            (conv_w[0:C], args["L2_conv_weight"].rearrange("o c h w -> o c (h w)")),
            (conv_w[C:P], args["L2_conv_weight"].rearrange("o c h w -> o c (h w)")),
            (to["cbias"][0:C], args["L2_conv_bias"]), (to["cbias"][C:P], args["L2_conv_bias"]),
            (stencil[:].rearrange("p d t -> p (d t)"),
             args["L3_conv_dwc_w"].rearrange("d i h w -> (d i h w)").partition_broadcast(P)),
            (qkw[:], args["L3_conv_qkv_w"][0:P]), (vw[:], args["L3_conv_qkv_w"][P:3 * C]),
            (pw[:], args["L3_conv_proj_w"]),
            (qkvb[:], args["L3_conv_qkv_b"].partition_broadcast(P)),
            (pos[0:C], args["L3_conv_pos_enc"].rearrange("i t c -> (i t) c")),
            (pos[C:P], args["L3_conv_pos_enc"].rearrange("i t c -> (i t) c")),
            (scale[:], args["L3_conv_scale"].rearrange("i j c -> (i j c)").partition_broadcast(P)),
            (pb[0:C], args["L3_conv_proj_b"]), (pb[C:P], args["L3_conv_proj_b"]),
        ] + [(sbias[WS * h:WS * h + WS], args["L3_conv_dwc_b"]) for h in range(P // WS)]
        block = ctx.enter_context(nc.Block())

        @block.sync
        def _(sp):
            for dst, src in LOADS:
                if len(src.shape) == 1:
                    src = src.rearrange("(c i) -> c i", i=1)
                sp.dma_start(dst, src).then_inc(loaded, 16)

        @block.gpsimd
        def _(pool):
            pool.memset(to["wst"][:], 0.0)
            pool.memset(to["wproj"][:], 0.0)
            pool.memset(to["wqkv"][:], 0.0).then_inc(cleared, 1)

        @block.scalar
        def _(act):
            link = Chain(act, act_at, 0, 0)
            act.wait_ge(loaded, 16 * len(LOADS))
            link(act.activation(soft[:], scale[:], ACT.Abs))
            link(act.activation(soft[:], soft[:], ACT.Exp, scale=-1.0))
            act.activation(soft[:], soft[:], ACT.Ln, bias=1.0).then_inc(soft_done, 1)

        @block.tensor
        def _(pe):
            pe.wait_ge(loaded, 16 * len(LOADS))
            pe.transpose(ps[0:C, 7, 0:P], qkw[:], to["ident"][:])
            pe.transpose(ps[0:C, 7, P:P + C], vw[:], to["ident"][0:C, 0:C])
            pe.transpose(ps[0:C, 7, P + C:2 * P], pw[:], to["ident"][0:C, 0:C]).then_inc(turned, 1)
            pe.wait_ge(scaled_up, 1)
            for ky in range(7):
                for kx in range(7):
                    ins = pe.transpose(ps[0:C, ky, C * kx:C * kx + C], conv_w[0:C, :, 7 * ky + kx],
                                       to["ident"][0:C, 0:C])
                ins.then_inc(turned, 1)
            pe.wait_ge(put, 1)
            pe.matmul(ps[:, 7, 0:1], to["wproj"][:].rearrange("p r c -> p (r c)"), sbias[:],
                      start=True, stop=True).then_inc(bias_sum, 1)

        @block.vector
        def _(dve):
            link = Chain(dve, dve_at, 0, 0)
            dve.wait_ge(loaded, 16 * len(LOADS))
            link(dve.tensor_reduce(top[:], conv_w[:].rearrange("p c t -> p (c t)"), AX.X, ALU.max,
                                   apply_absolute_value=True))
            link(dve.tensor_scalar(top[:], top[:], 1e-30, None, ALU.max))
            link(dve.reciprocal(up[:], top[:]))
            dve.tensor_scalar(to["unscale"][:], top[:], 1.0 / 256, None, ALU.mult)
            dve.tensor_scalar(conv_w[:], conv_w[:], up[:], 256.0, ALU.mult, ALU.mult).then_inc(scaled_up, 1)
            dve.wait_ge(soft_done, 1)
            link(dve.scalar_tensor_tensor(soft[:], scale[:], 0.0, soft[:], ALU.max, ALU.add))
            link(dve.reciprocal(inv_sc[:], soft[:]))
            link(dve.tensor_tensor(qkvb[:, C:2 * C], qkvb[:, C:2 * C], pos[:], ALU.add))
            for r in range(2):
                for k in range(2):
                    dve.tensor_tensor(to["bqk"][:, k, r], qkvb[:, C * k:C * k + C], inv_sc[:], ALU.mult)
                dve.tensor_copy(to["bv"][:, C * r:C * r + C], qkvb[:, 2 * C:3 * C])
            for k in range(4):
                dve.tensor_scalar(to["epsc"][:, k], inv_sc[:], EPS, None, ALU.mult)
            dve.wait_ge(turned, 1)
            dve.wait_ge(cleared, 1)
            for r in range(2):
                rows = slice(C * r, C * r + C)
                for k in range(2):
                    dve.tensor_tensor(to["wqkv"][rows, k, r], ps[0:C, 7, C * k:C * k + C], inv_sc[0:C], ALU.mult)
                dve.tensor_copy(to["wqkv"][rows, 2, r], ps[0:C, 7, P:P + C])
                ins = dve.tensor_copy(to["wproj"][rows, r], ps[0:C, 7, P + C:2 * P])
            ins.then_inc(put, 1)
            for ky in range(7):
                dve.wait_ge(turned, ky + 2)
                for q in range(2):
                    pr, rp = divmod(ky + q, 2)
                    got = ps[0:C, ky, 0:7 * C].rearrange("c (k o) -> c k o", k=7)
                    high = to["wst"][C * rp:C * rp + C, 0, pr, :, q]
                    link(dve.tensor_copy(high, got))
                    dve.tensor_tensor(to["wst"][C * rp:C * rp + C, 1, pr, :, q], got, high, ALU.subtract)
            for t in range(25):
                for d in range(WS):
                    if t == 0:
                        ins = dve.tensor_scalar(to["spread"][:, d], taps[:, t], stencil[:, d, t:t + 1], None, ALU.mult)
                    else:
                        ins = dve.scalar_tensor_tensor(to["spread"][:, d], taps[:, t], stencil[:, d, t:t + 1],
                                                       to["spread"][:, d], ALU.mult, ALU.add)
                link(ins)
            dve.wait_ge(bias_sum, 1)
            dve.tensor_tensor(to["pbias"][:], ps[:, 7, 0:1], pb[:], ALU.add)


def image_steps(eng, images, bring, both, last):
    def step(t):
        for odd in range(2):
            bring(2 * t + (1 + odd), 1 - odd)
            both(2 * t + (1 + odd), 1 - odd, True)

    bring(0, 0)
    both(0, 0, False)
    pairs(eng, images, step)
    bring(images - 1, 1)
    both(images - 1, 1, True)
    last(images, 0)


def large_conv_and_attention(nc, B, args, cst, x1, yf, out):
    with ExitStack() as keep:
        sb = lambda name, shape, dt=F32: keep.enter_context(nc.sbuf_tensor("c_" + name, shape, dt))
        ident = sb("ident", [P, P])
        group = sb("group", [P, P])
        head = sb("head", [P, P])
        inv_h = sb("inv_h", [P, 2, H])
        inv_w = sb("inv_w", [P, W])
        wst = sb("wst", [P, 2, 4, 7, 2, C], F16)
        unscale = sb("unscale", [P, 1])
        cbias = sb("cbias", [P, 1])
        wqkv = sb("wqkv", [P, 3, 2, C])
        wproj = sb("wproj", [P, 2, C])
        bqk = sb("bqk", [P, 2, 2, C])
        bv = sb("bv", [P, 2 * C])
        epsc = sb("epsc", [P, 4, C])
        spread = sb("spread", [P, WS, P])
        pbias = sb("pbias", [P, 1])
        prepare_weights(nc, args, cst, dict(
            ident=ident, group=group, head=head, inv_h=inv_h, inv_w=inv_w, wst=wst, unscale=unscale,
            cbias=cbias, wqkv=wqkv, wproj=wproj, bqk=bqk, bv=bv, epsc=epsc, spread=spread, pbias=pbias))

        sem = lambda name: keep.enter_context(nc.semaphore("c_" + name))
        ps = keep.enter_context(nc.psum_tensor("c_ps", [P, 8, BANK], F32))
        xr = sb("xr", [P, 2, J, W])
        ys = sb("ys", [P, C, FP])
        z = sb("z", [P, H, C])
        xp = z[:].rearrange("p h c -> p (h c)").bitcast(F16)[:, 0:2 * 59 * 118].rearrange(
            "p (s j w) -> p s j w", s=2, j=59)
        tn = sb("tn", [P, 2, ROWS, W])
        cv = sb("cv", [P, 2, N4])
        bn2 = sb("bn2", [P, CHUNKS, 6])
        bn3 = sb("bn3", [P, CHUNKS, 6])
        mv = sb("mv", [P, 2])
        st = sb("st", [P, 2])
        gst = sb("gst", [P, 4])
        nrm = sb("nrm", [P, 2, 2])
        xn = sb("xn", [P, 2 * Q7, TOK])
        qk = sb("qk", [P, Q7, 2, 2, C])
        v = sb("v", [P, Q7, 2 * C + 2])
        sq = sb("sq", [P, Q7, 2, 2, C])
        cube = sb("cube", [P, Q7, 2, 2, C])
        s2 = sb("s2", [P, 4 * Q7])
        s6 = sb("s6", [P, 4 * Q7])
        fac = sb("fac", [P, 4 * Q7])
        qt = sb("qt", [P, QTOK])
        qs = sb("qs", [P, QTOK])
        km = sb("km", [P, Q7, 2])
        kvm = sb("kvm", [P, 2, Q7, P])
        dw = sb("dw", [P, Q7, 2, WS, WS])
        den = sb("den", [P, QTOK])
        att = sb("att", [P, 2 * Q7, TOK])
        o2 = sb("o2", [P, 8, W])

        x1_in = [sem("x1_in0"), sem("x1_in1")]
        names = """ys_in zeros c1_done c1_taken c2_done x2_done bn_at stats_done grouped var_done std_done
            rstd_done normed hi_done lo_done conv_done conv_taken x3_done xn_done qkv_done qk_taken u_done u2_done
            s2_done u3_done u6_done s6_done ratio_at ratio_done f_done scaled dwc_done dw_taken qt_done qt_taken
            kv_done kvm_done km_done qs_done num_done den_done den_taken ones x2_stats dwt_done inv_done mul_done att_done
            proj_done o2_done xo_done out_done bn3_done""".split()
        s = type("Semaphores", (), {n: sem(n) for n in names})
        block = keep.enter_context(nc.Block())
        spans = [(1 + ROWS * k, min(1 + ROWS * (k + 1), J + 2)) for k in range(NCH)]

        @block.sync
        def _(sp):
            def load_ys(n):
                wait(sp, s.c1_done, 16 * n)
                src = yf[:, :, bass.ds(n, 1)].rearrange("k (kp o) b f -> (k kp) o (b f)", kp=2)
                sp.dma_start(ys[0:KH], src).then_inc(s.ys_in, 16)
                sp.dma_start(ys[64:64 + KH, :, 0:FP - 1], src[:, :, 1:FP]).then_inc(s.ys_in, 16)

            def load_x1(n, odd):
                sp.dma_start(xr[:, odd], x1[bass.ds(n, 1)].rearrange("b hp c j w -> (b hp c) j w")
                             ).then_inc(x1_in[odd], 16)

            def store(n, odd):
                for a in range(A7):
                    wait(sp, s.xo_done, n * A7 + (a + 1))
                    for hp in range(2):
                        dst = out[bass.ds(n, 1), :, 16 * a:16 * a + 16].rearrange(
                            "b c (j hp) w -> hp (b c) j w", hp=2)[hp]
                        sp.dma_start(dst, xr[C * hp:C * hp + C, odd, 8 * a:8 * a + 8]).then_inc(s.out_done, 16)

            sp.wait_ge(s.zeros, 1)
            load_ys(0)
            load_x1(0, 0)
            load_ys(1)
            load_x1(1, 1)

            def step(t):
                for odd in range(2):
                    load_ys(2 * t + (2 + odd))
                    store(2 * t + odd, odd)
                    wait(sp, s.out_done, (2 * t + (1 + odd)) * (A7 * 32))
                    load_x1(2 * t + (2 + odd), odd)

            pairs(sp, B, step)
            store(B - 2, 0)
            store(B - 1, 1)
            sp.wait_ge(s.out_done, B * A7 * 32)

        @block.tensor
        def _(pe):
            at = [0]
            pe.wait_ge(s.ones, 1)

            def conv_some(n, upto):
                while at[0] < upto:
                    c, i = divmod(at[0], CONV_MMS)
                    t, part = divmod(i, 3)
                    pr, kx = divmod(t, 7)
                    if i == 0:
                        wait(pe, s.lo_done, n * NCH + min(c + 2, NCH))
                        wait(pe, s.conv_taken, n * CHUNKS + (c - 1))
                    ws, xs = ((0, 0), (0, 1), (1, 0))[part]
                    ins = pe.matmul(ps[:, c % 2, 0:N4], wst[:, ws, pr, kx].rearrange("p q o -> p (q o)"),
                                    xp[:, xs, ROWS * c + pr:ROWS * c + pr + ROWS, kx:kx + W],
                                    start=(i == 0), stop=(i == CONV_MMS - 1))
                    if i == CONV_MMS - 1:
                        ins.then_inc(s.conv_done, 1)
                    at[0] += 1

            def stats(count):
                wait(pe, s.stats_done, count + 1)
                wait(pe, s.rstd_done, count)
                pe.matmul(ps[:, 7, 0:2], group[:], st[:], start=True, stop=True).then_inc(s.grouped, 1)

            def bring(n, odd):
                wait(pe, s.ys_in, 32 * (n + 1))
                wait(pe, s.o2_done, (n - 1) * A7)
                for g in range(16):
                    if g >= 5:
                        wait_apart(pe, s.c1_taken, n * 16 + (g - 4))
                    for o in range(4 * g, 4 * g + 4):
                        for r in range(2):
                            ins = pe.matmul(ps[64 * r:64 * r + 64, 2 + g % 5, H * (o % 4):H * (o % 4) + H],
                                            ys[0:120, o, 0:FP:2], inv_h[0:120, r],
                                            start=(o % 4 == 0), stop=(o % 4 == 3), skip_group_check=True)
                    ins.then_inc(s.c1_done, 1)
                if not isinstance(n, int) or n:
                    stats(2 * n - 1)
                wait(pe, s.c1_taken, n * 16 + 16)
                for g in range(CHUNKS):
                    wait(pe, s.x2_done, n * CHUNKS + max(g - 4, 0))
                    for j in range(4 * g, 4 * g + 4):
                        ins = pe.matmul(ps[:, 2 + g % 5, W * (j % 4):W * (j % 4) + W],
                                        z[:, 2 * j:2 * j + 2].rearrange("p h c -> p (h c)"), inv_w[:],
                                        start=(j % 4 == 0), stop=(j % 4 == 3), skip_group_check=True)
                    ins.then_inc(s.c2_done, 1)
                stats(2 * n)

            def attend(l, a, conv):
                wait(pe, s.xn_done, l + 1)
                wait(pe, s.o2_done, l)
                for q in range(Q7):
                    if q == 6:
                        wait(pe, s.qk_taken, 3 * l + 1)
                    ins = pe.matmul(ps[:, 2 + q % 6, 0:6 * C], xn[:, 2 * q:2 * q + 2].rearrange("p w t -> p (w t)"),
                                    wqkv[:].rearrange("p k r c -> p (k r c)"), start=True, stop=True)
                    if q in (3, 5, 6):
                        ins.then_inc(s.qkv_done, 1)
                conv(10)
                wait(pe, s.qk_taken, 3 * l + 3)
                for d in range(WS):
                    ins = pe.matmul(ps[:, 3 + d // 4, 112 * (d % 4):112 * (d % 4) + 112], spread[:, d],
                                    v[:, :, 0:2 * C].rearrange("p q (r h d) -> p q r h d", r=2, d=WS)[:, :, :, :, d],
                                    start=(d % 4 == 0), stop=(d % 4 == 3), skip_group_check=True)
                ins.then_inc(s.dwc_done, 1)
                conv(100)
                wait(pe, s.scaled, l + 1)
                for q in range(Q7):
                    ins = pe.transpose(ps[:, 5 + q // 4, P * (q % 4):P * (q % 4) + P], cube[:, q, 0].rearrange("p r c -> p (r c)"), ident[:])
                ins.then_inc(s.qt_done, 1)
                conv(105)
                for w in range(2):
                    if w == 0:
                        wait_apart(pe, s.dw_taken, l + 1)
                    else:
                        wait_apart(pe, s.qt_taken, l + 1)
                    rows = slice(TOK * w, TOK * w + TOK)
                    for q in range(Q7):
                        ins = pe.matmul(ps[:, 2 + 3 * w + q // 3, 129 * (q % 3):129 * (q % 3) + 129],
                                        cube[rows, q, 1].rearrange("p r c -> p (r c)"), v[rows, q, 0:129],
                                        start=(q % 3 == 0), stop=(q % 3 == 2 or q == 6), skip_group_check=True)
                    ins.then_inc(s.kv_done, 1)
                conv(120)
                wait(pe, s.kvm_done, 6 * l + 6)
                wait(pe, s.km_done, 2 * l + 2)
                for q in range(Q7):
                    for w in range(2):
                        col = (2 * q + w) * TOK
                        ins = pe.matmul(ps[:, 2 + col // BANK, col % BANK:col % BANK + TOK], kvm[:, w, q],
                                        qt[:, col:col + TOK], start=(col % BANK == 0),
                                        stop=(col % BANK == BANK - TOK or col == QTOK - TOK), skip_group_check=True)
                ins.then_inc(s.num_done, 1)
                wait(pe, s.qs_done, l + 1)
                for lo, hi in ((0, BANK), (BANK, QTOK)):
                    ins = pe.matmul(ps[:, 5 + lo // BANK, 0:hi - lo], head[:], qs[:, lo:hi], start=True, stop=True)
                ins.then_inc(s.den_done, 1)
                for q in range(Q7):
                    ins = pe.transpose(ps[:, 4 + 3 * (q // 4), P * (q % 4):P * (q % 4) + P],
                                       dw[:, q].rearrange("p r h d -> p (r h d)"), ident[:])
                ins.then_inc(s.dwt_done, 1)
                conv(145)
                wait(pe, s.att_done, l + 1)
                for y in range(2):
                    ins = pe.matmul(ps[:, 5 + y, 0:N4], wproj[:].rearrange("p r c -> p (r c)"),
                                    att[:].rearrange("p w (y x) -> p y w x", y=WS)[:, 4 * y:4 * y + 4],
                                    start=True, stop=True)
                ins.then_inc(s.proj_done, 1)
                conv(2 * CONV_MMS)

            def both(n, odd, attention):
                at[0] = 0
                if attention:
                    wait(pe, s.x2_done, (n + 1) * CHUNKS)
                    wait_apart(pe, s.rstd_done, 2 * n + 1)
                    for a in range(A7):
                        attend((n - 1) * A7 + a, a, lambda k: conv_some(n, 2 * CONV_MMS * a + k))
                else:
                    conv_some(n, CHUNKS * CONV_MMS)

            def last(n, odd):
                stats(2 * n - 1)
                wait(pe, s.rstd_done, 2 * n)
                for a in range(A7):
                    attend((n - 1) * A7 + a, a, lambda k: None)

            image_steps(pe, B, bring, both, last)

        @block.scalar
        def _(act):
            def deviation(count):
                wait(act, s.var_done, count + 1)
                act.activation(gst[:, 3:4], gst[:, 3:4], ACT.Sqrt).then_inc(s.std_done, 1)

            def bring(n, odd):
                wait(act, s.conv_done, n * CHUNKS)
                for g in range(16):
                    wait(act, s.c1_done, n * 16 + (g + 1))
                    act.activation(z[:, :, 4 * g:4 * g + 4].rearrange("p h o -> p o h"),
                                   ps[:, 2 + g % 5, 0:4 * H].rearrange("p (o h) -> p o h", o=4), ACT.Copy
                                   ).then_inc(s.c1_taken, 1)
                if not isinstance(n, int) or n:
                    deviation(2 * n - 1)
                deviation(2 * n)
                wait(act, s.rstd_done, 2 * n + 1)
                for k, (lo, hi) in enumerate(spans):
                    wait(act, s.lo_done, n * NCH + (k - 1))
                    if k == 0:
                        act.activation(tn[0:C, 0, 0:1], xr[C:P, odd, 0:1], ACT.Copy, scale=0.0)
                    a = max(lo, 2)
                    act.activation(tn[0:C, k % 2, a - lo:hi - lo], xr[C:P, odd, a - 2:hi - 2], ACT.Identity,
                                   scale=nrm[C:P, 0, 0:1], bias=nrm[C:P, 0, 1:2])
                    if k < NCH - 1:
                        ins = act.activation(tn[C:P, k % 2, 0:hi - lo], xr[0:C, odd, lo - 1:hi - 1], ACT.Identity,
                                             scale=nrm[0:C, 0, 0:1], bias=nrm[0:C, 0, 1:2])
                    else:
                        ins = act.activation(tn[C:P, k % 2, 0:1], xr[0:C, odd, 0:1], ACT.Copy, scale=0.0)
                    ins.then_inc(s.normed, 1)

            def take_conv(n, c):
                wait(act, s.conv_done, n * CHUNKS + (c + 1))
                wait(act, s.x3_done, n * CHUNKS + (c - 1))
                act.activation(cv[:, c % 2], ps[:, c % 2, 0:N4], ACT.Identity, scale=unscale[:], bias=cbias[:]
                               ).then_inc(s.conv_taken, 1)

            def attend(l, a, odd, conv):
                wait(act, s.qkv_done, 3 * l)
                for wr in range(2):
                    for hp in range(2):
                        ins = act.activation(
                            xn[C * wr:C * wr + C].rearrange("p w (j hp x) -> p hp j w x", hp=2, x=WS)[:, hp],
                            xr[C * hp:C * hp + C, odd, 8 * a + 4 * wr:8 * a + 4 * wr + 4].rearrange(
                                "p j (w x) -> p j w x", x=WS),
                            ACT.Identity, scale=nrm[C * hp:C * hp + C, 1, 0:1], bias=nrm[C * hp:C * hp + C, 1, 1:2])
                ins.then_inc(s.xn_done, 1)
                conv(-1)
                wait(act, s.u_done, l + 1)
                wait(act, s.s6_done, l)
                act.activation(sq[:], qk[:], ACT.Square).then_inc(s.u2_done, 1)
                wait(act, s.dwc_done, l + 1)
                wait(act, s.dwt_done, l)
                for b in range(2):
                    ins = act.activation(
                        dw[:].rearrange("p q r h d -> p d (q r h)")[:, 4 * b:4 * b + 4],
                        ps[:, 3 + b, 0:448].rearrange("p (d x) -> p d x", d=4), ACT.Copy)
                ins.then_inc(s.dw_taken, 1)
                wait(act, s.u3_done, l + 1)
                wait(act, s.s2_done, l + 1)
                act.activation(sq[:], cube[:], ACT.Square).then_inc(s.u6_done, 1)
                wait(act, s.ratio_done, l + 1)
                act.activation(fac[:], fac[:], ACT.Sqrt).then_inc(s.f_done, 1)
                conv(0)
                wait(act, s.qt_done, l + 1)
                wait(act, s.num_done, l)
                wait(act, s.qs_done, l)
                act.activation(qt[:], ps[:, 5:7].rearrange("p b x -> p (b x)")[:, 0:QTOK], ACT.Copy
                               ).then_inc(s.qt_taken, 1)
                wait(act, s.den_done, l + 1)
                wait(act, s.att_done, l)
                act.activation(den[:], ps[:, 5:7].rearrange("p b x -> p (b x)")[:, 0:QTOK], ACT.Copy, bias=EPS
                               ).then_inc(s.den_taken, 1)
                wait(act, s.proj_done, l + 1)
                wait(act, s.xo_done, l)
                for wr in range(2):
                    for hp in range(2):
                        ins = act.activation(
                            o2[C * hp:C * hp + C, 4 * wr:4 * wr + 4].rearrange("p (b j) x -> p b j x", b=2),
                            ps[C * wr:C * wr + C, 5:7, 0:N4].rearrange("p b (j hp x) -> p hp b j x", hp=2, x=W)[:, hp],
                            ACT.Identity, bias=pbias[C * wr:C * wr + C])
                ins.then_inc(s.o2_done, 1)

            def both(n, odd, attention):
                if attention:
                    for a in range(A7):
                        attend((n - 1) * A7 + a, a, 1 - odd, lambda k: take_conv(n, 2 * a + k) if a or k == 0 else None)
                    take_conv(n, CHUNKS - 1)
                else:
                    for c in range(CHUNKS):
                        take_conv(n, c)

            def last(n, odd):
                deviation(2 * n - 1)
                wait(act, s.rstd_done, 2 * n)
                for a in range(A7):
                    attend((n - 1) * A7 + a, a, 1 - odd, lambda k: None)

            image_steps(act, B, bring, both, last)

        @block.vector
        def _(dve):
            dve.wait_ge(s.ones, 1)

            def norm(which, count, bn):
                link = Chain(dve, s.bn_at, 4, count)
                wait_apart(dve, s.grouped, count)
                link(dve.bn_aggr(mv[:], bn[:]))
                dve.tensor_copy(st[:, 0:1], mv[:, 0:1])
                dve.scalar_tensor_tensor(st[:, 1:2], mv[:, 0:1], mv[:, 0:1], mv[:, 1:2], ALU.mult, ALU.add
                                         ).then_inc(s.stats_done, 1)
                wait(dve, s.grouped, count + 1)
                link(dve.tensor_copy(gst[:, 0:2], ps[:, 7, 0:2]))
                link(dve.scalar_tensor_tensor(gst[:, 2:3], gst[:, 0:1], gst[:, 0:1], gst[:, 1:2],
                                              ALU.mult, ALU.subtract))
                dve.tensor_scalar(gst[:, 3:4], gst[:, 2:3], -1.0, GN_EPS, ALU.mult, ALU.add).then_inc(s.var_done, 1)
                wait(dve, s.std_done, count + 1)
                link(dve.reciprocal(nrm[:, which, 0:1], gst[:, 3:4]))
                dve.scalar_tensor_tensor(nrm[:, which, 1:2], gst[:, 0:1], -1.0, nrm[:, which, 0:1],
                                         ALU.mult, ALU.mult).then_inc(s.rstd_done, 1)

            def bring(n, odd):
                if not isinstance(n, int) or n:
                    wait(dve, s.xn_done, (n - 1) * A7)
                    wait(dve, s.bn3_done, n * CHUNKS)
                    norm(1, 2 * n - 1, bn3)
                wait(dve, x1_in[odd], 8 * (n + (2 - odd)))
                for c in range(CHUNKS):
                    wait(dve, s.c2_done, n * CHUNKS + (c + 1))
                    here = xr[:, odd, ROWS * c:ROWS * c + ROWS].rearrange("p a w -> p (a w)")
                    dve.tensor_tensor(here, ps[:, 2 + c % 5, 0:N4], here, ALU.add).then_inc(s.x2_done, 1)
                wait(dve, s.x2_done, (n + 1) * CHUNKS)
                for c in range(CHUNKS):
                    here = xr[:, odd, ROWS * c:ROWS * c + ROWS].rearrange("p a w -> p (a w)")
                    ins = dve.bn_stats(bn2[:, c], here)
                ins.then_inc(s.x2_stats, 1)
                wait(dve, s.x2_stats, n + 1)
                wait(dve, s.normed, n * NCH)
                norm(0, 2 * n, bn2)
                for k, (lo, hi) in enumerate(spans):
                    wait(dve, s.hi_done, n * NCH + (k + 1))
                    dve.tensor_tensor(xp[:, 1, lo:hi, 3:3 + W], tn[:, k % 2, 0:hi - lo], xp[:, 0, lo:hi, 3:3 + W],
                                      ALU.subtract).then_inc(s.lo_done, 1)

            def x3_stats(n, odd, c):
                wait(dve, s.x3_done, n * CHUNKS + (c + 1))
                dve.bn_stats(bn3[:, c], xr[:, odd, ROWS * c:ROWS * c + ROWS].rearrange("p a w -> p (a w)")
                             ).then_inc(s.bn3_done, 1)

            def attend(l, a, conv):
                conv(-1)
                wait(dve, s.u3_done, l)
                wait(dve, s.kv_done, 2 * l)
                for g, (q, n, b) in enumerate(((0, 4, 2), (4, 2, 6), (6, 1, 2))):
                    wait(dve, s.qkv_done, 3 * l + (g + 1))
                    dve.tensor_tensor(qk[:, q:q + n].rearrange("p q k r c -> p q (k r c)"), ps[:, b:b + n, 0:4 * C],
                                      bqk[:].rearrange("p k r c -> p (k r c)").unsqueeze(1).to_broadcast(
                                          [P, n, 4 * C]), ALU.add)
                    dve.tensor_tensor(v[:, q:q + n, 0:2 * C], ps[:, b:b + n, 4 * C:6 * C],
                                      bv[:].unsqueeze(1).to_broadcast([P, n, 2 * C]), ALU.add
                                      ).then_inc(s.qk_taken, 1)
                wait(dve, s.qk_taken, 3 * l + 3)
                flat = qk[:].rearrange("p q k r c -> p q (k r c)")
                dve.scalar_tensor_tensor(flat, flat, 0.0, epsc[:].rearrange("p k c -> p (k c)").unsqueeze(1)
                                         .to_broadcast([P, Q7, 4 * C]), ALU.max, ALU.add).then_inc(s.u_done, 1)
                wait(dve, s.u2_done, l + 1)
                dve.tensor_reduce(s2[:], sq[:].rearrange("p q k r c -> p (q k r) c"), AX.X, ALU.add
                                  ).then_inc(s.s2_done, 1)
                wait(dve, s.u6_done, l + 1)
                dve.tensor_reduce(s6[:], sq[:].rearrange("p q k r c -> p (q k r) c"), AX.X, ALU.add
                                  ).then_inc(s.s6_done, 1)
                wait(dve, s.s6_done, l + 1)
                dve.reciprocal(s6[:], s6[:]).then_inc(s.ratio_at, 1)
                wait(dve, s.ratio_at, l + 1)
                dve.tensor_tensor(fac[:], s2[:], s6[:], ALU.mult).then_inc(s.ratio_done, 1)
                wait(dve, s.f_done, l + 1)
                cubes = cube[:].rearrange("p q k r c -> p (q k r) c")
                dve.tensor_tensor(cubes, cubes, fac[:].unsqueeze(2).to_broadcast([P, 4 * Q7, C]), ALU.mult
                                  ).then_inc(s.scaled, 1)
                conv(0)
                wait(dve, s.num_done, l)
                wait(dve, s.qs_done, l)
                for w in range(2):
                    wait(dve, s.kv_done, 2 * l + (w + 1))
                    dve.tensor_copy(km[:, 0:6, w].rearrange("p (b q) -> p b q", b=2),
                                    ps[:, 2 + 3 * w:4 + 3 * w, 128:387:129])
                    dve.tensor_copy(km[:, 6:7, w], ps[:, 4 + 3 * w, 128:129]).then_inc(s.km_done, 1)
                    for b in range(3):
                        n = min(3, Q7 - 3 * b)
                        dve.tensor_tensor(kvm[:, w, 3 * b:3 * b + n],
                                          ps[:, 2 + 3 * w + b, 0:129 * n].rearrange("p (q x) -> p q x", q=n)[:, :, 0:P],
                                          head[:].unsqueeze(1).to_broadcast([P, n, P]), ALU.mult
                                          ).then_inc(s.kvm_done, 1)
                wait(dve, s.den_taken, l + 1)
                dve.reciprocal(den[:], den[:]).then_inc(s.inv_done, 1)
                wait(dve, s.num_done, l + 1)
                wait(dve, s.inv_done, l + 1)
                wait(dve, s.proj_done, l)
                flat = att[:].rearrange("p w t -> p (w t)")
                dve.tensor_tensor(flat, ps[:, 2:4].rearrange("p b x -> p (b x)")[:, 0:QTOK], den[:], ALU.mult
                                  ).then_inc(s.mul_done, 1)
                wait(dve, s.dwt_done, l + 1)
                wait(dve, s.mul_done, l + 1)
                dve.tensor_tensor(flat[:, 0:BANK], ps[:, 4], flat[:, 0:BANK], ALU.add)
                dve.tensor_tensor(flat[:, BANK:QTOK], ps[:, 7, 0:QTOK - BANK], flat[:, BANK:QTOK], ALU.add
                                  ).then_inc(s.att_done, 1)

            def both(n, odd, attention):
                if attention:
                    for a in range(A7):
                        attend((n - 1) * A7 + a, a, lambda k: x3_stats(n, odd, 2 * a + k) if a or k == 0 else None)
                    x3_stats(n, odd, CHUNKS - 1)
                else:
                    for c in range(CHUNKS):
                        x3_stats(n, odd, c)

            def last(n, odd):
                wait(dve, s.bn3_done, n * CHUNKS)
                wait(dve, s.xn_done, (n - 1) * A7)
                norm(1, 2 * n - 1, bn3)
                for a in range(A7):
                    attend((n - 1) * A7 + a, a, lambda k: None)

            image_steps(dve, B, bring, both, last)

        @block.gpsimd
        def _(pool):
            pool.memset(ys[:], 0.0).then_inc(s.zeros, 1)
            pool.memset(v[:], 1.0).then_inc(s.ones, 1)

            def bring(n, odd):
                wait_apart(pool, s.c2_done, (n + 1) * CHUNKS)
                for lo, hi in ((0, 1), (58, 59)):
                    pool.memset(xp[:, :, lo:hi], 0.0)
                for lo in (0, 115):
                    pool.memset(xp[:, :, 1:58, lo:lo + 3], 0.0)
                for k, (lo, hi) in enumerate(spans):
                    wait(pool, s.normed, n * NCH + (k + 1))
                    pool.tensor_copy(xp[:, 0, lo:hi, 3:3 + W], tn[:, k % 2, 0:hi - lo]).then_inc(s.hi_done, 1)

            def add_conv(n, odd, c):
                wait(pool, s.conv_taken, n * CHUNKS + (c + 1))
                here = xr[:, odd, ROWS * c:ROWS * c + ROWS].rearrange("p a w -> p (a w)")
                pool.tensor_tensor(here, cv[:, c % 2], here, ALU.add).then_inc(s.x3_done, 1)

            def attend(l, a, odd, conv):
                conv(-1)
                wait(pool, s.u2_done, l + 1)
                wait(pool, s.kv_done, 2 * l)
                pool.tensor_tensor(cube[:], sq[:], qk[:], ALU.mult).then_inc(s.u3_done, 1)
                conv(0)
                wait(pool, s.qt_taken, l + 1)
                wait(pool, s.km_done, 2 * l + 2)
                wait(pool, s.den_done, l)
                pool.tensor_tensor(qs[:].rearrange("p (q w t) -> p (q w) t", w=2, t=TOK),
                                   qt[:].rearrange("p (q w t) -> p (q w) t", w=2, t=TOK),
                                   km[:].rearrange("p q w -> p (q w)").unsqueeze(2)
                                   .to_broadcast([P, 2 * Q7, TOK]), ALU.mult).then_inc(s.qs_done, 1)
                wait(pool, s.o2_done, l + 1)
                here = xr[:, odd, 8 * a:8 * a + 8]
                pool.tensor_tensor(here, o2[:], here, ALU.add).then_inc(s.xo_done, 1)

            def both(n, odd, attention):
                if attention:
                    for a in range(A7):
                        attend((n - 1) * A7 + a, a, 1 - odd, lambda k: add_conv(n, odd, 2 * a + k) if a or k == 0 else None)
                    add_conv(n, odd, CHUNKS - 1)
                else:
                    for c in range(CHUNKS):
                        add_conv(n, odd, c)

            def last(n, odd):
                for a in range(A7):
                    attend((n - 1) * A7 + a, a, 1 - odd, lambda k: None)

            image_steps(pool, B, bring, both, last)


def build(nc, a, cst, x1, xf, yf, out):
    B = a["x"].shape[0]
    local_conv_and_forward_dft(nc, B, a["x"], a["L0_conv_weight"],
                               a["L0_conv_alpha"].rearrange("c i j -> c (i j)"), cst, x1, xf)
    mix_frequencies(nc, B, a["L1_conv_weight"], xf, yf)
    large_conv_and_attention(nc, B, a, cst, x1, yf, out)


def kernel(**inputs):
    import numpy as _np
    import concourse.bacc as _bacc
    from concourse import mybir as _mybir
    from concourse.bass_utils import run_bass_kernel_spmd as _run

    nc = _bacc.Bacc("TRN2", target_bir_lowering=False, num_devices=1)
    f32 = _mybir.dt.float32
    arrays, args, cst = {}, {}, {}
    for name, a in inputs.items():
        arrays[f"in_{name}"] = a = _np.ascontiguousarray(a)
        args[name] = nc.dram_tensor(f"in_{name}", a.shape, f32, kind="ExternalInput").ap()
    for name, a in constants().items():
        arrays[f"cst_{name}"] = a
        cst[name] = nc.dram_tensor(f"cst_{name}", a.shape, f32, kind="ExternalInput").ap()
    B = inputs["x"].shape[0]
    x1 = nc.dram_tensor("x1", (B, 2, C, J, W), f32, kind="Internal").ap()
    xf = nc.dram_tensor("xf", (KP, P, B, FP), f32, kind="Internal").ap()
    yf = nc.dram_tensor("yf", (KP, P, B, FP), f32, kind="Internal").ap()
    out = nc.dram_tensor("out", (B, C, H, W), f32, kind="ExternalOutput").ap()
    build(nc, args, cst, x1, xf, yf, out)
    return _run(nc, [arrays], core_ids=[0]).results[0]["out"]
```

```python
from contextlib import ExitStack

import numpy as np

import concourse.bass as bass
from concourse import mybir

ALU = mybir.AluOpType
ACT = mybir.ActivationFunctionType
AX = mybir.AxisListType
F32 = mybir.dt.float32
F16 = mybir.dt.float16
BF16 = mybir.dt.bfloat16

P = 128
C = 64
H = W = 112
J = H // 2
PIX = J * W
KH = H // 2
KW = W // 2 + 1
KP = KH // 2
FR = 2 * KW
FP = 128
ROWS = 4
CHUNKS = J // ROWS
N4 = ROWS * W
BANK = 512
GN_EPS = 1e-5


def wait(eng, sem, value):
    if isinstance(value, int) and value <= 0:
        return
    eng.wait_ge(sem, value)
    if eng.engine in (mybir.EngineType.SP, mybir.EngineType.Pool) and not isinstance(value, int):
        eng.nop(nofuse=True)


def wait_apart(eng, sem, value):
    wait(eng, sem, value)
    if not isinstance(value, int):
        eng.nop(nofuse=True)


class Chain:

    def __init__(self, eng, sem, per, n):
        self.eng, self.sem, self.at = eng, sem, n * per

    def __call__(self, ins):
        ins.then_inc(self.sem, 1)
        self.at = self.at + 1
        self.eng.wait_ge(self.sem, self.at)


def constants():
    k, w = np.arange(KH), np.arange(KW)
    n = np.arange(H)
    ang = 2 * np.pi * np.outer(n, k) / H
    fwd_h = (np.stack([np.cos(ang), -np.sin(ang)], -1).reshape(H, 2 * KH) / H).reshape(J, 2, -1).transpose(1, 0, 2)
    fwd_h = fwd_h.reshape(H, -1)
    aw = 2 * np.pi * np.outer(n, w) / W
    fwd_w = np.concatenate([
        np.stack([np.cos(aw), -np.sin(aw)], -1).reshape(W, FR),
        np.stack([np.sin(aw), np.cos(aw)], -1).reshape(W, FR)], 1)
    inv_h = np.zeros((P, 2, H))
    inv_h[0:KH, 0], inv_h[64:64 + KH, 0] = np.cos(ang).T, -np.sin(ang).T
    inv_h[0:KH, 1], inv_h[64:64 + KH, 1] = np.sin(ang).T, np.cos(ang).T
    inv_w = np.zeros((P, W))
    twice = np.where((w == 0) | (w == W // 2), 1.0, 2.0)[:, None] / W
    inv_w[0:KW], inv_w[64:64 + KW] = np.cos(aw).T * twice, -np.sin(aw).T * twice
    p = np.arange(P)
    group = ((p[:, None] % C) // 2 == (p[None, :] % C) // 2) / 4.0
    head = (p[:, None] // 8 == p[None, :] // 8) / 64.0
    tok = np.arange(P)
    win, y, x = tok // 64, tok % 64 // 8, tok % 8
    taps = np.zeros((P, 25, P))
    for t in range(25):
        ok = ((win[:, None] == win[None, :]) & (y[:, None] == y[None, :] + t // 5 - 2)
              & (x[:, None] == x[None, :] + t % 5 - 2))
        taps[:, t] = ok
    made = dict(fwd_h=fwd_h, fwd_w=fwd_w, inv_h=inv_h.reshape(P, 2 * H), inv_w=inv_w, group=group,
                head=head, ident=np.eye(P), taps=taps.reshape(P, 25 * P))
    return {k: np.ascontiguousarray(v, np.float32) for k, v in made.items()}


def pairs(eng, images, step):
    if images > 2:
        step(0)
    if images > 4:
        with eng.Fori(1, images // 2 - 1) as t:
            step(t)


def overlapped(eng, images, prep, conv, rest):
    def step(t):
        for odd in range(2):
            prep(2 * t + (2 + odd), odd)
            conv(2 * t + (1 + odd), 1 - odd)
            rest(2 * t + odd, odd)

    prep(0, 0)
    prep(1, 1)
    conv(0, 0)
    pairs(eng, images, step)
    conv(images - 1, 1)
    rest(images - 2, 0)
    rest(images - 1, 1)


def local_conv_and_forward_dft(nc, B, x, weight, alpha, cst, x1, xf):
    with ExitStack() as ctx:
        sb = lambda name, shape, dt=F32: ctx.enter_context(nc.sbuf_tensor("a_" + name, shape, dt))
        sem = lambda name: ctx.enter_context(nc.semaphore("a_" + name))
        ps = ctx.enter_context(nc.psum_tensor("a_ps", [P, 8, BANK], F32))
        xc = sb("xc", [P, 2, J, W])
        x1s = sb("x1s", [P, J, W])
        signs = sb("signs", [P, 2, J + 1, W + 2], BF16)
        xh = sb("xh", [P, C, W])
        yw = sb("yw", [P, 2, KH, C])
        freq = sb("freq", [P, KP, FP])
        wraw = sb("wraw", [C, C, 9])
        wpos = sb("wpos", [C, C, 9])
        wtern = sb("wtern", [C, C, 9])
        wst = sb("wst", [P, 2, 3, 2, C], BF16)
        ident = sb("ident", [P, P])
        group = sb("group", [P, P])
        fh = sb("fh", [H, 2 * KH])
        fw = sb("fw", [W, 2, FR])
        alph = sb("alph", [P, 1])
        bn = sb("bn", [P, CHUNKS, 6])
        mv = sb("mv", [P, 2])
        stx = sb("stx", [P, 2, 2])
        sty = sb("sty", [P, 2, 2])
        negm = sb("negm", [P, 2])
        gst = sb("gst", [P, 4])
        rstd = sb("rstd", [P, 1])
        dc = sb("dc", [P, 1])

        cst_in = sem("cst_in")
        pads = sem("pads")
        w_tern = sem("w_tern")
        w_turned = sem("w_turned")
        w_put = sem("w_put")
        x_in = [sem("x_in0"), sem("x_in1")]
        x_stats = sem("x_stats")
        x_mean = sem("x_mean")
        neg_mean = sem("neg_mean")
        signed = sem("signed")
        conv_done = sem("conv_done")
        x1_done = sem("x1_done")
        x1_out = sem("x1_out")
        x1_stats = sem("x1_stats")
        x1_group = sem("x1_group")
        x1_var = sem("x1_var")
        x1_std = sem("x1_std")
        x1_rstd = sem("x1_rstd")
        xh_in = sem("xh_in")
        dft_done = sem("dft_done")
        dft_copied = sem("dft_copied")
        dc_done = sem("dc_done")
        freq_out = sem("freq_out")
        prep_at, conv_at, rest_at = sem("prep_at"), sem("conv_at"), sem("rest_at")
        PREP_LINKS, CONV_LINKS, REST_LINKS = 3, 3, 3
        GROUPS = C // 4 + KP // 4

        block = ctx.enter_context(nc.Block())

        @block.sync
        def _(sp):
            for dst, src in ((wraw[:], weight.rearrange("o c h w -> o c (h w)")), (ident[:], cst["ident"]),
                             (group[:], cst["group"]), (fh[:], cst["fwd_h"]),
                             (fw[:], cst["fwd_w"].rearrange("h (r f) -> h r f", r=2)),
                             (alph[0:C], alpha), (alph[C:P], alpha)):
                sp.dma_start(dst, src).then_inc(cst_in, 16)

            def load(n, odd):
                for hp in range(2):
                    src = x[bass.ds(n, 1)].rearrange("b c (j hp) w -> hp (b c) j w", hp=2)[hp]
                    sp.dma_start(xc[C * hp:C * hp + C, odd], src).then_inc(x_in[odd], 16)

            def turn(n):
                wait(sp, x1_out, 16 * (n + 1))
                wait(sp, dft_done, n * GROUPS)
                for hp in range(2):
                    src = x1[bass.ds(n, 1)].rearrange("b hp c j w -> hp (b j) c w")[hp]
                    sp.dma_start(xh[J * hp:J * hp + J], src).then_inc(xh_in, 16)

            load(0, 0)
            load(1, 1)

            def step(t):
                for odd in range(2):
                    wait(sp, x1_done, (2 * t + (odd + 1)) * CHUNKS)
                    load(2 * t + (2 + odd), odd)
                    turn(2 * t + odd)

            pairs(sp, B, step)
            turn(B - 2)
            turn(B - 1)

        @block.gpsimd
        def _(pool):
            pool.memset(signs[:], 0.0)
            pool.memset(freq[:], 0.0)
            pool.memset(wst[:], 0.0).then_inc(pads, 1)

            def store_x1(n):
                wait(pool, x1_done, (n + 1) * CHUNKS)
                dst = x1[bass.ds(n, 1)].rearrange("b hp c j w -> (b hp c) j w")
                pool.dma_start(dst, x1s[:]).then_inc(x1_out, 16)

            def store_freq(n):
                wait(pool, dft_copied, (n + 1) * GROUPS)
                wait(pool, dc_done, n + 1)
                dst = xf[:, :, bass.ds(n, 1)].rearrange("k p b f -> p k (b f)")
                pool.dma_start(dst, freq[:]).then_inc(freq_out, 16)

            overlapped(pool, B, lambda n, odd: None, lambda n, odd: store_x1(n), lambda n, odd: store_freq(n))
            pool.wait_ge(x1_out, 16 * B)
            pool.wait_ge(freq_out, 16 * B)

        @block.vector
        def _(dve):
            EDGE = 0.5493061443340549
            dve.wait_ge(cst_in, 16 * 7)
            dve.tensor_scalar(wpos[:], wraw[:], EDGE, None, ALU.is_gt).then_inc(w_tern, 1)
            dve.tensor_scalar(wtern[:], wraw[:], -EDGE, None, ALU.is_lt).then_inc(w_tern, 1)
            dve.wait_ge(w_tern, 2)
            dve.tensor_tensor(wtern[:], wpos[:], wtern[:], ALU.subtract).then_inc(w_tern, 1)
            dve.wait_ge(w_turned, 3)
            dve.wait_ge(pads, 1)
            for ky in range(3):
                for q in range(2):
                    pr, rp = divmod(ky + q, 2)
                    dve.tensor_copy(wst[C * rp:C * rp + C, pr, :, q, :],
                                    ps[0:C, ky, 0:3 * C].rearrange("c (k o) -> c k o", k=3)).then_inc(w_put, 1)

            def moments(st, link):
                dve.nop(nofuse=True)
                link(dve.bn_aggr(mv[:], bn[:]))
                link(dve.tensor_copy(st[:, 0:1], mv[:, 0:1]))
                return dve.scalar_tensor_tensor(st[:, 1:2], mv[:, 0:1], mv[:, 0:1], mv[:, 1:2],
                                                ALU.mult, ALU.add)

            def prep(n, odd):
                link = Chain(dve, prep_at, PREP_LINKS, n)
                wait(dve, x_in[odd], 16 * (n + (2 - odd)))
                for c in range(CHUNKS):
                    ins = dve.bn_stats(bn[:, c], xc[:, odd, ROWS * c:ROWS * c + ROWS].rearrange("p a w -> p (a w)"))
                link(ins)
                moments(stx[:, odd], link).then_inc(x_stats, 1)

            def conv(n, odd):
                link = Chain(dve, conv_at, CONV_LINKS, n)
                wait(dve, x1_out, 16 * n)
                for c in range(CHUNKS):
                    wait(dve, conv_done, n * CHUNKS + (c + 1))
                    dve.scalar_tensor_tensor(
                        x1s[:, ROWS * c:ROWS * c + ROWS].rearrange("p a w -> p (a w)"), ps[:, c % 3, 0:N4],
                        alph[:], xc[:, odd, ROWS * c:ROWS * c + ROWS].rearrange("p a w -> p (a w)"),
                        ALU.mult, ALU.add).then_inc(x1_done, 1)
                wait(dve, x1_done, (n + 1) * CHUNKS)
                for c in range(CHUNKS):
                    ins = dve.bn_stats(bn[:, c], x1s[:, ROWS * c:ROWS * c + ROWS].rearrange("p a w -> p (a w)"))
                link(ins)
                moments(sty[:, odd], link).then_inc(x1_stats, 1)

            def rest(n, odd):
                link = Chain(dve, rest_at, REST_LINKS, n)
                wait(dve, x1_group, n + 1)
                wait(dve, dc_done, n)
                link(dve.tensor_copy(gst[:, 0:2], ps[:, 7, 0:2]))
                link(dve.scalar_tensor_tensor(gst[:, 2:3], gst[:, 0:1], gst[:, 0:1], gst[:, 1:2],
                                              ALU.mult, ALU.subtract))
                wait(dve, dft_copied, n * GROUPS)
                dve.tensor_scalar(gst[:, 3:4], gst[:, 2:3], -1.0, GN_EPS, ALU.mult, ALU.add).then_inc(x1_var, 1)
                wait(dve, x1_std, n + 1)
                link(dve.reciprocal(rstd[:], rstd[:]))
                dve.scalar_tensor_tensor(dc[:], gst[:, 0:1], -float(H), rstd[:], ALU.mult, ALU.mult).then_inc(x1_rstd, 1)
                wait(dve, x1_rstd, n + 1)
                wait(dve, dft_copied, n * GROUPS + (C // 4 + 1))
                dve.tensor_tensor(freq[0:C, 0, 0:1], freq[0:C, 0, 0:1], dc[0:C], ALU.add).then_inc(dc_done, 1)

            overlapped(dve, B, prep, conv, rest)

        @block.scalar
        def _(act):
            act.wait_ge(pads, 1)

            def prep(n, odd):
                wait(act, x_mean, n + 1)
                act.activation(negm[:, odd:odd + 1], ps[:, 3, 0:1], ACT.Copy, scale=-1.0).then_inc(neg_mean, 1)
                wait(act, neg_mean, n + 1)
                wait(act, conv_done, (n - 1) * CHUNKS)
                act.activation(signs[C:P, odd, 0:J, 1:W + 1], xc[0:C, odd], ACT.Sign,
                               bias=negm[0:C, odd:odd + 1]).then_inc(signed, 1)
                act.activation(signs[0:C, odd, 1:J + 1, 1:W + 1], xc[C:P, odd], ACT.Sign,
                               bias=negm[C:P, odd:odd + 1]).then_inc(signed, 1)

            def rest(n, odd):
                wait(act, x1_var, n + 1)
                act.activation(rstd[:], gst[:, 3:4], ACT.Sqrt).then_inc(x1_std, 1)
                for g in range(C // 4):
                    wait(act, dft_done, n * GROUPS + (g + 1))
                    act.activation(yw[0:W, :, :, 4 * g:4 * g + 4].rearrange("w r k c -> w c k r"),
                                   ps[0:W, 4 + g % 3, 0:4 * H].rearrange("w (c k r) -> w c k r", c=4, r=2),
                                   ACT.Copy).then_inc(dft_copied, 1)
                wait(act, x1_rstd, n + 1)
                wait(act, freq_out, 16 * n)
                for g in range(KP // 4):
                    wait(act, dft_done, n * GROUPS + (C // 4 + g + 1))
                    act.activation(freq[:, 4 * g:4 * g + 4, 0:FR],
                                   ps[:, 4 + (C // 4 + g) % 3, 0:4 * FR].rearrange("p (k f) -> p k f", k=4), ACT.Copy,
                                   scale=rstd[:]).then_inc(dft_copied, 1)

            overlapped(act, B, prep, lambda n, odd: None, rest)

        @block.tensor
        def _(pe):
            pe.wait_ge(w_tern, 3)
            for ky in range(3):
                for kx in range(3):
                    ins = pe.transpose(ps[0:C, ky, C * kx:C * kx + C], wtern[:, :, 3 * ky + kx], ident[0:C, 0:C])
                ins.then_inc(w_turned, 1)
            pe.wait_ge(w_put, 6)

            def prep(n, odd):
                wait(pe, x_stats, n + 1)
                wait(pe, neg_mean, n)
                pe.matmul(ps[:, 3, 0:2], group[:], stx[:, odd], start=True, stop=True,
                          skip_group_check=True).then_inc(x_mean, 1)

            def conv(n, odd):
                wait(pe, signed, 2 * (n + 1))
                for c in range(CHUNKS):
                    wait(pe, x1_done, n * CHUNKS + max(c - 2, 0))
                    for t in range(6):
                        pr, kx = divmod(t, 3)
                        ins = pe.matmul(ps[:, c % 3, 0:N4], wst[:, pr, kx].rearrange("p q o -> p (q o)"),
                                        signs[:, odd, ROWS * c + pr:ROWS * c + pr + ROWS, kx:kx + W],
                                        start=(t == 0), stop=(t == 5))
                    ins.then_inc(conv_done, 1)

            def rest(n, odd):
                wait(pe, x1_stats, n + 1)
                wait(pe, x1_var, n)
                pe.matmul(ps[:, 7, 0:2], group[:], sty[:, odd], start=True, stop=True,
                          skip_group_check=True).then_inc(x1_group, 1)
                wait(pe, xh_in, 32 * (n + 1))
                for g in range(C // 4):
                    wait(pe, dft_copied, n * GROUPS + max(g - 2, 0))
                    for c in range(4):
                        ins = pe.matmul(ps[0:W, 4 + g % 3, H * c:H * c + H], xh[0:H, 4 * g + c], fh[:],
                                        start=(c == 0), stop=(c == 3), skip_group_check=True)
                    ins.then_inc(dft_done, 1)
                for g in range(KP // 4):
                    wait(pe, dft_copied, n * GROUPS + (C // 4 if g == 0 else C // 4 + g - 2))
                    for k in range(4 * g, 4 * g + 4):
                        for r in range(2):
                            ins = pe.matmul(ps[:, 4 + (C // 4 + g) % 3, FR * (k % 4):FR * (k % 4) + FR],
                                            yw[0:W, r, 2 * k:2 * k + 2].rearrange("w k c -> w (k c)"), fw[:, r],
                                            start=(k % 4 == 0 and r == 0), stop=(k % 4 == 3 and r == 1),
                                            skip_group_check=True)
                    ins.then_inc(dft_done, 1)

            overlapped(pe, B, prep, conv, rest)


def mix_frequencies(nc, B, weight, xf, yf):
    with ExitStack() as ctx:
        sb = lambda name, shape, dt=F32: ctx.enter_context(nc.sbuf_tensor("b_" + name, shape, dt))
        sem = lambda name: ctx.enter_context(nc.semaphore("b_" + name))
        ps = ctx.enter_context(nc.psum_tensor("b_ps", [P, 8, BANK], F32))
        wt = sb("wt", [P, 2, C, FP // 2, 2])
        xs = sb("xs", [P, 2, B, FP // 2, 2])
        xj = sb("xj", [P, 2, B, FP // 2, 2])
        ys = sb("ys", [P, 2, B, FP // 2, 2])
        loaded = [sem("loaded0"), sem("loaded1")]
        turned = sem("turned")
        mixed = [sem("mixed_low"), sem("mixed_high")]
        copied = [sem("copied_low"), sem("copied_high")]
        stored = [sem("stored0"), sem("stored1")]
        padded = sem("padded")
        PER = min(BANK // (2 * B), 8)
        GROUPS = -(-KW // PER)

        block = ctx.enter_context(nc.Block())

        @block.sync
        def _(sp):
            def load(k, odd):
                for half in range(2):
                    wait(sp, mixed[half], (k - 1) * GROUPS)
                src = weight.rearrange("c o (k two) w r -> two k c o w r", two=2)
                for half in range(2):
                    sp.dma_start(wt[C * half:C * half + C, odd],
                                 src[half, bass.ds(k, 1)].rearrange("k c o w r -> (k c) o (w r)")
                                 ).then_inc(loaded[odd], 16)
                sp.dma_start(xs[:, odd], xf[bass.ds(k, 1)].rearrange("k p b f -> (k p) (b f)")).then_inc(loaded[odd], 16)

            load(0, 0)
            load(1, 1)
            with sp.Fori(0, KP // 2 - 1) as t:
                for odd in range(2):
                    load(2 * t + (2 + odd), odd)

        @block.gpsimd
        def _(pool):
            pool.memset(ys[:], 0.0).then_inc(padded, 1)

            def turn(k, odd):
                wait(pool, loaded[odd], 24 * (k + (2 - odd)))
                for half in range(2):
                    wait_apart(pool, mixed[half], (k - 1) * GROUPS)
                pool.tensor_scalar(xj[:, odd, :, 0:KW, 0], xs[:, odd, :, 0:KW, 1], -1.0, None, ALU.mult).then_inc(turned, 1)
                pool.tensor_copy(xj[:, odd, :, 0:KW, 1], xs[:, odd, :, 0:KW, 0]).then_inc(turned, 1)

            def store(k, odd):
                for half in range(2):
                    wait(pool, copied[half], (k + 1) * GROUPS)
                pool.dma_start(yf[bass.ds(k, 1)].rearrange("k p b f -> (k p) (b f)"), ys[:, odd]
                               ).then_inc(stored[odd], 16)

            def step(t):
                for odd in range(2):
                    turn(2 * t + (1 + odd), 1 - odd)
                    store(2 * t + odd, odd)

            turn(0, 0)
            pairs(pool, KP, step)
            turn(KP - 1, 1)
            store(KP - 2, 0)
            store(KP - 1, 1)
            for odd in range(2):
                pool.wait_ge(stored[odd], 16 * (KP // 2))

        def take(eng, copy, half):
            def body(k, odd):
                wait(eng, stored[odd], 8 * (k - odd))
                for g in range(GROUPS):
                    lo, hi = g * PER, min(g * PER + PER, KW)
                    wait(eng, mixed[half], k * GROUPS + (g + 1))
                    copy(ys[C * half:C * half + C, odd, :, lo:hi].rearrange("p b w r -> p w b r"),
                         ps[C * half:C * half + C, 4 * half + g % 4, 0:2 * B * (hi - lo)].rearrange(
                             "p (w b r) -> p w b r", b=B, r=2)).then_inc(copied[half], 1)
            eng.wait_ge(padded, 1)
            body(0, 0)
            body(1, 1)
            with eng.Fori(1, KP // 2) as t:
                for odd in range(2):
                    body(2 * t + odd, odd)

        @block.scalar
        def _(act):
            take(act, lambda o, i: act.activation(o, i, ACT.Copy), 0)

        @block.vector
        def _(dve):
            take(dve, lambda o, i: dve.tensor_copy(o, i), 1)

        @block.tensor
        def _(pe):
            def body(k, odd):
                wait(pe, loaded[odd], 24 * (k + (2 - odd)))
                wait(pe, turned, 2 * (k + 1))
                for g in range(GROUPS):
                    lo, hi = g * PER, min(g * PER + PER, KW)
                    for half in range(2):
                        rows = slice(C * half, C * half + C)
                        wait_apart(pe, copied[half], k * GROUPS + (g - 3))
                        for f in range(lo, hi):
                            at = 2 * B * (f - lo)
                            for r, src in ((0, xs), (1, xj)):
                                ins = pe.matmul(ps[rows, 4 * half + g % 4, at:at + 2 * B], wt[rows, odd, :, f, r],
                                                src[rows, odd, :, f], start=(f == lo and r == 0),
                                                stop=(f == hi - 1 and r == 1), skip_group_check=True)
                        ins.then_inc(mixed[half], 1)
            body(0, 0)
            body(1, 1)
            with pe.Fori(1, KP // 2) as t:
                for odd in range(2):
                    body(2 * t + odd, odd)


WS = 8
TOK = WS * WS
A7 = H // (2 * WS)
Q7 = W // (2 * WS)
QTOK = Q7 * 2 * TOK
PW = W // 2 + 4
SUMS = ((4, 3, 0, 1, W // 2 + 1), (0, 4, 1, 0, W // 2), (7, 4, 2, 0, W // 2))
TAPS = sum(x[1] for x in SUMS)
CONV_MMS = TAPS * 4 * 3
EARLY = 4
NCH = 15
EPS = 1e-6


def prepare_weights(nc, args, cst, to):
    with ExitStack() as ctx:
        sb = lambda name, shape, dt=F32: ctx.enter_context(nc.sbuf_tensor("w_" + name, shape, dt))
        sem = lambda name: ctx.enter_context(nc.semaphore("w_" + name))
        ps = ctx.enter_context(nc.psum_tensor("w_ps", [P, 8, BANK], F32))
        conv_w = sb("conv_w", [P, C, 49])
        parts = sb("parts", [C, C, 7, TAPS])
        taps = sb("taps", [P, 25, P])
        stencil = sb("stencil", [P, WS, 25])
        qkw = sb("qkw", [P, C])
        vw = sb("vw", [C, C])
        pw = sb("pw", [C, C])
        qkvb = sb("qkvb", [P, 3 * C])
        pos = sb("pos", [P, C])
        scale = sb("scale", [P, C])
        soft = sb("soft", [P, C])
        inv_sc = sb("inv_sc", [P, C])
        top = sb("top", [P, 1])
        up = sb("up", [P, 1])
        sbias = sb("sbias", [P, 1])
        pb = sb("pb", [P, 1])
        loaded, act_at, dve_at = sem("loaded"), sem("act_at"), sem("dve_at")
        cleared, turned, put, bias_sum = sem("cleared"), sem("turned"), sem("put"), sem("bias_sum")
        soft_done, scaled_up, split = sem("soft_done"), sem("scaled_up"), sem("split")
        LOADS = [
            (to["ident"][:], cst["ident"]), (to["group"][:], cst["group"]), (to["head"][:], cst["head"]),
            (to["inv_h"][:], cst["inv_h"].rearrange("p (r h) -> p r h", r=2)), (to["inv_w"][:], cst["inv_w"]),
            (taps[:], cst["taps"].rearrange("p (t q) -> p t q", t=25)),
            (conv_w[0:C], args["L2_conv_weight"].rearrange("o c h w -> o c (h w)")),
            (conv_w[C:P], args["L2_conv_weight"].rearrange("o c h w -> o c (h w)")),
            (to["cbias"][0:C], args["L2_conv_bias"]), (to["cbias"][C:P], args["L2_conv_bias"]),
            (stencil[:].rearrange("p d t -> p (d t)"),
             args["L3_conv_dwc_w"].rearrange("d i h w -> (d i h w)").partition_broadcast(P)),
            (qkw[:], args["L3_conv_qkv_w"][0:P]), (vw[:], args["L3_conv_qkv_w"][P:3 * C]),
            (pw[:], args["L3_conv_proj_w"]),
            (qkvb[:], args["L3_conv_qkv_b"].partition_broadcast(P)),
            (pos[0:C], args["L3_conv_pos_enc"].rearrange("i t c -> (i t) c")),
            (pos[C:P], args["L3_conv_pos_enc"].rearrange("i t c -> (i t) c")),
            (scale[:], args["L3_conv_scale"].rearrange("i j c -> (i j c)").partition_broadcast(P)),
            (pb[0:C], args["L3_conv_proj_b"]), (pb[C:P], args["L3_conv_proj_b"]),
        ] + [(sbias[WS * h:WS * h + WS], args["L3_conv_dwc_b"]) for h in range(P // WS)]
        block = ctx.enter_context(nc.Block())

        @block.sync
        def _(sp):
            for dst, src in LOADS:
                if len(src.shape) == 1:
                    src = src.rearrange("(c i) -> c i", i=1)
                sp.dma_start(dst, src).then_inc(loaded, 16)

        @block.gpsimd
        def _(pool):
            pool.memset(to["wst"][:], 0.0)
            pool.memset(to["wproj"][:], 0.0)
            pool.memset(to["wqkv"][:], 0.0).then_inc(cleared, 1)

        @block.scalar
        def _(act):
            link = Chain(act, act_at, 0, 0)
            act.wait_ge(loaded, 16 * len(LOADS))
            link(act.activation(soft[:], scale[:], ACT.Abs))
            link(act.activation(soft[:], soft[:], ACT.Exp, scale=-1.0))
            act.activation(soft[:], soft[:], ACT.Ln, bias=1.0).then_inc(soft_done, 1)

        @block.tensor
        def _(pe):
            pe.wait_ge(loaded, 16 * len(LOADS))
            pe.transpose(ps[0:C, 7, 0:P], qkw[:], to["ident"][:])
            pe.transpose(ps[0:C, 7, P:P + C], vw[:], to["ident"][0:C, 0:C])
            pe.transpose(ps[0:C, 7, P + C:2 * P], pw[:], to["ident"][0:C, 0:C]).then_inc(turned, 1)
            pe.wait_ge(scaled_up, 1)
            for ky in range(7):
                if ky >= 3:
                    pe.wait_ge(split, ky - 2)
                for t in range(TAPS):
                    ins = pe.transpose(ps[0:C, 2 * (ky % 3) + t // 8, C * (t % 8):C * (t % 8) + C],
                                       parts[:, :, ky, t], to["ident"][0:C, 0:C])
                ins.then_inc(turned, 1)
            pe.wait_ge(put, 1)
            pe.matmul(ps[:, 7, 0:1], to["wproj"][:].rearrange("p r c -> p (r c)"), sbias[:],
                      start=True, stop=True).then_inc(bias_sum, 1)

        @block.vector
        def _(dve):
            link = Chain(dve, dve_at, 0, 0)
            dve.wait_ge(loaded, 16 * len(LOADS))
            link(dve.tensor_reduce(top[:], conv_w[:].rearrange("p c t -> p (c t)"), AX.X, ALU.max,
                                   apply_absolute_value=True))
            link(dve.tensor_scalar(top[:], top[:], 1e-30, None, ALU.max))
            link(dve.reciprocal(up[:], top[:]))
            dve.tensor_scalar(to["unscale"][:], top[:], 1.0 / 256, None, ALU.mult)
            link(dve.tensor_scalar(conv_w[:], conv_w[:], up[:], 256.0, ALU.mult, ALU.mult))
            h = conv_w[0:C].rearrange("o c (y x) -> o c y x", y=7)
            for y in range(7):
                dve.tensor_copy(parts[:, :, y, 0:4], h[:, :, y, 0:7:2])
                dve.tensor_copy(parts[:, :, y, 4:7], h[:, :, y, 1:7:2])
                dve.tensor_copy(parts[:, :, y, 7:8], h[:, :, y, 0:1])
                ins = dve.tensor_tensor(parts[:, :, y, 8:11], h[:, :, y, 2:7:2], h[:, :, y, 1:7:2], ALU.add)
            ins.then_inc(scaled_up, 1)
            dve.wait_ge(soft_done, 1)
            link(dve.scalar_tensor_tensor(soft[:], scale[:], 0.0, soft[:], ALU.max, ALU.add))
            link(dve.reciprocal(inv_sc[:], soft[:]))
            link(dve.tensor_tensor(qkvb[:, C:2 * C], qkvb[:, C:2 * C], pos[:], ALU.add))
            for r in range(2):
                for k in range(2):
                    dve.tensor_tensor(to["bqk"][:, k, r], qkvb[:, C * k:C * k + C], inv_sc[:], ALU.mult)
                dve.tensor_copy(to["bv"][:, C * r:C * r + C], qkvb[:, 2 * C:3 * C])
            dve.tensor_scalar(to["epsc"][:], inv_sc[:], EPS, None, ALU.mult)
            dve.wait_ge(turned, 1)
            dve.wait_ge(cleared, 1)
            for r in range(2):
                rows = slice(C * r, C * r + C)
                for k in range(2):
                    dve.tensor_tensor(to["wqkv"][rows, k, r], ps[0:C, 7, C * k:C * k + C], inv_sc[0:C], ALU.mult)
                dve.tensor_copy(to["wqkv"][rows, 2, r], ps[0:C, 7, P:P + C])
                ins = dve.tensor_copy(to["wproj"][rows, r], ps[0:C, 7, P + C:2 * P])
            ins.then_inc(put, 1)
            for ky in range(7):
                dve.wait_ge(turned, ky + 2)
                got = ps[0:C, 2 * (ky % 3):2 * (ky % 3) + 2].rearrange("c b x -> c (b x)")[:, 0:TAPS * C].rearrange(
                    "c (k o) -> c k o", k=TAPS)
                for q in range(2):
                    pr, rp = divmod(ky + q, 2)
                    high = to["wst"][C * rp:C * rp + C, 0, pr, :, q]
                    link(dve.tensor_copy(high, got))
                    ins = dve.tensor_tensor(to["wst"][C * rp:C * rp + C, 1, pr, :, q], got, high, ALU.subtract)
                ins.then_inc(split, 1)
            for t in range(25):
                for d in range(WS):
                    if t == 0:
                        ins = dve.tensor_scalar(to["spread"][:, d], taps[:, t], stencil[:, d, t:t + 1], None, ALU.mult)
                    else:
                        ins = dve.scalar_tensor_tensor(to["spread"][:, d], taps[:, t], stencil[:, d, t:t + 1],
                                                       to["spread"][:, d], ALU.mult, ALU.add)
                link(ins)
            dve.wait_ge(bias_sum, 1)
            dve.tensor_tensor(to["pbias"][:], ps[:, 7, 0:1], pb[:], ALU.add)


QBANK = (2, 3, 4, 7, 5, 6, 2)
QGROUPS = ((0, 3, 2), (3, 1, 7), (4, 2, 5), (6, 1, 2))
PIECES = (16, 126, 132, 154, 236)


def image_steps(eng, images, bring, both, last):
    def step(t):
        for odd in range(2):
            bring(2 * t + (1 + odd), 1 - odd)
            both(2 * t + (1 + odd), 1 - odd, True)

    bring(0, 0)
    both(0, 0, False)
    pairs(eng, images, step)
    bring(images - 1, 1)
    both(images - 1, 1, True)
    last(images, 0)


def large_conv_and_attention(nc, B, args, cst, x1, yf, out):
    with ExitStack() as keep:
        sb = lambda name, shape, dt=F32: keep.enter_context(nc.sbuf_tensor("c_" + name, shape, dt))
        ident = sb("ident", [P, P])
        group = sb("group", [P, P])
        head = sb("head", [P, P])
        inv_h = sb("inv_h", [P, 2, H])
        inv_w = sb("inv_w", [P, W])
        wst = sb("wst", [P, 2, 4, TAPS, 2, C], F16)
        unscale = sb("unscale", [P, 1])
        cbias = sb("cbias", [P, 1])
        wqkv = sb("wqkv", [P, 3, 2, C])
        wproj = sb("wproj", [P, 2, C])
        bqk = sb("bqk", [P, 2, 2, C])
        bv = sb("bv", [P, 2 * C])
        epsc = sb("epsc", [P, C])
        spread = sb("spread", [P, WS, P])
        pbias = sb("pbias", [P, 1])
        prepare_weights(nc, args, cst, dict(
            ident=ident, group=group, head=head, inv_h=inv_h, inv_w=inv_w, wst=wst, unscale=unscale,
            cbias=cbias, wqkv=wqkv, wproj=wproj, bqk=bqk, bv=bv, epsc=epsc, spread=spread, pbias=pbias))

        sem = lambda name: keep.enter_context(nc.semaphore("c_" + name))
        ps = keep.enter_context(nc.psum_tensor("c_ps", [P, 8, BANK], F32))
        xr = sb("xr", [P, 2, J, W])
        ys = sb("ys", [P, C, FP])
        xp_all = sb("xp", [P, 2 * 3 * (J + 3) * PW], F16)
        xp = xp_all[:].rearrange("p (s k j w) -> p s k j w", s=2, k=3, j=J + 3)
        z = xp_all[:, 0:2 * H * C].bitcast(F32).rearrange("p (h c) -> p h c", h=H)
        tn = sb("tn", [P, 2, 3, ROWS, PW])
        cv = sb("cv", [P, 2, ROWS, W])
        part = sb("part", [P, ROWS, W // 2 + 1])
        bn2 = sb("bn2", [P, CHUNKS, 6])
        bn3 = sb("bn3", [P, CHUNKS, 6])
        mv = sb("mv", [P, 2])
        st = sb("st", [P, 2])
        gst = sb("gst", [P, 4])
        nrm = sb("nrm", [P, 2, 2])
        xn = sb("xn", [P, 2 * Q7, TOK])
        qk = sb("qk", [P, Q7, 2, 2, C])
        v = sb("v", [P, Q7, 2 * C + 2])
        sq = sb("sq", [P, Q7, 2, 2, C])
        cube = sb("cube", [P, Q7, 2, 2, C])
        s2 = sb("s2", [P, 4 * Q7])
        s6 = sb("s6", [P, 4 * Q7])
        fac = sb("fac", [P, 4 * Q7])
        kvm = sb("kvm", [P, 2, Q7, P])
        km = sb("km", [P, Q7, 2])
        qt = qk[:].rearrange("p q k r c -> p (q k r c)")[:, 0:QTOK]
        qs = sq[:].rearrange("p q k r c -> p (q k r c)")[:, 0:QTOK]
        den = sq[:].rearrange("p q k r c -> p (q k r c)")[:, QTOK:2 * QTOK]
        att = sb("att", [P, 2 * Q7, TOK])
        dw = att[:].rearrange("p w t -> p (w t)").rearrange("p (q r h d) -> p q r h d", q=Q7, r=2, d=WS)
        o2 = kvm[:].rearrange("p w q x -> p (w q x)")[:, 0:8 * W].rearrange("p (j x) -> p j x", j=8)

        x1_in = [sem("x1_in0"), sem("x1_in1")]
        names = """ys_in zeros c1_done c1_taken c2_done padded x2_done bn_at stats_done grouped var_done std_done
            rstd_done normed hi_done lo_done ab_done ab_taken g_done g_taken conv_scaled part_done x3_done xn_done qkv_done qk_taken u_done u2_done
            s2_done u3_done u6_done s6_done ratio_at ratio_done f_done scaled dwc_done dw_taken qt_done qt_taken
            kv_done kvm_done km_done qs_done num_done den_done den_taken ones x2_stats dwt_done inv_done mul_done att_done
            proj_done o2_done xo_done out_done bn3_done""".split()
        s = type("Semaphores", (), {n: sem(n) for n in names})
        block = keep.enter_context(nc.Block())
        spans = [(1 + ROWS * k, min(1 + ROWS * (k + 1), J + 2)) for k in range(NCH)]

        @block.sync
        def _(sp):
            def load_ys(n):
                wait(sp, s.c1_done, 16 * n)
                src = yf[:, :, bass.ds(n, 1)].rearrange("k (kp o) b f -> (k kp) o (b f)", kp=2)
                sp.dma_start(ys[0:KH], src).then_inc(s.ys_in, 16)
                sp.dma_start(ys[64:64 + KH, :, 0:FP - 1], src[:, :, 1:FP]).then_inc(s.ys_in, 16)

            def load_x1(n, odd):
                sp.dma_start(xr[:, odd], x1[bass.ds(n, 1)].rearrange("b hp c j w -> (b hp c) j w")
                             ).then_inc(x1_in[odd], 16)

            def store(n, odd):
                for a in range(A7):
                    wait(sp, s.xo_done, n * A7 + (a + 1))
                    for hp in range(2):
                        dst = out[bass.ds(n, 1), :, 16 * a:16 * a + 16].rearrange(
                            "b c (j hp) w -> hp (b c) j w", hp=2)[hp]
                        sp.dma_start(dst, xr[C * hp:C * hp + C, odd, 8 * a:8 * a + 8]).then_inc(s.out_done, 16)

            sp.wait_ge(s.zeros, 1)
            load_ys(0)
            load_x1(0, 0)
            load_ys(1)
            load_x1(1, 1)

            def step(t):
                for odd in range(2):
                    load_ys(2 * t + (2 + odd))
                    store(2 * t + odd, odd)
                    wait(sp, s.out_done, (2 * t + (1 + odd)) * (A7 * 32))
                    load_x1(2 * t + (2 + odd), odd)

            pairs(sp, B, step)
            store(B - 2, 0)
            store(B - 1, 1)
            sp.wait_ge(s.out_done, B * A7 * 32)

        @block.tensor
        def _(pe):
            at = [0]
            pe.wait_ge(s.ones, 1)

            def conv_some(n, upto):
                while at[0] < upto:
                    c, i = divmod(at[0], CONV_MMS)
                    which = 0 if i < 36 else 1 if i < 84 else 2
                    first, taps, kind, shift, width = SUMS[which]
                    i -= (0, 36, 84)[which]
                    t, part = divmod(i, 3)
                    pr, k = divmod(t, taps)
                    if i == 0 and which == 0:
                        wait(pe, s.lo_done, n * NCH + min(c + 2, NCH))
                        wait(pe, s.ab_taken, n * CHUNKS + c)
                    if i == 0 and which == 2:
                        wait(pe, s.g_taken, n * CHUNKS + c)
                    ws, xs = ((0, 0), (0, 1), (1, 0))[part]
                    col = ROWS * (W // 2) if which == 0 else 0
                    ins = pe.matmul(ps[:, which // 2, col:col + ROWS * width],
                                    wst[:, ws, pr, first + k].rearrange("p q o -> p (q o)"),
                                    xp[:, xs, kind, ROWS * c + pr:ROWS * c + pr + ROWS, shift + k:shift + k + width],
                                    start=(i == 0), stop=(i == 12 * taps - 1), skip_group_check=True)
                    if i == 12 * taps - 1 and which:
                        ins.then_inc(s.ab_done if which == 1 else s.g_done, 1)
                    at[0] += 1

            def stats(count):
                wait(pe, s.stats_done, count + 1)
                wait(pe, s.rstd_done, count)
                pe.matmul(ps[:, 7, 0:2], group[:], st[:], start=True, stop=True).then_inc(s.grouped, 1)

            def bring(n, odd):
                wait(pe, s.ys_in, 32 * (n + 1))
                wait(pe, s.o2_done, (n - 1) * A7)
                for g in range(16):
                    if g >= 5:
                        wait_apart(pe, s.c1_taken, n * 16 + (g - 4))
                    for o in range(4 * g, 4 * g + 4):
                        for r in range(2):
                            ins = pe.matmul(ps[64 * r:64 * r + 64, 2 + g % 5, H * (o % 4):H * (o % 4) + H],
                                            ys[0:120, o, 0:FP:2], inv_h[0:120, r],
                                            start=(o % 4 == 0), stop=(o % 4 == 3), skip_group_check=True)
                    ins.then_inc(s.c1_done, 1)
                if not isinstance(n, int) or n:
                    stats(2 * n - 1)
                wait(pe, s.c1_taken, n * 16 + 16)
                for g in range(CHUNKS):
                    wait(pe, s.x2_done, n * CHUNKS + max(g - 4, 0))
                    for j in range(4 * g, 4 * g + 4):
                        ins = pe.matmul(ps[:, 2 + g % 5, W * (j % 4):W * (j % 4) + W],
                                        z[:, 2 * j:2 * j + 2].rearrange("p h c -> p (h c)"), inv_w[:],
                                        start=(j % 4 == 0), stop=(j % 4 == 3), skip_group_check=True)
                    ins.then_inc(s.c2_done, 1)
                stats(2 * n)

            def attend(l, a, conv):
                wait(pe, s.xn_done, l + 1)
                for q in range(Q7):
                    if q == 4:
                        wait(pe, s.o2_done, l)
                    if q == 6:
                        wait(pe, s.qk_taken, 4 * l + 1)
                    ins = pe.matmul(ps[:, QBANK[q], 0:6 * C], xn[:, 2 * q:2 * q + 2].rearrange("p w t -> p (w t)"),
                                    wqkv[:].rearrange("p k r c -> p (k r c)"), start=True, stop=True)
                    if q in (2, 3, 5, 6):
                        ins.then_inc(s.qkv_done, 1)
                conv(PIECES[0])
                wait(pe, s.qk_taken, 4 * l + 4)
                for d in range(WS):
                    ins = pe.matmul(ps[:, 3 + d // 4, 112 * (d % 4):112 * (d % 4) + 112], spread[:, d],
                                    v[:, :, 0:2 * C].rearrange("p q (r h d) -> p q r h d", r=2, d=WS)[:, :, :, :, d],
                                    start=(d % 4 == 0), stop=(d % 4 == 3), skip_group_check=True)
                ins.then_inc(s.dwc_done, 1)
                conv(PIECES[1])
                wait(pe, s.scaled, l + 1)
                for q in range(Q7):
                    ins = pe.transpose(ps[:, 5 + q // 4, P * (q % 4):P * (q % 4) + P], cube[:, q, 0].rearrange("p r c -> p (r c)"), ident[:])
                ins.then_inc(s.qt_done, 1)
                conv(PIECES[2])
                for w in range(2):
                    if w == 0:
                        wait_apart(pe, s.dw_taken, l + 1)
                    else:
                        wait_apart(pe, s.qt_taken, l + 1)
                    rows = slice(TOK * w, TOK * w + TOK)
                    for q in range(Q7):
                        ins = pe.matmul(ps[:, 2 + 3 * w + q // 3, 129 * (q % 3):129 * (q % 3) + 129],
                                        cube[rows, q, 1].rearrange("p r c -> p (r c)"), v[rows, q, 0:129],
                                        start=(q % 3 == 0), stop=(q % 3 == 2 or q == 6), skip_group_check=True)
                    ins.then_inc(s.kv_done, 1)
                conv(PIECES[3])
                wait(pe, s.kvm_done, 6 * l + 6)
                wait(pe, s.km_done, 2 * l + 2)
                for q in range(Q7):
                    for w in range(2):
                        col = (2 * q + w) * TOK
                        ins = pe.matmul(ps[:, 2 + col // BANK, col % BANK:col % BANK + TOK], kvm[:, w, q],
                                        qt[:, col:col + TOK], start=(col % BANK == 0),
                                        stop=(col % BANK == BANK - TOK or col == QTOK - TOK), skip_group_check=True)
                ins.then_inc(s.num_done, 1)
                wait(pe, s.qs_done, l + 1)
                for lo, hi in ((0, BANK), (BANK, QTOK)):
                    ins = pe.matmul(ps[:, 5 + lo // BANK, 0:hi - lo], head[:], qs[:, lo:hi], start=True, stop=True)
                ins.then_inc(s.den_done, 1)
                for q in range(Q7):
                    ins = pe.transpose(ps[:, 4 + 3 * (q // 4), P * (q % 4):P * (q % 4) + P],
                                       dw[:, q].rearrange("p r h d -> p (r h d)"), ident[:])
                ins.then_inc(s.dwt_done, 1)
                conv(PIECES[4])
                wait(pe, s.att_done, l + 1)
                for y in range(2):
                    ins = pe.matmul(ps[:, 5 + y, 0:N4], wproj[:].rearrange("p r c -> p (r c)"),
                                    att[:].rearrange("p w (y x) -> p y w x", y=WS)[:, 4 * y:4 * y + 4],
                                    start=True, stop=True)
                ins.then_inc(s.proj_done, 1)
                conv(2 * CONV_MMS)

            def both(n, odd, attention):
                at[0] = 0
                if attention:
                    wait(pe, s.x2_done, (n + 1) * CHUNKS)
                    wait_apart(pe, s.rstd_done, 2 * n + 1)
                    for a in range(A7):
                        attend((n - 1) * A7 + a, a, lambda k: conv_some(n, 2 * CONV_MMS * a + k))
                else:
                    conv_some(n, CHUNKS * CONV_MMS)

            def last(n, odd):
                stats(2 * n - 1)
                wait(pe, s.rstd_done, 2 * n)
                for a in range(A7):
                    attend((n - 1) * A7 + a, a, lambda k: None)

            image_steps(pe, B, bring, both, last)

        @block.scalar
        def _(act):
            def deviation(count):
                wait(act, s.var_done, count + 1)
                act.activation(gst[:, 3:4], gst[:, 3:4], ACT.Sqrt).then_inc(s.std_done, 1)

            def bring(n, odd):
                wait(act, s.g_done, n * CHUNKS)
                for g in range(16):
                    wait(act, s.c1_done, n * 16 + (g + 1))
                    act.activation(z[:, :, 4 * g:4 * g + 4].rearrange("p h o -> p o h"),
                                   ps[:, 2 + g % 5, 0:4 * H].rearrange("p (o h) -> p o h", o=4), ACT.Copy
                                   ).then_inc(s.c1_taken, 1)
                if not isinstance(n, int) or n:
                    deviation(2 * n - 1)
                    wait(act, s.rstd_done, 2 * n)
                    window_rows((n - 1) * A7, 0, 1 - odd)
                deviation(2 * n)
                wait(act, s.rstd_done, 2 * n + 1)
                for k in range(EARLY):
                    padded_chunk(n, odd, k)

            def padded_chunk(n, odd, k):
                if k >= NCH:
                    return
                lo, hi = spans[k]
                wait(act, s.lo_done, n * NCH + (k - 1))
                put = tn[:, k % 2, 0:2, :, 2:2 + W // 2].rearrange("p k j i -> p j i k")
                get = xr[:, odd].rearrange("p j (i k) -> p j i k", k=2)
                if k == 0:
                    act.activation(put[0:C, 0:1], get[C:P, 0:1], ACT.Copy, scale=0.0)
                a = max(lo, 2)
                act.activation(put[0:C, a - lo:hi - lo], get[C:P, a - 2:hi - 2], ACT.Identity,
                               scale=nrm[C:P, 0, 0:1], bias=nrm[C:P, 0, 1:2])
                if k < NCH - 1:
                    ins = act.activation(put[C:P, 0:hi - lo], get[0:C, lo - 1:hi - 1], ACT.Identity,
                                         scale=nrm[0:C, 0, 0:1], bias=nrm[0:C, 0, 1:2])
                else:
                    ins = act.activation(put[C:P, 0:1], get[0:C, 0:1], ACT.Copy, scale=0.0)
                ins.then_inc(s.normed, 1)

            def window_rows(l, a, odd):
                wait(act, s.qkv_done, 4 * l)
                for wr in range(2):
                    for hp in range(2):
                        ins = act.activation(
                            xn[C * wr:C * wr + C].rearrange("p w (j hp x) -> p hp j w x", hp=2, x=WS)[:, hp],
                            xr[C * hp:C * hp + C, odd, 8 * a + 4 * wr:8 * a + 4 * wr + 4].rearrange(
                                "p j (w x) -> p j w x", x=WS),
                            ACT.Identity, scale=nrm[C * hp:C * hp + C, 1, 0:1], bias=nrm[C * hp:C * hp + C, 1, 1:2])
                ins.then_inc(s.xn_done, 1)

            def scale_conv(n, c):
                wait(act, s.g_taken, n * CHUNKS + (c + 1))
                act.activation(cv[:, c % 2], cv[:, c % 2], ACT.Identity, scale=unscale[:], bias=cbias[:]
                               ).then_inc(s.conv_scaled, 1)

            def attend(l, a, odd, conv, pad):
                conv(-1)
                pad()
                wait(act, s.u_done, l + 1)
                wait(act, s.s6_done, l)
                act.activation(sq[:], qk[:], ACT.Square).then_inc(s.u2_done, 1)
                wait(act, s.dwc_done, l + 1)
                wait(act, s.dwt_done, l)
                for b in range(2):
                    ins = act.activation(
                        dw[:].rearrange("p q r h d -> p d (q r h)")[:, 4 * b:4 * b + 4],
                        ps[:, 3 + b, 0:448].rearrange("p (d x) -> p d x", d=4), ACT.Copy)
                ins.then_inc(s.dw_taken, 1)
                if a < A7 - 1:
                    window_rows(l + 1, a + 1, odd)
                wait(act, s.u3_done, l + 1)
                wait(act, s.s2_done, l + 1)
                act.activation(sq[:], cube[:], ACT.Square).then_inc(s.u6_done, 1)
                wait(act, s.ratio_done, l + 1)
                act.activation(fac[:], fac[:], ACT.Sqrt).then_inc(s.f_done, 1)
                wait(act, s.qt_done, l + 1)
                act.activation(qt, ps[:, 5:7].rearrange("p b x -> p (b x)")[:, 0:QTOK], ACT.Copy
                               ).then_inc(s.qt_taken, 1)
                conv(0)
                wait(act, s.den_done, l + 1)
                act.activation(den, ps[:, 5:7].rearrange("p b x -> p (b x)")[:, 0:QTOK], ACT.Copy, bias=EPS
                               ).then_inc(s.den_taken, 1)
                wait(act, s.proj_done, l + 1)
                wait(act, s.xo_done, l)
                for wr in range(2):
                    for hp in range(2):
                        ins = act.activation(
                            o2[C * hp:C * hp + C, 4 * wr:4 * wr + 4].rearrange("p (b j) x -> p b j x", b=2),
                            ps[C * wr:C * wr + C, 5:7, 0:N4].rearrange("p b (j hp x) -> p hp b j x", hp=2, x=W)[:, hp],
                            ACT.Identity, bias=pbias[C * wr:C * wr + C])
                ins.then_inc(s.o2_done, 1)

            def both(n, odd, attention):
                if attention:
                    for a in range(A7):
                        attend((n - 1) * A7 + a, a, 1 - odd,
                               lambda k: scale_conv(n, 2 * a + k) if a or k == 0 else None,
                               lambda: [padded_chunk(n, odd, EARLY + 2 * a + k) for k in range(2)])
                    scale_conv(n, CHUNKS - 1)
                else:
                    for k in range(EARLY, NCH):
                        padded_chunk(n, odd, k)
                    for c in range(CHUNKS):
                        scale_conv(n, c)

            def last(n, odd):
                deviation(2 * n - 1)
                wait(act, s.rstd_done, 2 * n)
                window_rows((n - 1) * A7, 0, 1 - odd)
                for a in range(A7):
                    attend((n - 1) * A7 + a, a, 1 - odd, lambda k: None, lambda: None)

            image_steps(act, B, bring, both, last)

        @block.vector
        def _(dve):
            dve.wait_ge(s.ones, 1)

            def norm(which, count, bn):
                link = Chain(dve, s.bn_at, 4, count)
                wait_apart(dve, s.grouped, count)
                link(dve.bn_aggr(mv[:], bn[:]))
                dve.tensor_copy(st[:, 0:1], mv[:, 0:1])
                dve.scalar_tensor_tensor(st[:, 1:2], mv[:, 0:1], mv[:, 0:1], mv[:, 1:2], ALU.mult, ALU.add
                                         ).then_inc(s.stats_done, 1)
                wait(dve, s.grouped, count + 1)
                link(dve.tensor_copy(gst[:, 0:2], ps[:, 7, 0:2]))
                link(dve.scalar_tensor_tensor(gst[:, 2:3], gst[:, 0:1], gst[:, 0:1], gst[:, 1:2],
                                              ALU.mult, ALU.subtract))
                dve.tensor_scalar(gst[:, 3:4], gst[:, 2:3], -1.0, GN_EPS, ALU.mult, ALU.add).then_inc(s.var_done, 1)
                wait(dve, s.std_done, count + 1)
                link(dve.reciprocal(nrm[:, which, 0:1], gst[:, 3:4]))
                dve.scalar_tensor_tensor(nrm[:, which, 1:2], gst[:, 0:1], -1.0, nrm[:, which, 0:1],
                                         ALU.mult, ALU.mult).then_inc(s.rstd_done, 1)

            def bring(n, odd):
                if not isinstance(n, int) or n:
                    wait(dve, s.xn_done, (n - 1) * A7)
                    wait(dve, s.bn3_done, n * CHUNKS)
                    norm(1, 2 * n - 1, bn3)
                wait(dve, x1_in[odd], 8 * (n + (2 - odd)))
                for c in range(CHUNKS):
                    wait(dve, s.c2_done, n * CHUNKS + (c + 1))
                    here = xr[:, odd, ROWS * c:ROWS * c + ROWS].rearrange("p a w -> p (a w)")
                    dve.tensor_tensor(here, ps[:, 2 + c % 5, 0:N4], here, ALU.add).then_inc(s.x2_done, 1)
                    if c:
                        x2_stats(n, odd, c - 1)
                x2_stats(n, odd, CHUNKS - 1)
                wait(dve, s.x2_stats, (n + 1) * CHUNKS)
                norm(0, 2 * n, bn2)
                for k in range(EARLY):
                    low_part(n, k)

            def x2_stats(n, odd, c):
                wait(dve, s.x2_done, n * CHUNKS + (c + 1))
                dve.bn_stats(bn2[:, c], xr[:, odd, ROWS * c:ROWS * c + ROWS].rearrange("p a w -> p (a w)")
                             ).then_inc(s.x2_stats, 1)

            def low_part(n, k):
                if k >= NCH:
                    return
                lo, hi = spans[k]
                wait(dve, s.hi_done, n * NCH + (k + 1))
                for kind in range(3):
                    ins = dve.tensor_tensor(xp[:, 1, kind, lo:hi].rearrange("p j w -> p (j w)"),
                                            tn[:, k % 2, kind, 0:hi - lo].rearrange("p j w -> p (j w)"),
                                            xp[:, 0, kind, lo:hi].rearrange("p j w -> p (j w)"), ALU.subtract)
                ins.then_inc(s.lo_done, 1)

            def take_ab(n, c):
                wait(dve, s.ab_done, n * CHUNKS + (c + 1))
                wait(dve, s.x3_done, n * CHUNKS + (c - 1))
                second = ps[:, 0, 0:ROWS * (W // 2)].rearrange("p (j i) -> p j i", j=ROWS)
                first = ps[:, 0, ROWS * (W // 2):ROWS * (W + 1)].rearrange("p (j i) -> p j i", j=ROWS)
                dve.tensor_copy(part[:], first).then_inc(s.part_done, 1)
                wait(dve, s.part_done, n * CHUNKS + (c + 1))
                dve.tensor_tensor(cv[:, c % 2, :, 0:W:2], second, part[:, :, 0:W // 2], ALU.add)
                dve.tensor_tensor(cv[:, c % 2, :, 1:W:2], second, part[:, :, 1:W // 2 + 1], ALU.add
                                  ).then_inc(s.ab_taken, 1)

            def take_g(n, c):
                wait(dve, s.g_done, n * CHUNKS + (c + 1))
                wait(dve, s.ab_taken, n * CHUNKS + (c + 1))
                dve.tensor_tensor(cv[:, c % 2, :, 1:W:2], ps[:, 1, 0:ROWS * (W // 2)].rearrange("p (j i) -> p j i", j=ROWS),
                                  cv[:, c % 2, :, 1:W:2], ALU.subtract).then_inc(s.g_taken, 1)

            def x3_stats(n, odd, c):
                wait(dve, s.x3_done, n * CHUNKS + (c + 1))
                dve.bn_stats(bn3[:, c], xr[:, odd, ROWS * c:ROWS * c + ROWS].rearrange("p a w -> p (a w)")
                             ).then_inc(s.bn3_done, 1)

            def attend(l, a, conv, pad):
                conv("g", -1)
                for g, (q, n, b) in enumerate(QGROUPS):
                    wait(dve, s.qkv_done, 4 * l + (g + 1))
                    dve.tensor_tensor(qk[:, q:q + n].rearrange("p q k r c -> p q (k r c)"), ps[:, b:b + n, 0:4 * C],
                                      bqk[:].rearrange("p k r c -> p (k r c)").unsqueeze(1).to_broadcast(
                                          [P, n, 4 * C]), ALU.add)
                    dve.tensor_tensor(v[:, q:q + n, 0:2 * C], ps[:, b:b + n, 4 * C:6 * C],
                                      bv[:].unsqueeze(1).to_broadcast([P, n, 2 * C]), ALU.add
                                      ).then_inc(s.qk_taken, 1)
                wait(dve, s.qk_taken, 4 * l + 4)
                flat = qk[:].rearrange("p q k r c -> p (q k r) c")
                dve.scalar_tensor_tensor(flat, flat, 0.0, epsc[:].unsqueeze(1).to_broadcast([P, 4 * Q7, C]),
                                         ALU.max, ALU.add).then_inc(s.u_done, 1)
                pad()
                conv("x", -1)
                wait(dve, s.u2_done, l + 1)
                dve.tensor_reduce(s2[:], sq[:].rearrange("p q k r c -> p (q k r) c"), AX.X, ALU.add
                                  ).then_inc(s.s2_done, 1)
                conv("ab", 0)
                wait(dve, s.u6_done, l + 1)
                dve.tensor_reduce(s6[:], sq[:].rearrange("p q k r c -> p (q k r) c"), AX.X, ALU.add
                                  ).then_inc(s.s6_done, 1)
                wait(dve, s.s6_done, l + 1)
                dve.reciprocal(s6[:], s6[:]).then_inc(s.ratio_at, 1)
                wait(dve, s.ratio_at, l + 1)
                dve.tensor_tensor(fac[:], s2[:], s6[:], ALU.mult).then_inc(s.ratio_done, 1)
                wait(dve, s.f_done, l + 1)
                cubes = cube[:].rearrange("p q k r c -> p (q k r) c")
                dve.tensor_tensor(cubes, cubes, fac[:].unsqueeze(2).to_broadcast([P, 4 * Q7, C]), ALU.mult
                                  ).then_inc(s.scaled, 1)
                conv("g", 0)
                wait(dve, s.xo_done, l)
                for w in range(2):
                    wait(dve, s.kv_done, 2 * l + (w + 1))
                    dve.tensor_copy(km[:, 0:6, w].rearrange("p (b q) -> p b q", b=2),
                                    ps[:, 2 + 3 * w:4 + 3 * w, 128:387:129])
                    dve.tensor_copy(km[:, 6:7, w], ps[:, 4 + 3 * w, 128:129]).then_inc(s.km_done, 1)
                    for b in range(3):
                        n = min(3, Q7 - 3 * b)
                        dve.tensor_tensor(kvm[:, w, 3 * b:3 * b + n],
                                          ps[:, 2 + 3 * w + b, 0:129 * n].rearrange("p (q x) -> p q x", q=n)[:, :, 0:P],
                                          head[:].unsqueeze(1).to_broadcast([P, n, P]), ALU.mult
                                          ).then_inc(s.kvm_done, 1)
                wait(dve, s.den_taken, l + 1)
                dve.reciprocal(den, den).then_inc(s.inv_done, 1)
                wait(dve, s.num_done, l + 1)
                wait(dve, s.inv_done, l + 1)
                wait(dve, s.dwt_done, l + 1)
                flat = att[:].rearrange("p w t -> p (w t)")
                dve.tensor_tensor(flat, ps[:, 2:4].rearrange("p b x -> p (b x)")[:, 0:QTOK], den, ALU.mult
                                  ).then_inc(s.mul_done, 1)
                wait(dve, s.mul_done, l + 1)
                dve.tensor_tensor(flat[:, 0:BANK], ps[:, 4], flat[:, 0:BANK], ALU.add)
                dve.tensor_tensor(flat[:, BANK:QTOK], ps[:, 7, 0:QTOK - BANK], flat[:, BANK:QTOK], ALU.add
                                  ).then_inc(s.att_done, 1)
                conv("ab", 1)
                conv("x", 0)

            def both(n, odd, attention):
                def conv(what, c):
                    if c >= 0:
                        {"ab": take_ab, "g": take_g}[what](n, c) if what != "x" else x3_stats(n, odd, c)

                if attention:
                    for a in range(A7):
                        attend((n - 1) * A7 + a, a, lambda what, k: conv(what, 2 * a + k),
                               lambda: [low_part(n, EARLY + 2 * a + k) for k in range(2)])
                else:
                    for k in range(EARLY, NCH):
                        low_part(n, k)
                    for c in range(CHUNKS - 1):
                        conv("ab", c)
                        conv("g", c)
                        conv("x", c - 1)
                    conv("ab", CHUNKS - 1)
                    conv("x", CHUNKS - 2)
                conv("g", CHUNKS - 1)
                conv("x", CHUNKS - 1)

            def last(n, odd):
                wait(dve, s.bn3_done, n * CHUNKS)
                norm(1, 2 * n - 1, bn3)
                for a in range(A7):
                    attend((n - 1) * A7 + a, a, lambda what, k: None, lambda: None)

            image_steps(dve, B, bring, both, last)

        @block.gpsimd
        def _(pool):
            pool.memset(tn[:], 0.0)
            pool.memset(ys[:], 0.0).then_inc(s.zeros, 1)
            pool.memset(v[:], 1.0).then_inc(s.ones, 1)

            def bring(n, odd):
                wait_apart(pool, s.c2_done, (n + 1) * CHUNKS)
                pool.memset(xp[:, :, :, 0:1], 0.0)
                pool.memset(xp[:, :, :, J + 2:J + 3], 0.0)
                for k in range(EARLY):
                    high_part(n, k)

            def high_part(n, k):
                if k >= NCH:
                    return
                lo, hi = spans[k]
                here = tn[:, k % 2, :, 0:hi - lo]
                wait(pool, s.normed, n * NCH + (k + 1))
                pool.tensor_tensor(here[:, 2, :, 0:PW - 1], here[:, 1, :, 0:PW - 1], here[:, 0, :, 1:PW], ALU.add
                                   ).then_inc(s.padded, 1)
                wait(pool, s.padded, n * NCH + (k + 1))
                for kind in range(3):
                    ins = pool.tensor_copy(xp[:, 0, kind, lo:hi].rearrange("p j w -> p (j w)"),
                                           here[:, kind].rearrange("p j w -> p (j w)"))
                ins.then_inc(s.hi_done, 1)

            def add_conv(n, odd, c):
                wait(pool, s.conv_scaled, n * CHUNKS + (c + 1))
                here = xr[:, odd, ROWS * c:ROWS * c + ROWS].rearrange("p a w -> p (a w)")
                pool.tensor_tensor(here, cv[:, c % 2].rearrange("p a w -> p (a w)"), here, ALU.add).then_inc(s.x3_done, 1)

            def attend(l, a, odd, conv, pad):
                conv(-1)
                pad()
                wait(pool, s.u2_done, l + 1)
                wait(pool, s.kv_done, 2 * l)
                pool.tensor_tensor(cube[:], sq[:], qk[:], ALU.mult).then_inc(s.u3_done, 1)
                wait(pool, s.qt_taken, l + 1)
                wait(pool, s.km_done, 2 * l + 2)
                wait(pool, s.den_done, l)
                pool.tensor_tensor(qs.rearrange("p (q w t) -> p (q w) t", w=2, t=TOK),
                                   qt.rearrange("p (q w t) -> p (q w) t", w=2, t=TOK),
                                   km[:].rearrange("p q w -> p (q w)").unsqueeze(2)
                                   .to_broadcast([P, 2 * Q7, TOK]), ALU.mult).then_inc(s.qs_done, 1)
                conv(0)
                wait(pool, s.o2_done, l + 1)
                here = xr[:, odd, 8 * a:8 * a + 8]
                pool.tensor_tensor(here, o2, here, ALU.add).then_inc(s.xo_done, 1)

            def both(n, odd, attention):
                if attention:
                    for a in range(A7):
                        attend((n - 1) * A7 + a, a, 1 - odd,
                               lambda k: add_conv(n, odd, 2 * a + k) if a or k == 0 else None,
                               lambda: [high_part(n, EARLY + 2 * a + k) for k in range(2)])
                    add_conv(n, odd, CHUNKS - 1)
                else:
                    for k in range(EARLY, NCH):
                        high_part(n, k)
                    for c in range(CHUNKS):
                        add_conv(n, odd, c)

            def last(n, odd):
                for a in range(A7):
                    attend((n - 1) * A7 + a, a, 1 - odd, lambda k: None, lambda: None)

            image_steps(pool, B, bring, both, last)


def build(nc, a, cst, x1, xf, yf, out):
    B = a["x"].shape[0]
    local_conv_and_forward_dft(nc, B, a["x"], a["L0_conv_weight"],
                               a["L0_conv_alpha"].rearrange("c i j -> c (i j)"), cst, x1, xf)
    mix_frequencies(nc, B, a["L1_conv_weight"], xf, yf)
    large_conv_and_attention(nc, B, a, cst, x1, yf, out)


def kernel(**inputs):
    import numpy as _np
    import concourse.bacc as _bacc
    from concourse import mybir as _mybir
    from concourse.bass_utils import run_bass_kernel_spmd as _run

    nc = _bacc.Bacc("TRN2", target_bir_lowering=False, num_devices=1)
    f32 = _mybir.dt.float32
    arrays, args, cst = {}, {}, {}
    for name, a in inputs.items():
        arrays[f"in_{name}"] = a = _np.ascontiguousarray(a)
        args[name] = nc.dram_tensor(f"in_{name}", a.shape, f32, kind="ExternalInput").ap()
    for name, a in constants().items():
        arrays[f"cst_{name}"] = a
        cst[name] = nc.dram_tensor(f"cst_{name}", a.shape, f32, kind="ExternalInput").ap()
    B = inputs["x"].shape[0]
    x1 = nc.dram_tensor("x1", (B, 2, C, J, W), f32, kind="Internal").ap()
    xf = nc.dram_tensor("xf", (KP, P, B, FP), f32, kind="Internal").ap()
    yf = nc.dram_tensor("yf", (KP, P, B, FP), f32, kind="Internal").ap()
    out = nc.dram_tensor("out", (B, C, H, W), f32, kind="ExternalOutput").ap()
    build(nc, args, cst, x1, xf, yf, out)
    return _run(nc, [arrays], core_ids=[0]).results[0]["out"]
```

```python
from contextlib import ExitStack

import numpy as np

import concourse.bass as bass
from concourse import mybir

ALU = mybir.AluOpType
ACT = mybir.ActivationFunctionType
AX = mybir.AxisListType
F32 = mybir.dt.float32
F16 = mybir.dt.float16
BF16 = mybir.dt.bfloat16

P = 128
C = 64
H = W = 112
J = H // 2
PIX = J * W
KH = H // 2
KW = W // 2 + 1
KP = KH // 2
FR = 2 * KW
FP = 128
ROWS = 4
CHUNKS = J // ROWS
N4 = ROWS * W
BANK = 512
GN_EPS = 1e-5


def above_zero(count):
    return not isinstance(count, int) or count > 0


class Count:

    def __init__(self):
        self.value = 0

    def next(self):
        self.value += 1
        return self.value


def constants():
    k, w = np.arange(KH), np.arange(KW)
    n = np.arange(H)
    ang = 2 * np.pi * np.outer(n, k) / H
    fwd_h = (np.stack([np.cos(ang), -np.sin(ang)], -1).reshape(H, 2 * KH) / H).reshape(J, 2, -1).transpose(1, 0, 2)
    fwd_h = fwd_h.reshape(H, -1)
    aw = 2 * np.pi * np.outer(n, w) / W
    fwd_w = np.concatenate([
        np.stack([np.cos(aw), -np.sin(aw)], -1).reshape(W, FR),
        np.stack([np.sin(aw), np.cos(aw)], -1).reshape(W, FR)], 1)
    inv_h = np.zeros((P, 2, H))
    inv_h[0:KH, 0], inv_h[64:64 + KH, 0] = np.cos(ang).T, -np.sin(ang).T
    inv_h[0:KH, 1], inv_h[64:64 + KH, 1] = np.sin(ang).T, np.cos(ang).T
    inv_w = np.zeros((P, W))
    twice = np.where((w == 0) | (w == W // 2), 1.0, 2.0)[:, None] / W
    inv_w[0:KW], inv_w[64:64 + KW] = np.cos(aw).T * twice, -np.sin(aw).T * twice
    p = np.arange(P)
    group = ((p[:, None] % C) // 2 == (p[None, :] % C) // 2) / 4.0
    head = (p[:, None] // 8 == p[None, :] // 8) / 64.0
    tok = np.arange(P)
    win, y, x = tok // 64, tok % 64 // 8, tok % 8
    taps = np.zeros((P, 25, P))
    for t in range(25):
        ok = ((win[:, None] == win[None, :]) & (y[:, None] == y[None, :] + t // 5 - 2)
              & (x[:, None] == x[None, :] + t % 5 - 2))
        taps[:, t] = ok
    made = dict(fwd_h=fwd_h, fwd_w=fwd_w, inv_h=inv_h.reshape(P, 2 * H), inv_w=inv_w, group=group,
                head=head, ident=np.eye(P), taps=taps.reshape(P, 25 * P))
    return {k: np.ascontiguousarray(v, np.float32) for k, v in made.items()}


def pairs(eng, images, step):
    if images > 2:
        step(0)
    if images > 4:
        with eng.Fori(1, images // 2 - 1) as t:
            step(t)


def overlapped(eng, images, prep, conv, rest):
    def step(t):
        for odd in range(2):
            prep(2 * t + (2 + odd), odd)
            conv(2 * t + (1 + odd), 1 - odd)
            rest(2 * t + odd, odd)

    prep(0, 0)
    prep(1, 1)
    conv(0, 0)
    pairs(eng, images, step)
    conv(images - 1, 1)
    rest(images - 2, 0)
    rest(images - 1, 1)


def local_conv_and_forward_dft(nc, B, x, weight, alpha, cst, x1, xf):
    with ExitStack() as ctx:
        sb = lambda name, shape, dt=F32: ctx.enter_context(nc.sbuf_tensor("a_" + name, shape, dt))
        sem = lambda name: ctx.enter_context(nc.semaphore("a_" + name))
        ps = ctx.enter_context(nc.psum_tensor("a_ps", [P, 8, BANK], F32))
        xc = sb("xc", [P, 2, J, W])
        x1s = sb("x1s", [P, J, W])
        signs = sb("signs", [P, 2, J + 1, W + 2], BF16)
        xh = sb("xh", [P, C, W])
        yw = sb("yw", [P, 2, KH, C])
        freq = sb("freq", [P, KP, FP])
        wraw = sb("wraw", [C, C, 9])
        wpos = sb("wpos", [C, C, 9])
        wtern = sb("wtern", [C, C, 9])
        wst = sb("wst", [P, 2, 3, 2, C], BF16)
        ident = sb("ident", [P, P])
        group = sb("group", [P, P])
        fh = sb("fh", [H, 2 * KH])
        fw = sb("fw", [W, 2, FR])
        alph = sb("alph", [P, 1])
        bn = sb("bn", [P, CHUNKS, 6])
        mv = sb("mv", [P, 2])
        stx = sb("stx", [P, 2, 2])
        sty = sb("sty", [P, 2, 2])
        negm = sb("negm", [P, 2])
        gst = sb("gst", [P, 4])
        rstd = sb("rstd", [P, 1])
        dc = sb("dc", [P, 1])

        cst_in = sem("cst_in")
        pads = sem("pads")
        w_tern = sem("w_tern")
        w_turned = sem("w_turned")
        w_put = sem("w_put")
        x_in = [sem("x_in0"), sem("x_in1")]
        x_stats = sem("x_stats")
        x_mean = sem("x_mean")
        neg_mean = sem("neg_mean")
        signed = sem("signed")
        conv_done = sem("conv_done")
        x1_done = sem("x1_done")
        x1_out = sem("x1_out")
        x1_stats = sem("x1_stats")
        x1_group = sem("x1_group")
        x1_var = sem("x1_var")
        x1_std = sem("x1_std")
        x1_rstd = sem("x1_rstd")
        xh_in = sem("xh_in")
        dft_done = sem("dft_done")
        dft_copied = sem("dft_copied")
        dc_done = sem("dc_done")
        freq_out = sem("freq_out")
        prep_at, conv_at, rest_at = sem("prep_at"), sem("conv_at"), sem("rest_at")
        GROUPS = C // 4 + KP // 4

        block = ctx.enter_context(nc.Block())

        @block.sync
        def _(sp):
            for dst, src in ((wraw[:], weight.rearrange("o c h w -> o c (h w)")), (ident[:], cst["ident"]),
                             (group[:], cst["group"]), (fh[:], cst["fwd_h"]),
                             (fw[:], cst["fwd_w"].rearrange("h (r f) -> h r f", r=2)),
                             (alph[0:C], alpha), (alph[C:P], alpha)):
                sp.dma_start(dst, src).then_inc(cst_in, 16)

            def load(n, odd):
                for hp in range(2):
                    src = x[bass.ds(n, 1)].rearrange("b c (j hp) w -> hp (b c) j w", hp=2)[hp]
                    sp.dma_start(xc[C * hp:C * hp + C, odd], src).then_inc(x_in[odd], 16)

            def turn(n):
                sp.wait_ge(x1_out, 16 * (n + 1))
                sp.nop(nofuse=True)
                if above_zero(n):
                    sp.wait_ge(dft_done, n * GROUPS - (GROUPS - C // 4))
                    sp.nop(nofuse=True)
                for hp in range(2):
                    src = x1[bass.ds(n, 1)].rearrange("b hp c j w -> hp (b j) c w")[hp]
                    sp.dma_start(xh[J * hp:J * hp + J], src).then_inc(xh_in, 16)

            load(0, 0)
            load(1, 1)

            def step(t):
                for odd in range(2):
                    sp.wait_ge(x1_done, (2 * t + (odd + 1)) * CHUNKS)
                    sp.nop(nofuse=True)
                    load(2 * t + (2 + odd), odd)
                    turn(2 * t + odd)

            pairs(sp, B, step)
            turn(B - 2)
            turn(B - 1)

        @block.gpsimd
        def _(pool):
            pool.memset(signs[:], 0.0)
            pool.memset(freq[:], 0.0)
            pool.memset(wst[:], 0.0).then_inc(pads, 1)

            def store_x1(n):
                pool.wait_ge(x1_done, (n + 1) * CHUNKS)
                pool.nop(nofuse=True)
                dst = x1[bass.ds(n, 1)].rearrange("b hp c j w -> (b hp c) j w")
                pool.dma_start(dst, x1s[:]).then_inc(x1_out, 16)

            def store_freq(n):
                pool.wait_ge(dft_copied, (n + 1) * GROUPS)
                pool.nop(nofuse=True)
                pool.wait_ge(dc_done, n + 1)
                pool.nop(nofuse=True)
                dst = xf[:, :, bass.ds(n, 1)].rearrange("k p b f -> p k (b f)")
                pool.dma_start(dst, freq[:]).then_inc(freq_out, 16)

            overlapped(pool, B, lambda n, odd: None, lambda n, odd: store_x1(n), lambda n, odd: store_freq(n))
            pool.wait_ge(x1_out, 16 * B)
            pool.wait_ge(freq_out, 16 * B)

        @block.vector
        def _(dve):
            EDGE = 0.5493061443340549
            dve.wait_ge(cst_in, 16 * 7)
            dve.tensor_scalar(wpos[:], wraw[:], EDGE, None, ALU.is_gt).then_inc(w_tern, 1)
            dve.tensor_scalar(wtern[:], wraw[:], -EDGE, None, ALU.is_lt).then_inc(w_tern, 1)
            dve.wait_ge(w_tern, 2)
            dve.tensor_tensor(wtern[:], wpos[:], wtern[:], ALU.subtract).then_inc(w_tern, 1)
            dve.wait_ge(w_turned, 3)
            dve.wait_ge(pads, 1)
            for ky in range(3):
                for q in range(2):
                    pr, rp = divmod(ky + q, 2)
                    dve.tensor_copy(wst[C * rp:C * rp + C, pr, :, q, :],
                                    ps[0:C, ky, 0:3 * C].rearrange("c (k o) -> c k o", k=3)).then_inc(w_put, 1)

            def moments(st, at, before):
                dve.wait_ge(at, before + 1)
                dve.nop(nofuse=True)
                dve.bn_aggr(mv[:], bn[:]).then_inc(at, 1)
                dve.wait_ge(at, before + 2)
                dve.tensor_copy(st[:, 0:1], mv[:, 0:1])
                return dve.scalar_tensor_tensor(st[:, 1:2], mv[:, 0:1], mv[:, 0:1], mv[:, 1:2],
                                                ALU.mult, ALU.add)

            def prep(n, odd):
                dve.wait_ge(x_in[odd], 16 * (n + (2 - odd)))
                for c in range(CHUNKS):
                    ins = dve.bn_stats(bn[:, c], xc[:, odd, ROWS * c:ROWS * c + ROWS].rearrange("p a w -> p (a w)"))
                ins.then_inc(prep_at, 1)
                moments(stx[:, odd], prep_at, 2 * n).then_inc(x_stats, 1)

            def conv(n, odd):
                if above_zero(16 * n):
                    dve.wait_ge(x1_out, 16 * n)
                for c in range(CHUNKS):
                    dve.wait_ge(conv_done, n * CHUNKS + (c + 1))
                    dve.scalar_tensor_tensor(
                        x1s[:, ROWS * c:ROWS * c + ROWS].rearrange("p a w -> p (a w)"), ps[:, c % 3, 0:N4],
                        alph[:], xc[:, odd, ROWS * c:ROWS * c + ROWS].rearrange("p a w -> p (a w)"),
                        ALU.mult, ALU.add).then_inc(x1_done, 1)
                dve.wait_ge(x1_done, (n + 1) * CHUNKS)
                for c in range(CHUNKS):
                    ins = dve.bn_stats(bn[:, c], x1s[:, ROWS * c:ROWS * c + ROWS].rearrange("p a w -> p (a w)"))
                ins.then_inc(conv_at, 1)
                moments(sty[:, odd], conv_at, 2 * n).then_inc(x1_stats, 1)

            def rest(n, odd):
                dve.wait_ge(x1_group, n + 1)
                if above_zero(n):
                    dve.wait_ge(dc_done, n)
                dve.tensor_copy(gst[:, 0:2], ps[:, 7, 0:2]).then_inc(rest_at, 1)
                dve.wait_ge(rest_at, n * 3 + 1)
                dve.scalar_tensor_tensor(gst[:, 2:3], gst[:, 0:1], gst[:, 0:1], gst[:, 1:2],
                                         ALU.mult, ALU.subtract).then_inc(rest_at, 1)
                dve.wait_ge(rest_at, n * 3 + 2)
                if above_zero(n * GROUPS):
                    dve.wait_ge(dft_copied, n * GROUPS)
                dve.tensor_scalar(gst[:, 3:4], gst[:, 2:3], -1.0, GN_EPS, ALU.mult, ALU.add).then_inc(x1_var, 1)
                dve.wait_ge(x1_std, n + 1)
                dve.reciprocal(rstd[:], rstd[:]).then_inc(rest_at, 1)
                dve.wait_ge(rest_at, n * 3 + 3)
                dve.scalar_tensor_tensor(dc[:], gst[:, 0:1], -float(H), rstd[:], ALU.mult, ALU.mult).then_inc(x1_rstd, 1)
                dve.wait_ge(x1_rstd, n + 1)
                dve.wait_ge(dft_copied, n * GROUPS + (C // 4 + 1))
                dve.tensor_tensor(freq[0:C, 0, 0:1], freq[0:C, 0, 0:1], dc[0:C], ALU.add).then_inc(dc_done, 1)

            overlapped(dve, B, prep, conv, rest)

        @block.scalar
        def _(act):
            act.wait_ge(pads, 1)

            def prep(n, odd):
                act.wait_ge(x_mean, n + 1)
                act.activation(negm[:, odd:odd + 1], ps[:, 3, 0:1], ACT.Copy, scale=-1.0).then_inc(neg_mean, 1)
                act.wait_ge(neg_mean, n + 1)
                if above_zero((n - 1) * CHUNKS):
                    act.wait_ge(conv_done, (n - 1) * CHUNKS)
                act.activation(signs[C:P, odd, 0:J, 1:W + 1], xc[0:C, odd], ACT.Sign,
                               bias=negm[0:C, odd:odd + 1]).then_inc(signed, 1)
                act.activation(signs[0:C, odd, 1:J + 1, 1:W + 1], xc[C:P, odd], ACT.Sign,
                               bias=negm[C:P, odd:odd + 1]).then_inc(signed, 1)

            def rest(n, odd):
                for g in range(C // 4):
                    act.wait_ge(dft_done, n * GROUPS + (g + 1))
                    act.activation(yw[0:W, :, :, 4 * g:4 * g + 4].rearrange("w r k c -> w c k r"),
                                   ps[0:W, 4 + g % 3, 0:4 * H].rearrange("w (c k r) -> w c k r", c=4, r=2),
                                   ACT.Copy).then_inc(dft_copied, 1)
                act.wait_ge(x1_var, n + 1)
                act.activation(rstd[:], gst[:, 3:4], ACT.Sqrt).then_inc(x1_std, 1)
                act.wait_ge(x1_rstd, n + 1)
                if above_zero(16 * n):
                    act.wait_ge(freq_out, 16 * n)
                for g in range(KP // 4):
                    act.wait_ge(dft_done, n * GROUPS + (C // 4 + g + 1))
                    act.activation(freq[:, 4 * g:4 * g + 4, 0:FR],
                                   ps[:, 4 + (C // 4 + g) % 3, 0:4 * FR].rearrange("p (k f) -> p k f", k=4), ACT.Copy,
                                   scale=rstd[:]).then_inc(dft_copied, 1)

            overlapped(act, B, prep, lambda n, odd: None, rest)

        @block.tensor
        def _(pe):
            pe.wait_ge(w_tern, 3)
            for ky in range(3):
                for kx in range(3):
                    ins = pe.transpose(ps[0:C, ky, C * kx:C * kx + C], wtern[:, :, 3 * ky + kx], ident[0:C, 0:C])
                ins.then_inc(w_turned, 1)
            pe.wait_ge(w_put, 6)

            def prep(n, odd):
                pe.wait_ge(x_stats, n + 1)
                if above_zero(n):
                    pe.wait_ge(neg_mean, n)
                pe.matmul(ps[:, 3, 0:2], group[:], stx[:, odd], start=True, stop=True,
                          skip_group_check=True).then_inc(x_mean, 1)

            def conv(n, odd):
                pe.wait_ge(signed, 2 * (n + 1))
                for c in range(CHUNKS):
                    if above_zero(n * CHUNKS + max(c - 2, 0)):
                        pe.wait_ge(x1_done, n * CHUNKS + max(c - 2, 0))
                    for t in range(6):
                        pr, kx = divmod(t, 3)
                        ins = pe.matmul(ps[:, c % 3, 0:N4], wst[:, pr, kx].rearrange("p q o -> p (q o)"),
                                        signs[:, odd, ROWS * c + pr:ROWS * c + pr + ROWS, kx:kx + W],
                                        start=(t == 0), stop=(t == 5))
                    ins.then_inc(conv_done, 1)

            def rest(n, odd):
                pe.wait_ge(x1_stats, n + 1)
                if above_zero(n):
                    pe.wait_ge(x1_var, n)
                pe.matmul(ps[:, 7, 0:2], group[:], sty[:, odd], start=True, stop=True,
                          skip_group_check=True).then_inc(x1_group, 1)
                pe.wait_ge(xh_in, 32 * (n + 1))
                for g in range(C // 4):
                    if above_zero(n * GROUPS + max(g - 2, 0)):
                        pe.wait_ge(dft_copied, n * GROUPS + max(g - 2, 0))
                    for c in range(4):
                        ins = pe.matmul(ps[0:W, 4 + g % 3, H * c:H * c + H], xh[0:H, 4 * g + c], fh[:],
                                        start=(c == 0), stop=(c == 3), skip_group_check=True)
                    ins.then_inc(dft_done, 1)
                for g in range(KP // 4):
                    pe.wait_ge(dft_copied, n * GROUPS + (C // 4 if g == 0 else C // 4 + g - 2))
                    for k in range(4 * g, 4 * g + 4):
                        for r in range(2):
                            ins = pe.matmul(ps[:, 4 + (C // 4 + g) % 3, FR * (k % 4):FR * (k % 4) + FR],
                                            yw[0:W, r, 2 * k:2 * k + 2].rearrange("w k c -> w (k c)"), fw[:, r],
                                            start=(k % 4 == 0 and r == 0), stop=(k % 4 == 3 and r == 1),
                                            skip_group_check=True)
                    ins.then_inc(dft_done, 1)

            overlapped(pe, B, prep, conv, rest)


def mix_frequencies(nc, B, weight, xf, yf):
    with ExitStack() as ctx:
        sb = lambda name, shape, dt=F32: ctx.enter_context(nc.sbuf_tensor("b_" + name, shape, dt))
        sem = lambda name: ctx.enter_context(nc.semaphore("b_" + name))
        ps = ctx.enter_context(nc.psum_tensor("b_ps", [P, 8, BANK], F32))
        wt = sb("wt", [P, 2, C, FP // 2, 2])
        xs = sb("xs", [P, 2, B, FP // 2, 2])
        xj = sb("xj", [P, 2, B, FP // 2, 2])
        ys = sb("ys", [P, 2, B, FP // 2, 2])
        loaded = [sem("loaded0"), sem("loaded1")]
        turned = sem("turned")
        mixed = [sem("mixed_low"), sem("mixed_high")]
        copied = [sem("copied_low"), sem("copied_high")]
        stored = [sem("stored0"), sem("stored1")]
        padded = sem("padded")
        PER = min(BANK // (2 * B), 8)
        GROUPS = -(-KW // PER)

        block = ctx.enter_context(nc.Block())

        @block.sync
        def _(sp):
            def load(k, odd):
                for half in range(2):
                    if above_zero((k - 1) * GROUPS):
                        sp.wait_ge(mixed[half], (k - 1) * GROUPS)
                        sp.nop(nofuse=True)
                src = weight.rearrange("c o (k two) w r -> two k c o w r", two=2)
                for half in range(2):
                    sp.dma_start(wt[C * half:C * half + C, odd],
                                 src[half, bass.ds(k, 1)].rearrange("k c o w r -> (k c) o (w r)")
                                 ).then_inc(loaded[odd], 16)
                sp.dma_start(xs[:, odd], xf[bass.ds(k, 1)].rearrange("k p b f -> (k p) (b f)")).then_inc(loaded[odd], 16)

            load(0, 0)
            load(1, 1)
            with sp.Fori(0, KP // 2 - 1) as t:
                for odd in range(2):
                    load(2 * t + (2 + odd), odd)

        @block.gpsimd
        def _(pool):
            pool.memset(ys[:], 0.0).then_inc(padded, 1)

            def store(k, odd):
                for half in range(2):
                    pool.wait_ge(copied[half], (k + 1) * GROUPS)
                    pool.nop(nofuse=True)
                pool.dma_start(yf[bass.ds(k, 1)].rearrange("k p b f -> (k p) (b f)"), ys[:, odd]
                               ).then_inc(stored[odd], 16)

            store(0, 0)
            store(1, 1)
            with pool.Fori(1, KP // 2) as t:
                for odd in range(2):
                    store(2 * t + odd, odd)
            for odd in range(2):
                pool.wait_ge(stored[odd], 16 * (KP // 2))

        def take(eng, copy, half, between):
            def body(k, odd):
                if above_zero(8 * (k - odd)):
                    eng.wait_ge(stored[odd], 8 * (k - odd))
                for g in range(GROUPS):
                    lo, hi = g * PER, min(g * PER + PER, KW)
                    eng.wait_ge(mixed[half], k * GROUPS + (g + 1))
                    copy(ys[C * half:C * half + C, odd, :, lo:hi].rearrange("p b w r -> p w b r"),
                         ps[C * half:C * half + C, 4 * half + g % 4, 0:2 * B * (hi - lo)].rearrange(
                             "p (w b r) -> p w b r", b=B, r=2)).then_inc(copied[half], 1)
                    if g == GROUPS // 2:
                        between(k, odd)

            def step(t):
                for odd in range(2):
                    body(2 * t + odd, odd)

            eng.wait_ge(padded, 1)
            step(0)
            with eng.Fori(1, KP // 2 - 1) as t:
                step(t)
            step(KP // 2 - 1)

        @block.scalar
        def _(act):
            take(act, lambda o, i: act.activation(o, i, ACT.Copy), 0, lambda k, odd: None)

        @block.vector
        def _(dve):
            def turn(k, odd):
                dve.wait_ge(loaded[odd], 24 * (k + (2 - odd)))
                for half in range(2):
                    if above_zero((k - 1) * GROUPS):
                        dve.wait_ge(mixed[half], (k - 1) * GROUPS)
                dve.tensor_scalar(xj[:, odd, :, 0:KW, 0], xs[:, odd, :, 0:KW, 1], -1.0, None, ALU.mult)
                dve.tensor_copy(xj[:, odd, :, 0:KW, 1], xs[:, odd, :, 0:KW, 0]).then_inc(turned, 1)

            turn(0, 0)
            turn_next = lambda k, odd: turn(k + 1, 1 - odd) if not isinstance(k, int) or k < KP - 1 else None
            take(dve, lambda o, i: dve.tensor_copy(o, i), 1, turn_next)

        @block.tensor
        def _(pe):
            def body(k, odd):
                pe.wait_ge(loaded[odd], 24 * (k + (2 - odd)))
                pe.wait_ge(turned, k + 1)
                for g in range(GROUPS):
                    lo, hi = g * PER, min(g * PER + PER, KW)
                    for half in range(2):
                        if above_zero(k * GROUPS + (g - 3)):
                            pe.wait_ge(copied[half], k * GROUPS + (g - 3))
                            pe.nop(nofuse=True)
                    for f in range(lo, hi):
                        at = 2 * B * (f - lo)
                        for r, src in ((0, xs), (1, xj)):
                            for half in range(2):
                                rows = slice(C * half, C * half + C)
                                ins = pe.matmul(ps[rows, 4 * half + g % 4, at:at + 2 * B], wt[rows, odd, :, f, r],
                                                src[rows, odd, :, f], start=(f == lo and r == 0),
                                                stop=(f == hi - 1 and r == 1), skip_group_check=True)
                                if f == hi - 1 and r == 1:
                                    ins.then_inc(mixed[half], 1)
            body(0, 0)
            body(1, 1)
            with pe.Fori(1, KP // 2) as t:
                for odd in range(2):
                    body(2 * t + odd, odd)


WS = 8
TOK = WS * WS
A7 = H // (2 * WS)
Q7 = W // (2 * WS)
QTOK = Q7 * 2 * TOK
PW = W // 2 + 4
SUMS = ((4, 3, 0, 1, W // 2 + 1), (0, 4, 1, 0, W // 2), (7, 4, 2, 0, W // 2))
TAPS = sum(x[1] for x in SUMS)
CONV_MMS = TAPS * 4 * 3
EARLY = 4
NCH = 15
EPS = 1e-6


def prepare_weights(nc, args, cst, to):
    with ExitStack() as ctx:
        sb = lambda name, shape, dt=F32: ctx.enter_context(nc.sbuf_tensor("w_" + name, shape, dt))
        sem = lambda name: ctx.enter_context(nc.semaphore("w_" + name))
        ps = ctx.enter_context(nc.psum_tensor("w_ps", [P, 8, BANK], F32))
        conv_w = sb("conv_w", [P, C, 49])
        parts = sb("parts", [C, C, 7, TAPS])
        taps = sb("taps", [P, 25, P])
        stencil = sb("stencil", [P, WS, 25])
        qkw = sb("qkw", [P, C])
        vw = sb("vw", [C, C])
        pw = sb("pw", [C, C])
        qkvb = sb("qkvb", [P, 3 * C])
        pos = sb("pos", [P, C])
        scale = sb("scale", [P, C])
        soft = sb("soft", [P, C])
        inv_sc = sb("inv_sc", [P, C])
        top = sb("top", [P, 1])
        up = sb("up", [P, 1])
        sbias = sb("sbias", [P, 1])
        pb = sb("pb", [P, 1])
        loaded, act_at, dve_at = sem("loaded"), sem("act_at"), sem("dve_at")
        cleared, turned, put, bias_sum = sem("cleared"), sem("turned"), sem("put"), sem("bias_sum")
        soft_done, scaled_up, split = sem("soft_done"), sem("scaled_up"), sem("split")
        LOADS = [
            (to["ident"][:], cst["ident"]), (to["group"][:], cst["group"]), (to["head"][:], cst["head"]),
            (to["inv_h"][:], cst["inv_h"].rearrange("p (r h) -> p r h", r=2)), (to["inv_w"][:], cst["inv_w"]),
            (taps[:], cst["taps"].rearrange("p (t q) -> p t q", t=25)),
            (conv_w[0:C], args["L2_conv_weight"].rearrange("o c h w -> o c (h w)")),
            (conv_w[C:P], args["L2_conv_weight"].rearrange("o c h w -> o c (h w)")),
            (to["cbias"][0:C], args["L2_conv_bias"]), (to["cbias"][C:P], args["L2_conv_bias"]),
            (stencil[:].rearrange("p d t -> p (d t)"),
             args["L3_conv_dwc_w"].rearrange("d i h w -> (d i h w)").partition_broadcast(P)),
            (qkw[:], args["L3_conv_qkv_w"][0:P]), (vw[:], args["L3_conv_qkv_w"][P:3 * C]),
            (pw[:], args["L3_conv_proj_w"]),
            (qkvb[:], args["L3_conv_qkv_b"].partition_broadcast(P)),
            (pos[0:C], args["L3_conv_pos_enc"].rearrange("i t c -> (i t) c")),
            (pos[C:P], args["L3_conv_pos_enc"].rearrange("i t c -> (i t) c")),
            (scale[:], args["L3_conv_scale"].rearrange("i j c -> (i j c)").partition_broadcast(P)),
            (pb[0:C], args["L3_conv_proj_b"]), (pb[C:P], args["L3_conv_proj_b"]),
        ] + [(sbias[WS * h:WS * h + WS], args["L3_conv_dwc_b"]) for h in range(P // WS)]
        block = ctx.enter_context(nc.Block())

        @block.sync
        def _(sp):
            for dst, src in LOADS:
                if len(src.shape) == 1:
                    src = src.rearrange("(c i) -> c i", i=1)
                sp.dma_start(dst, src).then_inc(loaded, 16)

        @block.gpsimd
        def _(pool):
            pool.memset(to["wst"][:], 0.0)
            pool.memset(to["wproj"][:], 0.0)
            pool.memset(to["wqkv"][:], 0.0).then_inc(cleared, 1)

        @block.scalar
        def _(act):
            done = Count()
            act.wait_ge(loaded, 16 * len(LOADS))
            act.activation(soft[:], scale[:], ACT.Abs).then_inc(act_at, 1)
            act.wait_ge(act_at, done.next())
            act.activation(soft[:], soft[:], ACT.Exp, scale=-1.0).then_inc(act_at, 1)
            act.wait_ge(act_at, done.next())
            act.activation(soft[:], soft[:], ACT.Ln, bias=1.0).then_inc(soft_done, 1)

        @block.tensor
        def _(pe):
            pe.wait_ge(loaded, 16 * len(LOADS))
            pe.transpose(ps[0:C, 7, 0:P], qkw[:], to["ident"][:])
            pe.transpose(ps[0:C, 7, P:P + C], vw[:], to["ident"][0:C, 0:C])
            pe.transpose(ps[0:C, 7, P + C:2 * P], pw[:], to["ident"][0:C, 0:C]).then_inc(turned, 1)
            pe.wait_ge(scaled_up, 1)
            for ky in range(7):
                if ky >= 3:
                    pe.wait_ge(split, ky - 2)
                for t in range(TAPS):
                    ins = pe.transpose(ps[0:C, 2 * (ky % 3) + t // 8, C * (t % 8):C * (t % 8) + C],
                                       parts[:, :, ky, t], to["ident"][0:C, 0:C])
                ins.then_inc(turned, 1)
            pe.wait_ge(put, 1)
            pe.matmul(ps[:, 7, 0:1], to["wproj"][:].rearrange("p r c -> p (r c)"), sbias[:],
                      start=True, stop=True).then_inc(bias_sum, 1)

        @block.vector
        def _(dve):
            done = Count()
            dve.wait_ge(loaded, 16 * len(LOADS))
            dve.tensor_reduce(top[:], conv_w[:].rearrange("p c t -> p (c t)"), AX.X, ALU.max,
                              apply_absolute_value=True).then_inc(dve_at, 1)
            dve.wait_ge(dve_at, done.next())
            dve.tensor_scalar(top[:], top[:], 1e-30, None, ALU.max).then_inc(dve_at, 1)
            dve.wait_ge(dve_at, done.next())
            dve.reciprocal(up[:], top[:]).then_inc(dve_at, 1)
            dve.wait_ge(dve_at, done.next())
            dve.tensor_scalar(to["unscale"][:], top[:], 1.0 / 256, None, ALU.mult)
            dve.tensor_scalar(conv_w[:], conv_w[:], up[:], 256.0, ALU.mult, ALU.mult).then_inc(dve_at, 1)
            dve.wait_ge(dve_at, done.next())
            h = conv_w[0:C].rearrange("o c (y x) -> o c y x", y=7)
            for y in range(7):
                dve.tensor_copy(parts[:, :, y, 0:4], h[:, :, y, 0:7:2])
                dve.tensor_copy(parts[:, :, y, 4:7], h[:, :, y, 1:7:2])
                dve.tensor_copy(parts[:, :, y, 7:8], h[:, :, y, 0:1])
                ins = dve.tensor_tensor(parts[:, :, y, 8:11], h[:, :, y, 2:7:2], h[:, :, y, 1:7:2], ALU.add)
            ins.then_inc(scaled_up, 1)
            dve.wait_ge(soft_done, 1)
            dve.scalar_tensor_tensor(soft[:], scale[:], 0.0, soft[:], ALU.max, ALU.add).then_inc(dve_at, 1)
            dve.wait_ge(dve_at, done.next())
            dve.reciprocal(inv_sc[:], soft[:]).then_inc(dve_at, 1)
            dve.wait_ge(dve_at, done.next())
            dve.tensor_tensor(qkvb[:, C:2 * C], qkvb[:, C:2 * C], pos[:], ALU.add).then_inc(dve_at, 1)
            dve.wait_ge(dve_at, done.next())
            for r in range(2):
                for k in range(2):
                    dve.tensor_tensor(to["bqk"][:, k, r], qkvb[:, C * k:C * k + C], inv_sc[:], ALU.mult)
                dve.tensor_copy(to["bv"][:, C * r:C * r + C], qkvb[:, 2 * C:3 * C])
            dve.tensor_scalar(to["epsc"][:], inv_sc[:], EPS, None, ALU.mult)
            dve.wait_ge(turned, 1)
            dve.wait_ge(cleared, 1)
            for r in range(2):
                rows = slice(C * r, C * r + C)
                for k in range(2):
                    dve.tensor_tensor(to["wqkv"][rows, k, r], ps[0:C, 7, C * k:C * k + C], inv_sc[0:C], ALU.mult)
                dve.tensor_copy(to["wqkv"][rows, 2, r], ps[0:C, 7, P:P + C])
                ins = dve.tensor_copy(to["wproj"][rows, r], ps[0:C, 7, P + C:2 * P])
            ins.then_inc(put, 1)
            for ky in range(7):
                dve.wait_ge(turned, ky + 2)
                got = ps[0:C, 2 * (ky % 3):2 * (ky % 3) + 2].rearrange("c b x -> c (b x)")[:, 0:TAPS * C].rearrange(
                    "c (k o) -> c k o", k=TAPS)
                for q in range(2):
                    pr, rp = divmod(ky + q, 2)
                    high = to["wst"][C * rp:C * rp + C, 0, pr, :, q]
                    dve.tensor_copy(high, got).then_inc(dve_at, 1)
                    dve.wait_ge(dve_at, done.next())
                    ins = dve.tensor_tensor(to["wst"][C * rp:C * rp + C, 1, pr, :, q], got, high, ALU.subtract)
                ins.then_inc(split, 1)
            for t in range(25):
                for d in range(WS):
                    if t == 0:
                        ins = dve.tensor_scalar(to["spread"][:, d], taps[:, t], stencil[:, d, t:t + 1], None, ALU.mult)
                    else:
                        ins = dve.scalar_tensor_tensor(to["spread"][:, d], taps[:, t], stencil[:, d, t:t + 1],
                                                       to["spread"][:, d], ALU.mult, ALU.add)
                ins.then_inc(dve_at, 1)
                dve.wait_ge(dve_at, done.next())
            dve.wait_ge(bias_sum, 1)
            dve.tensor_tensor(to["pbias"][:], ps[:, 7, 0:1], pb[:], ALU.add)


QBANK = (2, 3, 4, 7, 5, 6, 2)
CUBES = 4
QGROUPS = ((0, 3, 2), (3, 1, 7), (4, 2, 5), (6, 1, 2))
PIECES = (24, 138, 142, 160, 250)
FIRST_PIECES = (0, 208, 232, 250, 320)
SECOND_PIECES = (56, 170, 174, 190, 260)


def image_steps(eng, images, bring, both, last):
    def step(t):
        for odd in range(2):
            bring(2 * t + (1 + odd), 1 - odd)
            both(2 * t + (1 + odd), 1 - odd, True)

    bring(0, 0)
    both(0, 0, False)
    pairs(eng, images, step)
    bring(images - 1, 1)
    both(images - 1, 1, True)
    last(images, 0)


def large_conv_and_attention(nc, B, args, cst, x1, yf, out):
    with ExitStack() as keep:
        sb = lambda name, shape, dt=F32: keep.enter_context(nc.sbuf_tensor("c_" + name, shape, dt))
        ident = sb("ident", [P, P])
        group = sb("group", [P, P])
        head = sb("head", [P, P])
        inv_h = sb("inv_h", [P, 2, H])
        inv_w = sb("inv_w", [P, W])
        wst = sb("wst", [P, 2, 4, TAPS, 2, C], F16)
        unscale = sb("unscale", [P, 1])
        cbias = sb("cbias", [P, 1])
        wqkv = sb("wqkv", [P, 3, 2, C])
        wproj = sb("wproj", [P, 2, C])
        bqk = sb("bqk", [P, 2, 2, C])
        bv = sb("bv", [P, 2 * C])
        epsc = sb("epsc", [P, C])
        spread = sb("spread", [P, WS, P])
        pbias = sb("pbias", [P, 1])
        prepare_weights(nc, args, cst, dict(
            ident=ident, group=group, head=head, inv_h=inv_h, inv_w=inv_w, wst=wst, unscale=unscale,
            cbias=cbias, wqkv=wqkv, wproj=wproj, bqk=bqk, bv=bv, epsc=epsc, spread=spread, pbias=pbias))

        sem = lambda name: keep.enter_context(nc.semaphore("c_" + name))
        ps = keep.enter_context(nc.psum_tensor("c_ps", [P, 8, BANK], F32))
        xr = sb("xr", [P, 2, J, W])
        ys = sb("ys", [P, C, FP])
        xp_all = sb("xp", [P, 2 * 3 * (J + 3) * PW], F16)
        xp = xp_all[:].rearrange("p (s k j w) -> p s k j w", s=2, k=3, j=J + 3)
        z = xp_all[:, 0:2 * H * C].bitcast(F32).rearrange("p (h c) -> p h c", h=H)
        tn = sb("tn", [P, 2, 3, ROWS, PW])
        cv = sb("cv", [P, 2, ROWS, W])
        part = sb("part", [P, ROWS, W // 2 + 1])
        bn2 = sb("bn2", [P, CHUNKS, 6])
        bn3 = sb("bn3", [P, CHUNKS, 6])
        mv = sb("mv", [P, 2])
        st = sb("st", [P, 2])
        gst = sb("gst", [P, 4])
        nrm = sb("nrm", [P, 2, 2])
        xn = sb("xn", [P, 2 * Q7, TOK])
        qk = sb("qk", [P, Q7, 2, 2, C])
        v = sb("v", [P, 2 * Q7, C + 1])
        sq = sb("sq", [P, Q7, 2, 2, C])
        cube = sb("cube", [P, Q7, 2, 2, C])
        s2 = sb("s2", [P, 4 * Q7])
        s6 = sb("s6", [P, 4 * Q7])
        fac = sb("fac", [P, 4 * Q7])
        kvm = sb("kvm", [P, 2, Q7, P])
        km = sb("km", [P, Q7, 2])
        qt = qk[:].rearrange("p q k r c -> p (q k r c)")[:, 0:QTOK]
        qs = sq[:].rearrange("p q k r c -> p (q k r c)")[:, 0:QTOK]
        den = sq[:].rearrange("p q k r c -> p (q k r c)")[:, QTOK:2 * QTOK]
        att = sb("att", [P, 2 * Q7, TOK])
        dw = att[:].rearrange("p w t -> p (w t)").rearrange("p (q r h d) -> p q r h d", q=Q7, r=2, d=WS)
        o2 = kvm[:].rearrange("p w q x -> p (w q x)")[:, 0:8 * W].rearrange("p (j x) -> p j x", j=8)

        x1_in = [sem("x1_in0"), sem("x1_in1")]
        names = """ys_in zeros c1_done c1_taken c2_done padded high_done bordered x2_done bn_at stats_done grouped var_done std_done
            rstd_done normed hi_done lo_done ab_done ab_taken g_done g_taken conv_scaled part_done x3_done xn_done qkv_done qk_taken u_done u2_done
            s2_done u3_done u3_rest u6_done s6_done ratio_at ratio_done f_done scaled dwc_done dw_taken qt_done qt_taken
            kv_done kvm_done km_done qs_done num_done den_done den_taken ones x2_stats dwt_done inv_done mul_done att_done
            proj_done o2_done xo_done out_done bn3_done""".split()
        s = type("Semaphores", (), {n: sem(n) for n in names})
        block = keep.enter_context(nc.Block())
        spans = [(1 + ROWS * k, min(1 + ROWS * (k + 1), J + 2)) for k in range(NCH)]

        @block.sync
        def _(sp):
            def load_ys(n):
                if above_zero(16 * n):
                    sp.wait_ge(s.c1_done, 16 * n)
                    sp.nop(nofuse=True)
                src = yf[:, :, bass.ds(n, 1)].rearrange("k (kp o) b f -> (k kp) o (b f)", kp=2)
                sp.dma_start(ys[0:KH], src).then_inc(s.ys_in, 16)
                sp.dma_start(ys[64:64 + KH, :, 0:FP - 1], src[:, :, 1:FP]).then_inc(s.ys_in, 16)

            def load_x1(n, odd):
                sp.dma_start(xr[:, odd], x1[bass.ds(n, 1)].rearrange("b hp c j w -> (b hp c) j w")
                             ).then_inc(x1_in[odd], 16)

            def store(n, odd):
                for a in range(A7):
                    sp.wait_ge(s.xo_done, n * A7 + (a + 1))
                    sp.nop(nofuse=True)
                    for hp in range(2):
                        dst = out[bass.ds(n, 1), :, 16 * a:16 * a + 16].rearrange(
                            "b c (j hp) w -> hp (b c) j w", hp=2)[hp]
                        sp.dma_start(dst, xr[C * hp:C * hp + C, odd, 8 * a:8 * a + 8]).then_inc(s.out_done, 16)

            sp.wait_ge(s.zeros, 1)
            load_ys(0)
            load_x1(0, 0)
            load_ys(1)
            load_x1(1, 1)

            def step(t):
                for odd in range(2):
                    load_ys(2 * t + (2 + odd))
                    store(2 * t + odd, odd)
                    sp.wait_ge(s.out_done, (2 * t + (1 + odd)) * (A7 * 32))
                    sp.nop(nofuse=True)
                    load_x1(2 * t + (2 + odd), odd)

            pairs(sp, B, step)
            store(B - 2, 0)
            store(B - 1, 1)
            sp.wait_ge(s.out_done, B * A7 * 32)

        @block.tensor
        def _(pe):
            at = [0]
            pe.wait_ge(s.ones, 1)

            def conv_some(n, upto):
                while at[0] < upto:
                    c, i = divmod(at[0], CONV_MMS)
                    which = 0 if i < 36 else 1 if i < 84 else 2
                    first, taps, kind, shift, width = SUMS[which]
                    i -= (0, 36, 84)[which]
                    t, part = divmod(i, 3)
                    pr, k = divmod(t, taps)
                    if i == 0 and which == 0:
                        pe.wait_ge(s.lo_done, n * NCH + min(c + 2, NCH))
                        if above_zero(n * CHUNKS + c):
                            pe.wait_ge(s.ab_taken, n * CHUNKS + c)
                    if i == 0 and which == 2:
                        if above_zero(n * CHUNKS + c):
                            pe.wait_ge(s.g_taken, n * CHUNKS + c)
                    ws, xs = ((0, 0), (0, 1), (1, 0))[part]
                    col = ROWS * (W // 2) if which == 0 else 0
                    ins = pe.matmul(ps[:, which // 2, col:col + ROWS * width],
                                    wst[:, ws, pr, first + k].rearrange("p q o -> p (q o)"),
                                    xp[:, xs, kind, ROWS * c + pr:ROWS * c + pr + ROWS, shift + k:shift + k + width],
                                    start=(i == 0), stop=(i == 12 * taps - 1), skip_group_check=True)
                    if i == 12 * taps - 1 and which:
                        ins.then_inc(s.ab_done if which == 1 else s.g_done, 1)
                    at[0] += 1

            def stats(count):
                pe.wait_ge(s.stats_done, count + 1)
                if above_zero(count):
                    pe.wait_ge(s.rstd_done, count)
                pe.matmul(ps[:, 1, 0:2], group[:], st[:], start=True, stop=True).then_inc(s.grouped, 1)

            def bring(n, odd):
                pe.wait_ge(s.ys_in, 32 * (n + 1))
                if above_zero((n - 1) * A7):
                    pe.wait_ge(s.o2_done, (n - 1) * A7)
                for g in range(16):
                    if g >= 5:
                        pe.wait_ge(s.c1_taken, n * 16 + (g - 4))
                        pe.nop(nofuse=True)
                    for o in range(4 * g, 4 * g + 4):
                        for r in range(2):
                            ins = pe.matmul(ps[64 * r:64 * r + 64, 2 + g % 5, H * (o % 4):H * (o % 4) + H],
                                            ys[0:120, o, 0:FP:2], inv_h[0:120, r],
                                            start=(o % 4 == 0), stop=(o % 4 == 3), skip_group_check=True)
                    ins.then_inc(s.c1_done, 1)
                if above_zero(n):
                    if above_zero(n * CHUNKS):
                        pe.wait_ge(s.g_taken, n * CHUNKS)
                    stats(2 * n - 1)
                pe.wait_ge(s.c1_taken, n * 16 + 16)
                for g in range(CHUNKS):
                    pe.wait_ge(s.x2_done, n * CHUNKS + max(g - 4, 0))
                    for j in range(4 * g, 4 * g + 4):
                        ins = pe.matmul(ps[:, 2 + g % 5, W * (j % 4):W * (j % 4) + W],
                                        z[:, 2 * j:2 * j + 2].rearrange("p h c -> p (h c)"), inv_w[:],
                                        start=(j % 4 == 0), stop=(j % 4 == 3), skip_group_check=True)
                    ins.then_inc(s.c2_done, 1)
                if above_zero(n):
                    for q in range(4):
                        if q < 3:
                            pe.wait_ge(s.x2_done, n * CHUNKS + (CHUNKS - 3 + q))
                        project((n - 1) * A7, (q,))
                stats(2 * n)
                if above_zero(n):
                    project((n - 1) * A7, range(4, Q7))

            def project(l, quads):
                pe.wait_ge(s.xn_done, l + 1)
                for q in quads:
                    if q == 4:
                        if above_zero(l):
                            pe.wait_ge(s.o2_done, l)
                    if q == 6:
                        pe.wait_ge(s.qk_taken, 4 * l + 1)
                    ins = pe.matmul(ps[:, QBANK[q], 0:6 * C], xn[:, 2 * q:2 * q + 2].rearrange("p w t -> p (w t)"),
                                    wqkv[:].rearrange("p k r c -> p (k r c)"), start=True, stop=True)
                    if q in (2, 3, 5, 6):
                        ins.then_inc(s.qkv_done, 1)

            def attend(l, a, conv):
                pieces = (FIRST_PIECES, SECOND_PIECES, PIECES)[min(a, 2)]
                if a:
                    project(l, range(Q7))
                if a:
                    conv(pieces[0])
                pe.wait_ge(s.qk_taken, 4 * l + 4)
                for d in range(WS):
                    ins = pe.matmul(ps[:, 3 + d // 4, 112 * (d % 4):112 * (d % 4) + 112], spread[:, d],
                                    v[:, :, 0:C].rearrange("p q (h d) -> p q h d", d=WS)[:, :, :, d],
                                    start=(d % 4 == 0), stop=(d % 4 == 3), skip_group_check=True)
                ins.then_inc(s.dwc_done, 1)
                conv(pieces[1])
                pe.wait_ge(s.scaled, l + 1)
                for q in range(Q7):
                    ins = pe.transpose(ps[:, 5 + q // 4, P * (q % 4):P * (q % 4) + P], cube[:, q, 0].rearrange("p r c -> p (r c)"), ident[:])
                ins.then_inc(s.qt_done, 1)
                conv(pieces[2])
                pe.wait_ge(s.dw_taken, l + 1)
                pe.nop(nofuse=True)
                pe.wait_ge(s.qt_taken, l + 1)
                pe.nop(nofuse=True)
                for w in range(2):
                    rows = slice(TOK * w, TOK * w + TOK)
                    for q in range(Q7):
                        for r in range(2):
                            ins = pe.matmul(ps[C * r:C * r + C, 2 + 3 * w + q // 4, 65 * (q % 4):65 * (q % 4) + 65],
                                            cube[rows, q, 1, r], v[rows, 2 * q + r],
                                            start=(q % 4 == 0), stop=(q in (3, 6)), skip_group_check=True)
                    ins.then_inc(s.kv_done, 1)
                conv(pieces[3])
                pe.wait_ge(s.kvm_done, 4 * l + 4)
                pe.wait_ge(s.km_done, 2 * l + 2)
                for q in range(Q7):
                    for w in range(2):
                        col = (2 * q + w) * TOK
                        ins = pe.matmul(ps[:, 2 + col // BANK, col % BANK:col % BANK + TOK], kvm[:, w, q],
                                        qt[:, col:col + TOK], start=(col % BANK == 0),
                                        stop=(col % BANK == BANK - TOK or col == QTOK - TOK), skip_group_check=True)
                ins.then_inc(s.num_done, 1)
                pe.wait_ge(s.qs_done, l + 1)
                for lo, hi in ((0, BANK), (BANK, QTOK)):
                    ins = pe.matmul(ps[:, 5 + lo // BANK, 0:hi - lo], head[:], qs[:, lo:hi], start=True, stop=True)
                ins.then_inc(s.den_done, 1)
                for q in range(Q7):
                    ins = pe.transpose(ps[:, 4 + 3 * (q // 4), P * (q % 4):P * (q % 4) + P],
                                       dw[:, q].rearrange("p r h d -> p (r h d)"), ident[:])
                ins.then_inc(s.dwt_done, 1)
                conv(pieces[4])
                pe.wait_ge(s.att_done, l + 1)
                for y in range(2):
                    ins = pe.matmul(ps[:, 5 + y, 0:N4], wproj[:].rearrange("p r c -> p (r c)"),
                                    att[:].rearrange("p w (y x) -> p y w x", y=WS)[:, 4 * y:4 * y + 4],
                                    start=True, stop=True)
                ins.then_inc(s.proj_done, 1)
                conv(2 * CONV_MMS)

            def both(n, odd, attention):
                at[0] = 0
                if attention:
                    for a in range(A7):
                        attend((n - 1) * A7 + a, a, lambda k: conv_some(n, 2 * CONV_MMS * a + k))
                else:
                    conv_some(n, CHUNKS * CONV_MMS)

            def last(n, odd):
                if above_zero(n * CHUNKS):
                    pe.wait_ge(s.g_taken, n * CHUNKS)
                stats(2 * n - 1)
                project((n - 1) * A7, range(Q7))
                for a in range(A7):
                    attend((n - 1) * A7 + a, a, lambda k: None)

            image_steps(pe, B, bring, both, last)

        @block.scalar
        def _(act):
            def deviation(count):
                act.wait_ge(s.var_done, count + 1)
                act.activation(gst[:, 3:4], gst[:, 3:4], ACT.Sqrt).then_inc(s.std_done, 1)

            def bring(n, odd):
                if above_zero(n * CHUNKS):
                    act.wait_ge(s.g_done, n * CHUNKS)
                for g in range(16):
                    act.wait_ge(s.c1_done, n * 16 + (g + 1))
                    act.activation(z[:, :, 4 * g:4 * g + 4].rearrange("p h o -> p o h"),
                                   ps[:, 2 + g % 5, 0:4 * H].rearrange("p (o h) -> p o h", o=4), ACT.Copy
                                   ).then_inc(s.c1_taken, 1)
                if above_zero(n):
                    deviation(2 * n - 1)
                    if above_zero(2 * n):
                        act.wait_ge(s.rstd_done, 2 * n)
                    window_rows((n - 1) * A7, 0, 1 - odd)
                deviation(2 * n)
                act.wait_ge(s.rstd_done, 2 * n + 1)
                act.wait_ge(s.bordered, n + 1)
                for k in range(EARLY):
                    padded_chunk(n, odd, k)

            def padded_chunk(n, odd, k):
                if k >= NCH:
                    return
                lo, hi = spans[k]
                if above_zero(n * NCH + (k - 1)):
                    act.wait_ge(s.lo_done, n * NCH + (k - 1))
                put = tn[:, k % 2, 0:2, :, 2:2 + W // 2].rearrange("p k j i -> p j i k")
                get = xr[:, odd].rearrange("p j (i k) -> p j i k", k=2)
                if k == 0:
                    act.activation(put[0:C, 0:1], get[C:P, 0:1], ACT.Copy, scale=0.0)
                a = max(lo, 2)
                act.activation(put[0:C, a - lo:hi - lo], get[C:P, a - 2:hi - 2], ACT.Identity,
                               scale=nrm[C:P, 0, 0:1], bias=nrm[C:P, 0, 1:2])
                if k < NCH - 1:
                    ins = act.activation(put[C:P, 0:hi - lo], get[0:C, lo - 1:hi - 1], ACT.Identity,
                                         scale=nrm[0:C, 0, 0:1], bias=nrm[0:C, 0, 1:2])
                else:
                    ins = act.activation(put[C:P, 0:1], get[0:C, 0:1], ACT.Copy, scale=0.0)
                ins.then_inc(s.normed, 1)
                high = xp[:, 0, 0:2, :, 2:2 + W // 2].rearrange("p k j i -> p j i k")
                if k == 0:
                    act.activation(high[0:C, 1:2], get[C:P, 0:1], ACT.Copy, scale=0.0)
                act.activation(high[0:C, a:hi], get[C:P, a - 2:hi - 2], ACT.Identity,
                               scale=nrm[C:P, 0, 0:1], bias=nrm[C:P, 0, 1:2])
                if k < NCH - 1:
                    ins = act.activation(high[C:P, lo:hi], get[0:C, lo - 1:hi - 1], ACT.Identity,
                                         scale=nrm[0:C, 0, 0:1], bias=nrm[0:C, 0, 1:2])
                else:
                    ins = act.activation(high[C:P, lo:hi], get[0:C, 0:1], ACT.Copy, scale=0.0)
                ins.then_inc(s.high_done, 1)

            def window_rows(l, a, odd):
                if above_zero(4 * l):
                    act.wait_ge(s.qkv_done, 4 * l)
                for wr in range(2):
                    for hp in range(2):
                        ins = act.activation(
                            xn[C * wr:C * wr + C].rearrange("p w (j hp x) -> p hp j w x", hp=2, x=WS)[:, hp],
                            xr[C * hp:C * hp + C, odd, 8 * a + 4 * wr:8 * a + 4 * wr + 4].rearrange(
                                "p j (w x) -> p j w x", x=WS),
                            ACT.Identity, scale=nrm[C * hp:C * hp + C, 1, 0:1], bias=nrm[C * hp:C * hp + C, 1, 1:2])
                ins.then_inc(s.xn_done, 1)

            def scale_conv(n, c):
                act.wait_ge(s.g_taken, n * CHUNKS + (c + 1))
                act.activation(cv[:, c % 2], cv[:, c % 2], ACT.Identity, scale=unscale[:], bias=cbias[:]
                               ).then_inc(s.conv_scaled, 1)

            def attend(l, a, odd, conv, pad):
                conv(-1)
                pad()
                act.wait_ge(s.u_done, l + 1)
                if above_zero(l):
                    act.wait_ge(s.s6_done, l)
                act.activation(sq[:], qk[:], ACT.Square).then_inc(s.u2_done, 1)
                act.wait_ge(s.dwc_done, l + 1)
                if above_zero(l):
                    act.wait_ge(s.dwt_done, l)
                for b in range(2):
                    ins = act.activation(
                        dw[:].rearrange("p q r h d -> p d (q r h)")[:, 4 * b:4 * b + 4],
                        ps[:, 3 + b, 0:448].rearrange("p (d x) -> p d x", d=4), ACT.Copy)
                ins.then_inc(s.dw_taken, 1)
                if a < A7 - 1:
                    window_rows(l + 1, a + 1, odd)
                act.wait_ge(s.u3_done, l + 1)
                act.wait_ge(s.s2_done, l + 1)
                act.wait_ge(s.u3_rest, l + 1)
                act.activation(sq[:], cube[:], ACT.Square).then_inc(s.u6_done, 1)
                act.wait_ge(s.ratio_done, l + 1)
                act.activation(fac[:], fac[:], ACT.Sqrt).then_inc(s.f_done, 1)
                act.wait_ge(s.qt_done, l + 1)
                act.activation(qt, ps[:, 5:7].rearrange("p b x -> p (b x)")[:, 0:QTOK], ACT.Copy
                               ).then_inc(s.qt_taken, 1)
                conv(0)
                act.wait_ge(s.den_done, l + 1)
                act.activation(den, ps[:, 5:7].rearrange("p b x -> p (b x)")[:, 0:QTOK], ACT.Copy, bias=EPS
                               ).then_inc(s.den_taken, 1)
                act.wait_ge(s.proj_done, l + 1)
                if above_zero(l):
                    act.wait_ge(s.xo_done, l)
                for wr in range(2):
                    for hp in range(2):
                        ins = act.activation(
                            o2[C * hp:C * hp + C, 4 * wr:4 * wr + 4].rearrange("p (b j) x -> p b j x", b=2),
                            ps[C * wr:C * wr + C, 5:7, 0:N4].rearrange("p b (j hp x) -> p hp b j x", hp=2, x=W)[:, hp],
                            ACT.Identity, bias=pbias[C * wr:C * wr + C])
                ins.then_inc(s.o2_done, 1)

            def both(n, odd, attention):
                if attention:
                    for a in range(A7):
                        attend((n - 1) * A7 + a, a, 1 - odd,
                               lambda k: scale_conv(n, 2 * a + k) if a or k == 0 else None,
                               lambda: [padded_chunk(n, odd, EARLY + 2 * a + k) for k in range(2)])
                    scale_conv(n, CHUNKS - 1)
                else:
                    for k in range(EARLY, NCH):
                        padded_chunk(n, odd, k)
                    for c in range(CHUNKS):
                        scale_conv(n, c)

            def last(n, odd):
                deviation(2 * n - 1)
                if above_zero(2 * n):
                    act.wait_ge(s.rstd_done, 2 * n)
                window_rows((n - 1) * A7, 0, 1 - odd)
                for a in range(A7):
                    attend((n - 1) * A7 + a, a, 1 - odd, lambda k: None, lambda: None)

            image_steps(act, B, bring, both, last)

        @block.vector
        def _(dve):
            dve.wait_ge(s.ones, 1)

            def norm(which, count, bn):
                if above_zero(count):
                    dve.wait_ge(s.grouped, count)
                    dve.nop(nofuse=True)
                dve.bn_aggr(mv[:], bn[:]).then_inc(s.bn_at, 1)
                dve.wait_ge(s.bn_at, count * 4 + 1)
                dve.tensor_copy(st[:, 0:1], mv[:, 0:1])
                dve.scalar_tensor_tensor(st[:, 1:2], mv[:, 0:1], mv[:, 0:1], mv[:, 1:2], ALU.mult, ALU.add
                                         ).then_inc(s.stats_done, 1)
                dve.wait_ge(s.grouped, count + 1)
                dve.tensor_copy(gst[:, 0:2], ps[:, 1, 0:2]).then_inc(s.bn_at, 1)
                dve.wait_ge(s.bn_at, count * 4 + 2)
                dve.scalar_tensor_tensor(gst[:, 2:3], gst[:, 0:1], gst[:, 0:1], gst[:, 1:2],
                                         ALU.mult, ALU.subtract).then_inc(s.bn_at, 1)
                dve.wait_ge(s.bn_at, count * 4 + 3)
                dve.tensor_scalar(gst[:, 3:4], gst[:, 2:3], -1.0, GN_EPS, ALU.mult, ALU.add).then_inc(s.var_done, 1)
                dve.wait_ge(s.std_done, count + 1)
                dve.reciprocal(nrm[:, which, 0:1], gst[:, 3:4]).then_inc(s.bn_at, 1)
                dve.wait_ge(s.bn_at, count * 4 + 4)
                dve.scalar_tensor_tensor(nrm[:, which, 1:2], gst[:, 0:1], -1.0, nrm[:, which, 0:1],
                                         ALU.mult, ALU.mult).then_inc(s.rstd_done, 1)

            def bring(n, odd):
                if above_zero(n):
                    if above_zero((n - 1) * A7):
                        dve.wait_ge(s.xn_done, (n - 1) * A7)
                    if above_zero(n * CHUNKS):
                        dve.wait_ge(s.bn3_done, n * CHUNKS)
                    norm(1, 2 * n - 1, bn3)
                dve.wait_ge(x1_in[odd], 8 * (n + (2 - odd)))
                for c in range(CHUNKS):
                    dve.wait_ge(s.c2_done, n * CHUNKS + (c + 1))
                    here = xr[:, odd, ROWS * c:ROWS * c + ROWS].rearrange("p a w -> p (a w)")
                    dve.tensor_tensor(here, ps[:, 2 + c % 5, 0:N4], here, ALU.add).then_inc(s.x2_done, 1)
                    if c:
                        x2_stats(n, odd, c - 1)
                x2_stats(n, odd, CHUNKS - 1)
                dve.wait_ge(s.x2_stats, (n + 1) * CHUNKS)
                norm(0, 2 * n, bn2)
                if above_zero(n):
                    take_qkv((n - 1) * A7)
                for k in range(EARLY):
                    low_part(n, k)

            def x2_stats(n, odd, c):
                dve.wait_ge(s.x2_done, n * CHUNKS + (c + 1))
                dve.bn_stats(bn2[:, c], xr[:, odd, ROWS * c:ROWS * c + ROWS].rearrange("p a w -> p (a w)")
                             ).then_inc(s.x2_stats, 1)

            def low_part(n, k):
                if k >= NCH:
                    return
                lo, hi = spans[k]
                dve.wait_ge(s.hi_done, n * NCH + (k + 1))
                dve.wait_ge(s.high_done, n * NCH + (k + 1))
                for kind in range(3):
                    ins = dve.tensor_tensor(xp[:, 1, kind, lo:hi].rearrange("p j w -> p (j w)"),
                                            tn[:, k % 2, kind, 0:hi - lo].rearrange("p j w -> p (j w)"),
                                            xp[:, 0, kind, lo:hi].rearrange("p j w -> p (j w)"), ALU.subtract)
                ins.then_inc(s.lo_done, 1)

            def take_ab(n, c):
                dve.wait_ge(s.ab_done, n * CHUNKS + (c + 1))
                if above_zero(n * CHUNKS + (c - 1)):
                    dve.wait_ge(s.x3_done, n * CHUNKS + (c - 1))
                second = ps[:, 0, 0:ROWS * (W // 2)].rearrange("p (j i) -> p j i", j=ROWS)
                first = ps[:, 0, ROWS * (W // 2):ROWS * (W + 1)].rearrange("p (j i) -> p j i", j=ROWS)
                dve.tensor_copy(part[:], first).then_inc(s.part_done, 1)
                dve.wait_ge(s.part_done, n * CHUNKS + (c + 1))
                dve.tensor_tensor(cv[:, c % 2, :, 0:W:2], second, part[:, :, 0:W // 2], ALU.add)
                dve.tensor_tensor(cv[:, c % 2, :, 1:W:2], second, part[:, :, 1:W // 2 + 1], ALU.add
                                  ).then_inc(s.ab_taken, 1)

            def take_g(n, c):
                dve.wait_ge(s.g_done, n * CHUNKS + (c + 1))
                dve.wait_ge(s.ab_taken, n * CHUNKS + (c + 1))
                dve.tensor_tensor(cv[:, c % 2, :, 1:W:2], ps[:, 1, 0:ROWS * (W // 2)].rearrange("p (j i) -> p j i", j=ROWS),
                                  cv[:, c % 2, :, 1:W:2], ALU.subtract).then_inc(s.g_taken, 1)

            def x3_stats(n, odd, c):
                dve.wait_ge(s.x3_done, n * CHUNKS + (c + 1))
                dve.bn_stats(bn3[:, c], xr[:, odd, ROWS * c:ROWS * c + ROWS].rearrange("p a w -> p (a w)")
                             ).then_inc(s.bn3_done, 1)

            def take_qkv(l):
                for g, (q, n, b) in enumerate(QGROUPS):
                    dve.wait_ge(s.qkv_done, 4 * l + (g + 1))
                    dve.tensor_tensor(qk[:, q:q + n].rearrange("p q k r c -> p q (k r c)"), ps[:, b:b + n, 0:4 * C],
                                      bqk[:].rearrange("p k r c -> p (k r c)").unsqueeze(1).to_broadcast(
                                          [P, n, 4 * C]), ALU.add)
                    dve.tensor_tensor(v[:, 2 * q:2 * (q + n), 0:C].rearrange("p (q r) c -> p q r c", r=2),
                                      ps[:, b:b + n, 4 * C:6 * C].rearrange("p q (r c) -> p q r c", r=2),
                                      bv[:].rearrange("p (r c) -> p r c", r=2).unsqueeze(1).to_broadcast([P, n, 2, C]),
                                      ALU.add).then_inc(s.qk_taken, 1)
                dve.wait_ge(s.qk_taken, 4 * l + 4)
                flat = qk[:].rearrange("p q k r c -> p (q k r) c")
                dve.scalar_tensor_tensor(flat, flat, 0.0, epsc[:].unsqueeze(1).to_broadcast([P, 4 * Q7, C]),
                                         ALU.max, ALU.add).then_inc(s.u_done, 1)

            def attend(l, a, conv, pad):
                conv("g", -1)
                if a:
                    take_qkv(l)
                pad()
                conv("x", -1)
                dve.wait_ge(s.u2_done, l + 1)
                dve.tensor_reduce(s2[:], sq[:].rearrange("p q k r c -> p (q k r) c"), AX.X, ALU.add
                                  ).then_inc(s.s2_done, 1)
                if above_zero(2 * l):
                    dve.wait_ge(s.kv_done, 2 * l)
                dve.tensor_tensor(cube[:, CUBES:], sq[:, CUBES:], qk[:, CUBES:], ALU.mult).then_inc(s.u3_rest, 1)
                conv("ab", 0)
                if a == 0:
                    conv("g", 0)
                dve.wait_ge(s.u6_done, l + 1)
                dve.tensor_reduce(s6[:], sq[:].rearrange("p q k r c -> p (q k r) c"), AX.X, ALU.add
                                  ).then_inc(s.s6_done, 1)
                dve.wait_ge(s.s6_done, l + 1)
                dve.reciprocal(s6[:], s6[:]).then_inc(s.ratio_at, 1)
                dve.wait_ge(s.ratio_at, l + 1)
                dve.tensor_tensor(fac[:], s2[:], s6[:], ALU.mult).then_inc(s.ratio_done, 1)
                dve.wait_ge(s.f_done, l + 1)
                cubes = cube[:].rearrange("p q k r c -> p (q k r) c")
                dve.tensor_tensor(cubes, cubes, fac[:].unsqueeze(2).to_broadcast([P, 4 * Q7, C]), ALU.mult
                                  ).then_inc(s.scaled, 1)
                if a:
                    conv("g", 0)
                if above_zero(l):
                    dve.wait_ge(s.xo_done, l)
                for w in range(2):
                    dve.wait_ge(s.kv_done, 2 * l + (w + 1))
                    for b, n in ((0, 4), (1, 3)):
                        got = ps[:, 2 + 3 * w + b, 0:65 * n].rearrange("p (q x) -> p q x", q=n)
                        ins = dve.tensor_copy(km[:, 4 * b:4 * b + n, w], got[:, :, C])
                    ins.then_inc(s.km_done, 1)
                    for b, n in ((0, 4), (1, 3)):
                        got = ps[:, 2 + 3 * w + b, 0:65 * n].rearrange("p (q x) -> p q x", q=n)
                        for r in range(2):
                            ins = dve.tensor_tensor(kvm[:, w, 4 * b:4 * b + n, C * r:C * r + C], got[:, :, 0:C],
                                                    head[:, C * r:C * r + C].unsqueeze(1).to_broadcast([P, n, C]),
                                                    ALU.mult)
                        ins.then_inc(s.kvm_done, 1)
                if a == 0:
                    conv("ab", 1)
                dve.wait_ge(s.den_taken, l + 1)
                dve.reciprocal(den, den).then_inc(s.inv_done, 1)
                dve.wait_ge(s.num_done, l + 1)
                dve.wait_ge(s.inv_done, l + 1)
                dve.wait_ge(s.dwt_done, l + 1)
                flat = att[:].rearrange("p w t -> p (w t)")
                dve.tensor_tensor(flat, ps[:, 2:4].rearrange("p b x -> p (b x)")[:, 0:QTOK], den, ALU.mult
                                  ).then_inc(s.mul_done, 1)
                dve.wait_ge(s.mul_done, l + 1)
                dve.tensor_tensor(flat[:, 0:BANK], ps[:, 4], flat[:, 0:BANK], ALU.add)
                dve.tensor_tensor(flat[:, BANK:QTOK], ps[:, 7, 0:QTOK - BANK], flat[:, BANK:QTOK], ALU.add
                                  ).then_inc(s.att_done, 1)
                if a:
                    conv("ab", 1)
                conv("x", 0)

            def both(n, odd, attention):
                def conv(what, c):
                    if c >= 0:
                        {"ab": take_ab, "g": take_g}[what](n, c) if what != "x" else x3_stats(n, odd, c)

                if attention:
                    for a in range(A7):
                        attend((n - 1) * A7 + a, a, lambda what, k: conv(what, 2 * a + k),
                               lambda: [low_part(n, EARLY + 2 * a + k) for k in range(2)])
                else:
                    for k in range(EARLY, NCH):
                        low_part(n, k)
                    for c in range(CHUNKS - 1):
                        conv("ab", c)
                        conv("g", c)
                        conv("x", c - 1)
                    conv("ab", CHUNKS - 1)
                    conv("x", CHUNKS - 2)
                conv("g", CHUNKS - 1)
                conv("x", CHUNKS - 1)

            def last(n, odd):
                if above_zero(n * CHUNKS):
                    dve.wait_ge(s.bn3_done, n * CHUNKS)
                norm(1, 2 * n - 1, bn3)
                take_qkv((n - 1) * A7)
                for a in range(A7):
                    attend((n - 1) * A7 + a, a, lambda what, k: None, lambda: None)

            image_steps(dve, B, bring, both, last)

        @block.gpsimd
        def _(pool):
            pool.memset(tn[:], 0.0)
            pool.memset(ys[:], 0.0).then_inc(s.zeros, 1)
            pool.memset(v[:], 1.0).then_inc(s.ones, 1)

            def bring(n, odd):
                pool.wait_ge(s.c2_done, (n + 1) * CHUNKS)
                pool.nop(nofuse=True)
                pool.memset(xp[:, :, :, 0:1], 0.0)
                pool.memset(xp[:, :, :, J + 2:J + 3], 0.0)
                pool.memset(xp[:, 0, 0:2, 1:J + 2, 0:2], 0.0)
                pool.memset(xp[:, 0, 0:2, 1:J + 2, PW - 2:PW], 0.0).then_inc(s.bordered, 1)
                for k in range(EARLY):
                    high_part(n, k)

            def high_part(n, k):
                if k >= NCH:
                    return
                lo, hi = spans[k]
                here = tn[:, k % 2, :, 0:hi - lo]
                pool.wait_ge(s.normed, n * NCH + (k + 1))
                pool.nop(nofuse=True)
                pool.tensor_tensor(here[:, 2, :, 0:PW - 1], here[:, 1, :, 0:PW - 1], here[:, 0, :, 1:PW], ALU.add
                                   ).then_inc(s.padded, 1)
                pool.wait_ge(s.padded, n * NCH + (k + 1))
                pool.nop(nofuse=True)
                pool.tensor_copy(xp[:, 0, 2, lo:hi].rearrange("p j w -> p (j w)"),
                                 here[:, 2].rearrange("p j w -> p (j w)")).then_inc(s.hi_done, 1)

            def add_conv(n, odd, c):
                pool.wait_ge(s.conv_scaled, n * CHUNKS + (c + 1))
                pool.nop(nofuse=True)
                here = xr[:, odd, ROWS * c:ROWS * c + ROWS].rearrange("p a w -> p (a w)")
                pool.tensor_tensor(here, cv[:, c % 2].rearrange("p a w -> p (a w)"), here, ALU.add).then_inc(s.x3_done, 1)

            def attend(l, a, odd, conv, pad):
                conv(-1)
                pad()
                pool.wait_ge(s.u2_done, l + 1)
                pool.nop(nofuse=True)
                if above_zero(2 * l):
                    pool.wait_ge(s.kv_done, 2 * l)
                    pool.nop(nofuse=True)
                pool.tensor_tensor(cube[:, 0:CUBES], sq[:, 0:CUBES], qk[:, 0:CUBES], ALU.mult).then_inc(s.u3_done, 1)
                pool.wait_ge(s.qt_taken, l + 1)
                pool.nop(nofuse=True)
                pool.wait_ge(s.km_done, 2 * l + 2)
                pool.nop(nofuse=True)
                if above_zero(l):
                    pool.wait_ge(s.den_done, l)
                    pool.nop(nofuse=True)
                pool.tensor_tensor(qs.rearrange("p (q w t) -> p (q w) t", w=2, t=TOK),
                                   qt.rearrange("p (q w t) -> p (q w) t", w=2, t=TOK),
                                   km[:].rearrange("p q w -> p (q w)").unsqueeze(2)
                                   .to_broadcast([P, 2 * Q7, TOK]), ALU.mult).then_inc(s.qs_done, 1)
                conv(0)
                pool.wait_ge(s.o2_done, l + 1)
                pool.nop(nofuse=True)
                here = xr[:, odd, 8 * a:8 * a + 8]
                pool.tensor_tensor(here, o2, here, ALU.add).then_inc(s.xo_done, 1)

            def both(n, odd, attention):
                if attention:
                    for a in range(A7):
                        attend((n - 1) * A7 + a, a, 1 - odd,
                               lambda k: add_conv(n, odd, 2 * a + k) if a or k == 0 else None,
                               lambda: [high_part(n, EARLY + 2 * a + k) for k in range(2)])
                    add_conv(n, odd, CHUNKS - 1)
                else:
                    for k in range(EARLY, NCH):
                        high_part(n, k)
                    for c in range(CHUNKS):
                        add_conv(n, odd, c)

            def last(n, odd):
                for a in range(A7):
                    attend((n - 1) * A7 + a, a, 1 - odd, lambda k: None, lambda: None)

            image_steps(pool, B, bring, both, last)


def build(nc, a, cst, x1, xf, yf, out):
    B = a["x"].shape[0]
    local_conv_and_forward_dft(nc, B, a["x"], a["L0_conv_weight"],
                               a["L0_conv_alpha"].rearrange("c i j -> c (i j)"), cst, x1, xf)
    mix_frequencies(nc, B, a["L1_conv_weight"], xf, yf)
    large_conv_and_attention(nc, B, a, cst, x1, yf, out)


def kernel(**inputs):
    import numpy as _np
    import concourse.bacc as _bacc
    from concourse import mybir as _mybir
    from concourse.bass_utils import run_bass_kernel_spmd as _run

    nc = _bacc.Bacc("TRN2", target_bir_lowering=False, num_devices=1)
    f32 = _mybir.dt.float32
    arrays, args, cst = {}, {}, {}
    for name, a in inputs.items():
        arrays[f"in_{name}"] = a = _np.ascontiguousarray(a)
        args[name] = nc.dram_tensor(f"in_{name}", a.shape, f32, kind="ExternalInput").ap()
    for name, a in constants().items():
        arrays[f"cst_{name}"] = a
        cst[name] = nc.dram_tensor(f"cst_{name}", a.shape, f32, kind="ExternalInput").ap()
    B = inputs["x"].shape[0]
    x1 = nc.dram_tensor("x1", (B, 2, C, J, W), f32, kind="Internal").ap()
    xf = nc.dram_tensor("xf", (KP, P, B, FP), f32, kind="Internal").ap()
    yf = nc.dram_tensor("yf", (KP, P, B, FP), f32, kind="Internal").ap()
    out = nc.dram_tensor("out", (B, C, H, W), f32, kind="ExternalOutput").ap()
    build(nc, args, cst, x1, xf, yf, out)
    return _run(nc, [arrays], core_ids=[0]).results[0]["out"]
```
